# Optimizing a Trainium2 kernel written in Bass

```python
import numpy as np
import jax
import jax.numpy as jnp

def _softmax(x, axis=-1):
    return jax.nn.softmax(x, axis=axis)

def _gelu(x):
    return jax.nn.gelu(x, approximate=True)

def _silu(x):
    return jax.nn.silu(x)

def _sigmoid(x):
    return jax.nn.sigmoid(x)

def _layernorm(x, axis=-1, eps=1e-05):
    m = jnp.mean(x, axis=axis, keepdims=True)
    v = jnp.var(x, axis=axis, keepdims=True)
    return (x - m) / jnp.sqrt(v + eps)

def _scatter_add(tgt, idx, src, axis=0):
    return tgt.at[idx].add(src)

def _segment_sum(src, seg, n):
    return jax.ops.segment_sum(src, seg, n)
kernel_name = 'mk_sandwich_d2_jaxref_r8_f72051'

def setup_inputs(seed: int=0):
    np.random.seed(seed)
    _w = jnp.asarray

    def _L0_attn_setup():
        import jax, jax.numpy as jnp
        import numpy as np
        import math
        D_MODEL = 256
        NUM_HEADS = 16
        HEAD_DIM = D_MODEL // NUM_HEADS
        key = jax.random.key(seed)
        k_x, k_wqkv, k_bqkv, k_wo, k_bo = jax.random.split(key, 5)
        B, S = (2, 256)
        scale = 1.0 / math.sqrt(D_MODEL)
        return {'x': jax.random.normal(k_x, (B, S, D_MODEL), dtype=jnp.float32), 'w_qkv': jax.random.normal(k_wqkv, (3 * D_MODEL, D_MODEL), dtype=jnp.float32) * scale, 'b_qkv': jax.random.normal(k_bqkv, (3 * D_MODEL,), dtype=jnp.float32) * 0.01, 'w_out': jax.random.normal(k_wo, (D_MODEL, D_MODEL), dtype=jnp.float32) * scale, 'b_out': jax.random.normal(k_bo, (D_MODEL,), dtype=jnp.float32) * 0.01}
    _L0_attn_in = _L0_attn_setup()

    def _L0_ffn_setup():
        import jax, jax.numpy as jnp
        import numpy as np
        E, H, I, TOPK = (16, 256, 176, 4)
        B, S = (2, 128)
        key = jax.random.key(seed)
        ks = jax.random.split(key, 6)
        hidden_states = jax.random.normal(ks[0], (B, S, H), dtype=jnp.float32)
        topk_idx = jax.random.randint(ks[1], (B, S, TOPK), 0, E)
        topk_weight = jax.random.uniform(ks[2], (B, S, TOPK), dtype=jnp.float32) / TOPK
        gate_weight = jax.random.normal(ks[3], (E, I, H), dtype=jnp.float32) * (1.0 / np.sqrt(H))
        up_weight = jax.random.normal(ks[4], (E, I, H), dtype=jnp.float32) * (1.0 / np.sqrt(H))
        down_weight = jax.random.normal(ks[5], (E, H, I), dtype=jnp.float32) * (1.0 / np.sqrt(I))
        return {'hidden_states': hidden_states, 'topk_idx': topk_idx, 'topk_weight': topk_weight, 'gate_weight': gate_weight, 'up_weight': up_weight, 'down_weight': down_weight}
    _L0_ffn_in = _L0_ffn_setup()

    def _L1_attn_setup():
        import math
        import jax, jax.numpy as jnp
        import numpy as np

        def _alibi_slopes(n):

            def pow2_slopes(n):
                start = 2.0 ** (-2.0 ** (-(math.log2(n) - 3)))
                return [start * start ** i for i in range(n)]
            if math.log2(n).is_integer():
                return pow2_slopes(n)
            cp2 = 2 ** math.floor(math.log2(n))
            return pow2_slopes(cp2) + _alibi_slopes(2 * cp2)[0::2][:n - cp2]
        NUM_HEADS = 16
        key = jax.random.key(seed)
        ks = jax.random.split(key, 5)
        B, S, H = (2, 256, 256)
        return {'hidden_states': jax.random.normal(ks[0], (B, S, H), jnp.float32), 'w_qkv': jax.random.normal(ks[1], (H, 3 * H), jnp.float32) * H ** (-0.5), 'b_qkv': jax.random.normal(ks[2], (3 * H,), jnp.float32) * 0.02, 'w_proj': jax.random.normal(ks[3], (H, H), jnp.float32) * H ** (-0.5), 'b_proj': jax.random.normal(ks[4], (H,), jnp.float32) * 0.02}
    _L1_attn_in = _L1_attn_setup()

    def _L1_ffn_setup():
        import jax, jax.numpy as jnp
        import numpy as np

        def binarize_weight(w):
            alpha = jnp.mean(jnp.abs(w), axis=tuple(range(1, w.ndim)), keepdims=True)
            bw = jnp.where(w >= 0, 1.0, -1.0) * alpha
            return jax.lax.stop_gradient(bw - w) + w
        key = jax.random.key(seed)
        k1, k2, k3 = jax.random.split(key, 3)
        in_features, out_features = (256, 256)
        x = jax.random.normal(k1, (8, 256, in_features), dtype=jnp.float32)
        std = np.sqrt(2.0 / out_features).astype(np.float32)
        weight = jax.random.normal(k2, (out_features, in_features), dtype=jnp.float32) * std
        bias = jax.random.normal(k3, (out_features,), dtype=jnp.float32) * 0.01
        return {'x': x, 'weight': weight, 'bias': bias}
    _L1_ffn_in = _L1_ffn_setup()
    _d = {'L0_attn_x': _L0_attn_in['x'], 'L0_attn_w_qkv': _L0_attn_in['w_qkv'], 'L0_attn_b_qkv': _L0_attn_in['b_qkv'], 'L0_attn_w_out': _L0_attn_in['w_out'], 'L0_attn_b_out': _L0_attn_in['b_out'], 'L0_ffn_topk_idx': _L0_ffn_in['topk_idx'], 'L0_ffn_topk_weight': _L0_ffn_in['topk_weight'], 'L0_ffn_gate_weight': _L0_ffn_in['gate_weight'], 'L0_ffn_up_weight': _L0_ffn_in['up_weight'], 'L0_ffn_down_weight': _L0_ffn_in['down_weight'], 'L1_attn_w_qkv': _L1_attn_in['w_qkv'], 'L1_attn_b_qkv': _L1_attn_in['b_qkv'], 'L1_attn_w_proj': _L1_attn_in['w_proj'], 'L1_attn_b_proj': _L1_attn_in['b_proj'], 'L1_ffn_weight': _L1_ffn_in['weight'], 'L1_ffn_bias': _L1_ffn_in['bias']}
    _x0 = _d['L0_attn_x']
    _d['L0_attn_x'] = jax.random.normal(jax.random.fold_in(jax.random.key(seed), 1), (4, 1024, 256), dtype=_x0.dtype)
    del _x0
    return _d

def reference(L0_attn_x, L0_attn_w_qkv, L0_attn_b_qkv, L0_attn_w_out, L0_attn_b_out, L0_ffn_topk_idx, L0_ffn_topk_weight, L0_ffn_gate_weight, L0_ffn_up_weight, L0_ffn_down_weight, L1_attn_w_qkv, L1_attn_b_qkv, L1_attn_w_proj, L1_attn_b_proj, L1_ffn_weight, L1_ffn_bias):

    def _L0_attn_ref(x, w_qkv, b_qkv, w_out, b_out):
        import jax, jax.numpy as jnp
        import numpy as np
        import math
        D_MODEL = 256
        NUM_HEADS = 16
        HEAD_DIM = D_MODEL // NUM_HEADS
        B, S, D = x.shape
        H, Hd = (NUM_HEADS, HEAD_DIM)
        qkv = jnp.einsum('bsd,ed->bse', x, w_qkv) + b_qkv
        qkv = qkv.reshape(B, S, 3, H, Hd)
        q = jnp.transpose(qkv[:, :, 0], (0, 2, 1, 3))
        k = jnp.transpose(qkv[:, :, 1], (0, 2, 1, 3))
        v = jnp.transpose(qkv[:, :, 2], (0, 2, 1, 3))
        scores = jnp.einsum('bhqd,bhkd->bhqk', q, k) / math.sqrt(Hd)
        causal = jnp.triu(jnp.full((S, S), -jnp.inf, dtype=scores.dtype), k=1)
        scores = scores + causal[None, None]
        attn = jax.nn.softmax(scores, axis=-1)
        out = jnp.einsum('bhqk,bhkd->bhqd', attn, v)
        out = jnp.transpose(out, (0, 2, 1, 3)).reshape(B, S, D)
        return jnp.einsum('bsd,ed->bse', out, w_out) + b_out

    def _L0_ffn_ref(hidden_states, topk_idx, topk_weight, gate_weight, up_weight, down_weight):
        import jax, jax.numpy as jnp
        import numpy as np
        E, H, I, TOPK = (16, 256, 176, 4)
        B, S = (2, 128)
        b, s, h = hidden_states.shape
        n_tokens = b * s
        topk = topk_idx.shape[-1]
        x = hidden_states.reshape(n_tokens, h)
        flat_expert = topk_idx.reshape(-1)
        flat_weight = topk_weight.reshape(-1).astype(hidden_states.dtype)
        perm = jnp.argsort(flat_expert)
        tok = jnp.repeat(jnp.arange(n_tokens), topk)[perm]
        xs = x[tok]
        group_sizes = jnp.bincount(flat_expert, length=E).astype(jnp.int32)
        gate = jax.lax.ragged_dot(xs, jnp.swapaxes(gate_weight, 1, 2), group_sizes)
        up = jax.lax.ragged_dot(xs, jnp.swapaxes(up_weight, 1, 2), group_sizes)
        h_act = jax.nn.silu(gate) * up
        down = jax.lax.ragged_dot(h_act, jnp.swapaxes(down_weight, 1, 2), group_sizes)
        w_sorted = flat_weight[perm]
        out = jnp.zeros((n_tokens, h), hidden_states.dtype).at[tok].add(down * w_sorted[:, None])
        return out.reshape(b, s, h)

    def _L1_attn_ref(hidden_states, w_qkv, b_qkv, w_proj, b_proj):
        import math
        import jax, jax.numpy as jnp
        import numpy as np

        def _alibi_slopes(n):

            def pow2_slopes(n):
                start = 2.0 ** (-2.0 ** (-(math.log2(n) - 3)))
                return [start * start ** i for i in range(n)]
            if math.log2(n).is_integer():
                return pow2_slopes(n)
            cp2 = 2 ** math.floor(math.log2(n))
            return pow2_slopes(cp2) + _alibi_slopes(2 * cp2)[0::2][:n - cp2]
        NUM_HEADS = 16
        B, S, H = hidden_states.shape
        nh = NUM_HEADS
        hd = H // nh
        scale = 1.0 / hd
        qkv = hidden_states @ w_qkv + b_qkv
        q, k, v = jnp.split(qkv, 3, axis=-1)
        q = q.reshape(B, S, nh, hd)
        k = k.reshape(B, S, nh, hd)
        v = v.reshape(B, S, nh, hd)
        scores = jnp.einsum('bqhd,bkhd->bhqk', q, k) * scale
        slopes = jnp.asarray(_alibi_slopes(nh), dtype=scores.dtype)
        pos = jnp.arange(S)
        rel = (pos[None, :] - pos[:, None]).astype(scores.dtype)
        bias = slopes[:, None, None] * rel[None, :, :]
        causal = pos[None, :] <= pos[:, None]
        scores = jnp.where(causal[None, None], scores + bias[None], jnp.finfo(scores.dtype).min)
        attn = jax.nn.softmax(scores, axis=-1)
        out = jnp.einsum('bhqk,bkhd->bqhd', attn, v).reshape(B, S, H)
        return out @ w_proj + b_proj

    def _L1_ffn_ref(x, weight, bias):
        import jax, jax.numpy as jnp
        import numpy as np

        def binarize_weight(w):
            alpha = jnp.mean(jnp.abs(w), axis=tuple(range(1, w.ndim)), keepdims=True)
            bw = jnp.where(w >= 0, 1.0, -1.0) * alpha
            return jax.lax.stop_gradient(bw - w) + w
        bw = binarize_weight(weight)
        return jnp.einsum('bsi,oi->bso', x, bw) + bias
    x = L0_attn_x
    x = x + _layernorm(_L0_attn_ref(_layernorm(x, axis=-1), L0_attn_w_qkv, L0_attn_b_qkv, L0_attn_w_out, L0_attn_b_out), axis=-1)
    x = x + _layernorm(_L0_ffn_ref(_layernorm(x, axis=-1), L0_ffn_topk_idx, L0_ffn_topk_weight, L0_ffn_gate_weight, L0_ffn_up_weight, L0_ffn_down_weight), axis=-1)
    x = x + _layernorm(_L1_attn_ref(_layernorm(x, axis=-1), L1_attn_w_qkv, L1_attn_b_qkv, L1_attn_w_proj, L1_attn_b_proj), axis=-1)
    x = x + _layernorm(_L1_ffn_ref(_layernorm(x, axis=-1), L1_ffn_weight, L1_ffn_bias), axis=-1)
    return x

_drawn_inputs = setup_inputs


def setup_inputs(seed=0):
    import zlib

    import numpy as np

    out = dict(_drawn_inputs(seed))
    spreads = {}
    factors = {'L1_ffn_bias': 8.0}
    for name, (base, spread) in spreads.items():
        noise = np.random.default_rng([zlib.crc32(name.encode()), seed]).standard_normal(out[name].shape)
        drawn = base * np.exp(spread * noise) if base else spread * noise
        out[name] = jnp.asarray(drawn.astype(out[name].dtype))
    for name, factor in factors.items():
        out[name] = (out[name] * factor).astype(out[name].dtype)
    return out
```

```python
from contextlib import ExitStack

import numpy as np

import concourse.bass as bass
from concourse import mybir

F32 = mybir.dt.float32
BF16 = mybir.dt.bfloat16
I32 = mybir.dt.int32
ALU = mybir.AluOpType
ACT = mybir.ActivationFunctionType
AX_X = mybir.AxisListType.X

P = 128
B, S, D = 4, 1024, 256
NH, HD = 16, 16
DC = D // P
NT = B * S // P
TB = S // P
NG = 4
GH = NH // NG
VW = P // GH
C = 512
NE, FI, TOPK = 16, 176, 4
FC = FI // 2
MT_TILES = 2
EPS = 1e-5
MASKED = -1e30

PARTS = 3
QK_ROWS = 6 * HD
POS_ROWS = 12
MAX_ROWS = PARTS
K_MAX = QK_ROWS + POS_ROWS
K_EXP = K_MAX + MAX_ROWS
Q_RUNS = [(0, 0, 3), (3, 0, 2), (5, 0, 1)]
K_RUNS = [(0, 0), (1, 0), (2, 0), (3, 1), (4, 1), (5, 2)]
LOADS = len(Q_RUNS) + len(K_RUNS) + 3
SLOTS = 4
LEAD = 1.3
GROUPS = B * NG
FREE = 1


def maximum_units():
    units = []
    for cls in (0, 1):
        for n in range(1, 5):
            per = 4 // n if n < 3 else 1
            for h in range(0, GH, per):
                units.append((cls, list(range(h, h + per)), 4 * cls + n - 1, cls * C, n * P))
    for qb in range(4, 8):
        for h in range(GH):
            units.append((2, [h], qb, 0, C))
    return units


MAX_UNITS = maximum_units()


def attention_stream():
    steps = []
    for g in range(GROUPS):
        order = []
        for kb in range(TB):
            w = S - kb * P
            for h in range(GH):
                order.append((("E", g, kb, h), w + P))
                if kb and h == 1:
                    order.append((("V", g, kb - 1), 4 * (w + P)))
                if kb == 5 and h == 0:
                    order.append((("O", g, 0), 0))
                if kb == 6 and h == 2:
                    order.append((("N", g, 0), 4 * C))
        total, at = sum(c for _, c in order) * 1.03, 0.0
        for step, cost in order:
            steps.append((g + at / total, step))
            at += cost
        steps += [(g + 0.975, ("V", g, TB - 1)), (g + 0.976, ("O", g, 1)), (g + 0.9999, ("N", g, 1))]
        total, at = sum(len(hs) * (n + P) for _, hs, _, _, n in MAX_UNITS) * 1.001, 0.0
        for i, (_, hs, _, _, n) in enumerate(MAX_UNITS):
            steps.append((g - LEAD + at / total, ("M", g, i)))
            at += len(hs) * (n + P)
        steps += [(g - LEAD + 1, ("F", g)), (g - LEAD + 1.07, ("T", g))]
    steps.sort(key=lambda s: s[0])
    return steps


def relative(steps, it):
    return [(s[0], s[1] - NG * it, *s[2:]) for t, s in steps if NG * it <= t < NG * (it + 1)]


STREAM = attention_stream()
BEFORE = [s for t, s in STREAM if t < 0]
BODY = relative(STREAM, 0)
LAST = relative(STREAM, B - 1)
assert BODY == relative(STREAM, 1) == relative(STREAM, B - 2)


def banks(steps):
    return sum(s[0] in "MTN" for s in steps)


def sandwich(nc, io, out):
    with ExitStack() as ctx:
        def sb(name, shape, dt=F32):
            return ctx.enter_context(nc.sbuf_tensor(name, shape, dt))

        def sem(name):
            return ctx.enter_context(nc.semaphore(name))

        q_dram = nc.dram_tensor("q_parts", [B, NG, PARTS, HD, GH, S], BF16).ap()
        k_dram = nc.dram_tensor("k_parts", [B, NG, PARTS, HD, GH, S], BF16).ap()
        v_dram = nc.dram_tensor("values", [B, NG, P, TB, P], F32).ap()
        o_dram = nc.dram_tensor("attended", [B, D, S], F32).ap()

        x = sb("x", [P, NT, D])
        w_qkv = sb("w_qkv", [P, 2, DC, 3 * D])
        b_qk = sb("b_qk", [P, 2, 4])
        b_v = sb("b_v", [P, 2, D])
        w_out = sb("w_out", [P, 2, DC, D])
        b_out = sb("b_out", [P, 2, D])
        ident = sb("ident", [P, P])
        ident_b = sb("ident_b", [P, P], BF16)
        mask_exp = sb("mask_exp", [P, P], BF16)
        mask_max = sb("mask_max", [P, P], BF16)
        spread = sb("spread", [P, P])
        eps = sb("eps", [P, 1])
        stats = sb("stats", [P, 2, 4, 6])
        moments = sb("moments", [P, 2, 4, 2])
        rstd = sb("rstd", [P, 2, 4])
        shift = sb("shift", [P, 2, 4])
        norm = sb("norm", [P, 2, 4, D])
        normT = sb("normT", [P, 2, DC * C])

        big = ctx.enter_context(nc.psum_tensor("big", [P, 2, S], F32))
        ring = ctx.enter_context(nc.psum_tensor("ring", [P, 2, C], F32))
        accs = ctx.enter_context(nc.psum_tensor("accs", [P, 2, C], F32))

        loaded = sem("loaded")
        scaled = sem("scaled")
        with nc.Block() as block:
            loads = [(x[:], io["x"].rearrange("(t p) d -> p t d", p=P)),
                     (w_qkv[:], io["w_qkv"]), (b_qk[:], io["b_qk"]), (b_v[:], io["b_v"]),
                     (w_out[:], io["w_out"]), (b_out[:], io["b_out"]),
                     (ident[:], io["ident"]), (ident_b[:], io["ident_b"]), (mask_exp[:], io["mask_exp"]),
                     (mask_max[:], io["mask_max"]), (spread[:], io["spread"])]

            @block.sync
            def _(sp):
                for dst, src in loads:
                    sp.dma_start(dst, src).then_inc(loaded, 16)
                sp.wait_ge(loaded, 16 * len(loads))

            @block.vector
            def _(dve):
                nc.vector.memset(eps[:], EPS).then_inc(scaled, 1)
                dve.wait_ge(loaded, 16 * len(loads))
                for layer in range(2):
                    nc.vector.tensor_scalar(b_qk[:, layer, 0:2], b_qk[:, layer, 0:2], (0.25, 0.0625)[layer], None,
                                            ALU.mult).then_inc(scaled, 1)

        for layer in range(2):
            project_qkv(nc, sem, layer, dict(
                x=x, w_qkv=w_qkv, b_qk=b_qk, b_v=b_v, ident=ident, eps=eps, stats=stats, moments=moments, rstd=rstd,
                norm=norm, normT=normT, big=big, ring=ring, accs=accs,
                q_dram=q_dram, k_dram=k_dram, v_dram=v_dram))
            attend(nc, sem, layer, dict(
                ident_b=ident_b, mask_exp=mask_exp, mask_max=mask_max, spread=spread, big=big, ring=ring, accs=accs,
                q_dram=q_dram, k_dram=k_dram, v_dram=v_dram, o_dram=o_dram, pos_q=io["pos_q"], pos_k=io["pos_k"]))
            project_out(nc, sem, layer, dict(
                x=x, w_out=w_out, b_out=b_out, eps=eps, stats=stats, moments=moments, rstd=rstd, shift=shift, norm=norm, big=big, o_dram=o_dram))
            if layer == 0:
                experts(nc, sem, io, dict(
                    x=x, ident=ident, eps=eps, stats=stats, moments=moments, rstd=rstd, shift=shift, norm=norm, normT=normT,
                    big=big, ring=ring, accs=accs))
        linear(nc, sem, io, out, dict(
            x=x, ident=ident, eps=eps, stats=stats, moments=moments, rstd=rstd, shift=shift, norm=norm, normT=normT,
            big=big, ring=ring))


def project_qkv(nc, sem, layer, t):
    x, norm, normT = t["x"], t["norm"], t["normT"]
    stats, moments, rstd = t["stats"], t["moments"], t["rstd"]
    big, ring, accs = t["big"], t["ring"], t["accs"]
    scale = (0.25, 0.0625)[layer]
    n = f"p{layer}_"
    stats_done = sem(n + "stats_done")
    stats_seen = sem(n + "stats_seen")
    moments_done = sem(n + "moments_done")
    std_done = sem(n + "std_done")
    rstd_done = sem(n + "rstd_done")
    norm_done = sem(n + "norm_done")
    transposed = sem(n + "transposed")
    normT_done = sem(n + "normT_done")
    qk_made = sem(n + "qk_made")
    qk_left = sem(n + "qk_left")
    rest_done = sem(n + "rest_done")
    mid_done = sem(n + "mid_done")
    low_done = sem(n + "low_done")
    v_made = sem(n + "v_made")
    v_left = sem(n + "v_left")
    stored = [sem(n + f"stored{u}") for u in range(2)]
    ones_set = sem(n + "ones_set")
    stores = 4 * 2 + NG

    with (nc.sbuf_tensor(n + "qk32", [P, 4, C], F32) as qk32,
          nc.sbuf_tensor(n + "parts", [P, 2, 4, PARTS, C], BF16) as parts,
          nc.sbuf_tensor(n + "values", [P, 2, 4, NG, P], F32) as values,
          nc.Block() as block):
        @block.gpsimd
        def _(pool):
            nc.gpsimd.memset(values[:], 1.0).then_inc(ones_set, 1)

        @block.sync
        def _(sp):
            sp.sem_inc(stored[0], FREE)
            sp.sem_inc(stored[1], FREE)
            with sp.Fori(0, B) as b:
                for u in range(2):
                    k = 2 * b + u
                    for m in range(4):
                        sp.wait_ge(low_done, FREE + 4 * k + m + 1)
                        dram = (t["q_dram"], t["k_dram"])[m // 2]
                        for g in range(2):
                            dst = dram[bass.ds(b, 1), 2 * (m % 2) + g, :, :, :, u * C:(u + 1) * C]
                            sp.dma_start(dst.rearrange("b part r j t -> (b r j) part t"),
                                         parts[64 * g:64 * g + 64, u, m]).then_inc(stored[u], 16)
                    sp.wait_ge(v_left, FREE + 4 * k + 4)
                    for g in range(NG):
                        dst = t["v_dram"][bass.ds(b, 1), g, :, 4 * u:4 * u + 4, :]
                        sp.dma_start(dst.rearrange("b p s c -> (b p) s c"),
                                     values[:, u, :, g, :]).then_inc(stored[u], 16)
            for u in range(2):
                sp.wait_ge(stored[u], FREE + 16 * stores * B)

        @block.vector
        def _(dve):
            dve.sem_inc(norm_done, FREE)
            dve.sem_inc(low_done, FREE)
            dve.sem_inc(v_left, FREE)
            dve.wait_ge(ones_set, 1)
            with dve.Fori(0, B) as b:
                for u in range(2):
                    k = 2 * b + u
                    dve.wait_ge(norm_done, FREE + 8 * b)
                    for s in range(4):
                        nc.vector.bn_stats(stats[:, u, s, :], x[:, bass.ds(8 * b + 4 * u + s, 1), :])\
                            .then_inc(stats_done, 1)
                    dve.wait_ge(stats_done, 4 * k + 4)
                    dve.sem_inc(stats_seen, 1)
                    for s in range(4):
                        nc.vector.bn_aggr(moments[:, u, s, :], stats[:, u, s, :]).then_inc(moments_done, 1)
                for u in range(2):
                    k = 2 * b + u
                    dve.wait_ge(std_done, k + 1)
                    nc.vector.reciprocal(rstd[:, u, :], rstd[:, u, :]).then_inc(rstd_done, 1)
                    dve.wait_ge(rstd_done, k + 1)
                    dve.wait_ge(transposed, FREE + 2 * b)
                    for s in range(4):
                        nc.vector.tensor_scalar(norm[:, u, s:s + 1, :], x[:, bass.ds(8 * b + 4 * u + s, 1), :],
                                                moments[:, u, s, 0:1], rstd[:, u, s:s + 1],
                                                ALU.subtract, ALU.mult).then_inc(norm_done, 1)
                for u in range(2):
                    k = 2 * b + u
                    for m in range(4):
                        dve.wait_ge(qk_left, FREE + 2 * (4 * k + m) + 2)
                        nc.vector.tensor_tensor(qk32[:, m, :], qk32[:, m, :], parts[:, u, m, 0, :], ALU.subtract)\
                            .then_inc(rest_done, 1)
                        dve.wait_ge(rest_done, 4 * k + m + 1)
                        nc.vector.tensor_copy(parts[:, u, m, 1, :], qk32[:, m, :]).then_inc(mid_done, 1)
                        dve.wait_ge(mid_done, 4 * k + m + 1)
                        nc.vector.tensor_tensor(parts[:, u, m, 2, :], qk32[:, m, :], parts[:, u, m, 1, :],
                                                ALU.subtract).then_inc(low_done, 1)
                    for s in range(4):
                        dve.wait_ge(v_made, FREE + 2 * k + s // 2 + 1)
                        if s == 0:
                            dve.wait_ge(stored[u], FREE + 16 * stores * b)
                        dst = values[:, u, s].rearrange("p g (j c) -> p (g j) c", c=VW)[:, :, 0:HD]
                        nc.vector.tensor_tensor(
                            dst, accs[:, s // 2, s % 2 * D:s % 2 * D + D].rearrange("p (h d) -> p h d", d=HD),
                            t["b_v"][:, layer, :].rearrange("p (h d) -> p h d", d=HD), ALU.add).then_inc(v_left, 1)

        @block.scalar
        def _(act):
            act.sem_inc(normT_done, FREE)
            act.sem_inc(qk_left, FREE)
            with act.Fori(0, B) as b:
                for u in range(2):
                    act.wait_ge(moments_done, 4 * (2 * b + u) + 4)
                    nc.scalar.activation(rstd[:, u, :], moments[:, u, :, 1], ACT.Sqrt, bias=t["eps"][:, 0:1])\
                        .then_inc(std_done, 1)
                for u in range(2):
                    act.wait_ge(transposed, FREE + 2 * b + u + 1)
                    act.wait_ge(v_made, FREE + 4 * b)
                    nc.scalar.copy(normT[:, u, :], big[:, u, :]).then_inc(normT_done, 1)
                for u in range(2):
                    k = 2 * b + u
                    act.wait_ge(stored[u], FREE + 16 * stores * b)
                    for m in range(4):
                        act.wait_ge(qk_made, 4 * k + m + 1)
                        act.wait_ge(low_done, FREE + 4 * k)
                        for dst in (qk32[:, m, :], parts[:, u, m, 0, :]):
                            nc.scalar.activation(dst, ring[:, m % 2, :], ACT.Identity,
                                                 bias=t["b_qk"][:, layer, m:m + 1],
                                                 scale=scale if m < 2 else 1.0).then_inc(qk_left, 1)

        @block.tensor
        def _(pe):
            pe.sem_inc(transposed, FREE)
            pe.sem_inc(v_made, FREE)
            with pe.Fori(0, B) as b:
                for u in range(2):
                    k = 2 * b + u
                    pe.wait_ge(norm_done, FREE + 4 * k + 4)
                    pe.wait_ge(normT_done, FREE + 2 * b)
                    for s in range(4):
                        for c in range(DC):
                            last = nc.tensor.transpose(big[:, u, c * C + s * P:c * C + (s + 1) * P],
                                                       norm[:, u, s, c * P:(c + 1) * P], t["ident"][:])
                    last.then_inc(transposed, 1)
                for u in range(2):
                    k = 2 * b + u
                    pe.wait_ge(normT_done, FREE + k + 1)
                    for m in range(4):
                        if u or m >= 2:
                            pe.wait_ge(qk_left, FREE + 2 * (4 * k + m - 1))
                        else:
                            pe.wait_ge(qk_left, FREE + 16 * b)
                        for c in range(DC):
                            last = nc.tensor.matmul(ring[:, m % 2, :],
                                                    t["w_qkv"][:, layer, c, m * P:(m + 1) * P],
                                                    normT[:, u, c * C:(c + 1) * C], start=c == 0, stop=c == DC - 1)
                        last.then_inc(qk_made, 1)
                    for s in range(4):
                        if s % 2 == 0:
                            pe.wait_ge(v_left, FREE + 4 * k)
                        for c in range(DC):
                            last = nc.tensor.matmul(accs[:, s // 2, s % 2 * D:s % 2 * D + D],
                                                    normT[:, u, c * C + s * P:c * C + (s + 1) * P],
                                                    t["w_qkv"][:, layer, c, 2 * D:3 * D],
                                                    start=c == 0, stop=c == DC - 1)
                        if s % 2:
                            last.then_inc(v_made, 1)


def attend(nc, sem, layer, t):
    scores, ring, accs = t["big"], t["ring"], t["accs"]
    n = f"a{layer}_"
    with ExitStack() as ctx:
        def sb(name, shape, dt=F32):
            return ctx.enter_context(nc.sbuf_tensor(n + name, shape, dt))

        qT = sb("qT", [P, SLOTS, GH, S], BF16)
        kT = sb("kT", [P, SLOTS, GH, S], BF16)
        val = sb("val", [P, SLOTS, TB, P])
        prob = sb("prob", [P, 2, GH, S])
        tops = sb("tops", [P, SLOTS, 3, 4, GH])
        rest = sb("rest", [P, SLOTS, 2 * 4 * GH])
        topp = sb("topp", [P, SLOTS, PARTS, GH, 8], BF16)
        topT = sb("topT", [PARTS * GH * 8, SLOTS, P], BF16)
        heads = sb("heads", [P, 2, C])
        inverse = sb("inverse", [P, 2, C])
        atted = sb("atted", [P, 2, C])

        arrived = [sem(n + f"arrived{i}") for i in range(SLOTS)]
        toprows = [sem(n + f"toprows{i}") for i in range(SLOTS)]
        ring_made = sem(n + "ring_made")
        ring_free = sem(n + "ring_free")
        scores_made = sem(n + "scores_made")
        scores_free = sem(n + "scores_free")
        prob_used = sem(n + "prob_used")
        heads_left = sem(n + "heads_left")
        heads_used = sem(n + "heads_used")
        top_merged = sem(n + "top_merged")
        top_high = sem(n + "top_high")
        top_rest = sem(n + "top_rest")
        top_mid = sem(n + "top_mid")
        top_low = sem(n + "top_low")
        stored = [sem(n + f"stored{i}") for i in range(2)]

        def loop(eng, run):
            run(BEFORE, 0, 0)
            with eng.Fori(0, B - 1) as it:
                run(BODY, it, banks(BEFORE))
            run(LAST, B - 1, banks(BEFORE))

        CREDIT = 2

        def where(g):
            return g % SLOTS, g // SLOTS

        with nc.Block() as block:
            @block.sync
            def _(sp):
                def load(it, g):
                    s, more = where(g)
                    b = bass.ds(it + more, 1)
                    for block0, part, count in Q_RUNS:
                        sp.dma_start(qT[block0 * HD:(block0 + count) * HD, s],
                                     t["q_dram"][b, s, part:part + count].rearrange("b a r j t -> (b a r) j t"))\
                            .then_inc(arrived[s], 16)
                    for block0, part in K_RUNS:
                        sp.dma_start(kT[block0 * HD:(block0 + 1) * HD, s],
                                     t["k_dram"][b, s, part].rearrange("b r j t -> (b r) j t"))\
                            .then_inc(arrived[s], 16)
                    sp.dma_start(qT[QK_ROWS:K_MAX, s], t["pos_q"][layer, s]).then_inc(arrived[s], 16)
                    sp.dma_start(kT[QK_ROWS:K_EXP, s], t["pos_k"][layer, s]).then_inc(arrived[s], 16)
                    sp.dma_start(val[:, s], t["v_dram"][b, s].rearrange("b p k c -> (b p) k c"))\
                        .then_inc(arrived[s], 16)

                def run(steps, it, first):
                    r = 0
                    for step in steps:
                        g = step[1]
                        s, more = where(g)
                        if step[0] in "MTN":
                            made = first + r + it * banks(BODY)
                            r += 1
                        if step[0] == "T":
                            sp.wait_ge(ring_free, CREDIT + made + 1)
                            for part in range(PARTS):
                                rows = slice(part * GH * 8, (part + 1) * GH * 8)
                                sp.dma_start(qT[K_MAX + part:K_MAX + part + 1, s],
                                             topT[rows, s, :]).then_inc(toprows[s], 16)
                        if step[0] == "N":
                            qc = step[2]
                            sp.wait_ge(heads_used, CREDIT + 2 * (NG * it + g) + qc + 1)
                            for h in range(GH):
                                dst = t["o_dram"][bass.ds(it, 1), g * GH * HD + h * HD:g * GH * HD + (h + 1) * HD,
                                                  qc * C:(qc + 1) * C]
                                sp.dma_start(dst.rearrange("b d t -> (b d) t"),
                                             atted[h * VW:h * VW + HD, qc, :]).then_inc(stored[qc], 16)
                            if qc and steps is not LAST:
                                sp.wait_ge(prob_used, CREDIT + TB * (NG * it + g + 1))
                                load(it, g + SLOTS)

                for i in range(SLOTS):
                    sp.sem_inc(toprows[i], FREE)
                for qc in range(2):
                    sp.sem_inc(stored[qc], FREE)
                for g in range(SLOTS):
                    load(0, g)
                loop(sp, run)
                for qc in range(2):
                    sp.wait_ge(stored[qc], FREE + 16 * GH * GROUPS)

            @block.tensor
            def _(pe):
                pe.sem_inc(prob_used, CREDIT)

                def run(steps, it, first):
                    r = 0
                    for step in steps:
                        g = step[1]
                        s, more = where(g)
                        G = NG * it + g
                        if step[0] in "MTN":
                            bank = (first + r) % 2
                            made = first + r + it * banks(BODY)
                            r += 1
                        if step[0] == "M":
                            cls, hs, qb, k0, keys = MAX_UNITS[step[2]]
                            if step[2] == 0:
                                pe.wait_ge(arrived[s], 16 * LOADS * (it + more + 1))
                            pe.wait_ge(ring_free, made + 1)
                            for i, h in enumerate(hs):
                                cols = ring[:, bank, i * keys:(i + 1) * keys]
                                last = nc.tensor.matmul(cols, qT[0:K_MAX, s, h, qb * P:(qb + 1) * P],
                                                        kT[0:K_MAX, s, h, k0:k0 + keys],
                                                        start=i == 0, stop=cls == 2, skip_group_check=True)
                                if cls < 2:
                                    last = nc.tensor.matmul(cols[:, keys - P:keys], t["ident_b"][:], t["mask_max"][:],
                                                            start=False, stop=True, skip_group_check=True)
                            last.then_inc(ring_made, 1)
                        if step[0] == "T":
                            pe.wait_ge(top_low, G + 1)
                            pe.wait_ge(ring_free, made + 1)
                            nc.tensor.transpose(ring[:, bank, 0:P // 2].bitcast(BF16)[0:PARTS * GH * 8, :],
                                                topp[:, s].rearrange("p a h q -> p (a h q)"), t["ident_b"][:])\
                                .then_inc(ring_made, 1)
                        if step[0] == "N":
                            qc = step[2]
                            pe.wait_ge(heads_left, CREDIT + 2 * G + qc + 1)
                            pe.wait_ge(ring_free, made + 1)
                            nc.tensor.matmul(ring[:, bank, :], t["spread"][:], heads[:, qc, :],
                                             start=True, stop=True).then_inc(ring_made, 1)
                        if step[0] == "E":
                            _, _, kb, h = step
                            e = TB * GH * G + kb * GH + h
                            if kb == 0 and h == 0:
                                pe.wait_ge(toprows[s], FREE + 16 * PARTS * (it + more + 1))
                            pe.wait_ge(scores_free, e + 1)
                            for qc in range(kb // 4, 2):
                                q0 = max(kb * P, qc * C)
                                last = nc.tensor.matmul(scores[:, h % 2, q0:(qc + 1) * C],
                                                        kT[0:K_EXP, s, h, kb * P:(kb + 1) * P],
                                                        qT[0:K_EXP, s, h, q0:(qc + 1) * C],
                                                        start=True, stop=qc > kb // 4, skip_group_check=True)
                                if qc == kb // 4:
                                    last = nc.tensor.matmul(scores[:, h % 2, q0:q0 + P], t["ident_b"][:],
                                                            t["mask_exp"][:], start=False, stop=True,
                                                            skip_group_check=True)
                            last.then_inc(scores_made, 1)
                        if step[0] == "V":
                            kb = step[2]
                            v = TB * G + kb
                            pe.wait_ge(scores_free, CREDIT + GH * (v + 1))
                            if kb == 0:
                                pe.wait_ge(heads_left, 2 * G + 2)
                            for qc in range(kb // 4, 2):
                                q0 = max(kb * P, qc * C)
                                for h in range(GH):
                                    last = nc.tensor.matmul(accs[h * VW:(h + 1) * VW, qc, q0 - qc * C:C],
                                                            val[:, s, kb, h * VW:(h + 1) * VW],
                                                            prob[:, kb % 2, h, q0:(qc + 1) * C],
                                                            start=kb == 0, stop=kb == 4 * qc + 3,
                                                            skip_group_check=True)
                            last.then_inc(prob_used, 1)

                loop(pe, run)

            @block.scalar
            def _(act):
                act.sem_inc(scores_free, CREDIT)
                act.sem_inc(heads_left, CREDIT)

                def run(steps, it, _):
                    for step in steps:
                        G = NG * it + step[1]
                        if step[0] == "E":
                            _, _, kb, h = step
                            e = TB * GH * G + kb * GH + h
                            act.wait_ge(scores_made, e + 1)
                            if h == 0:
                                act.wait_ge(prob_used, TB * G + kb + 1)
                            nc.scalar.activation(prob[:, kb % 2, h, kb * P:S], scores[:, h % 2, kb * P:S], ACT.Exp)\
                                .then_inc(scores_free, 1)
                        if step[0] == "O":
                            qc = step[2]
                            act.wait_ge(prob_used, CREDIT + TB * G + 4 * qc + 4)
                            act.wait_ge(heads_used, 2 * G + qc + 1)
                            nc.scalar.copy(heads[:, qc, :], accs[:, qc, :]).then_inc(heads_left, 1)

                loop(act, run)

            @block.vector
            def _(dve):
                dve.sem_inc(ring_free, CREDIT)

                def run(steps, it, first):
                    r = 0
                    for step in steps:
                        g = step[1]
                        s, more = where(g)
                        G = NG * it + g
                        if step[0] in "MTN":
                            bank = (first + r) % 2
                            made = first + r + it * banks(BODY)
                            r += 1
                            dve.wait_ge(ring_made, made + 1)
                        if step[0] == "M":
                            cls, hs, qb, _, keys = MAX_UNITS[step[2]]
                            nc.vector.reduce_max(
                                tops[:, s, cls, qb % 4, hs[0]:hs[-1] + 1],
                                ring[:, bank, 0:len(hs) * keys].rearrange("p (h k) -> p h k", k=keys),
                                axis=AX_X).then_inc(ring_free, 1)
                        if step[0] == "F":
                            dve.wait_ge(ring_free, CREDIT + first + r + it * banks(BODY))
                            nc.vector.tensor_tensor(tops[:, s, 1], tops[:, s, 1], tops[:, s, 2], ALU.max)\
                                .then_inc(top_merged, 1)
                            top = tops[:, s, 0:2].rearrange("p c q h -> p (c q) h")
                            left = rest[:, s].rearrange("p (q h) -> p q h", h=GH)

                            def part(i):
                                return topp[:, s, i].rearrange("p h q -> p q h")

                            dve.wait_ge(top_merged, G + 1)
                            nc.vector.tensor_scalar(part(0), top, -1.0, None, ALU.mult).then_inc(top_high, 1)
                            dve.wait_ge(top_high, G + 1)
                            nc.vector.scalar_tensor_tensor(left, top, -1.0, part(0), ALU.mult, ALU.subtract)\
                                .then_inc(top_rest, 1)
                            dve.wait_ge(top_rest, G + 1)
                            nc.vector.tensor_copy(part(1), left).then_inc(top_mid, 1)
                            dve.wait_ge(top_mid, G + 1)
                            nc.vector.tensor_tensor(part(2), left, part(1), ALU.subtract).then_inc(top_low, 1)
                        if step[0] == "T":
                            dve.wait_ge(toprows[s], FREE + 16 * PARTS * (it + more))
                            nc.vector.tensor_copy(topT[:, s, :],
                                                  ring[:, bank, 0:P // 2].bitcast(BF16)[0:PARTS * GH * 8, :])\
                                .then_inc(ring_free, 1)
                        if step[0] == "N":
                            qc = step[2]
                            dve.wait_ge(heads_used, 2 * G + qc + 1)
                            nc.vector.reciprocal(inverse[:, qc, :], ring[:, bank, :]).then_inc(ring_free, 1)

                loop(dve, run)

            @block.gpsimd
            def _(pool):
                pool.sem_inc(heads_used, CREDIT)

                def run(steps, it, first):
                    r = 0
                    for step in steps:
                        if step[0] in "MTN":
                            made = first + r + it * banks(BODY)
                            r += 1
                        if step[0] == "N":
                            G, qc = NG * it + step[1], step[2]
                            pool.wait_ge(ring_free, CREDIT + made + 1)
                            pool.wait_ge(stored[qc], FREE + 16 * GH * G)
                            nc.gpsimd.tensor_tensor(atted[:, qc, :], heads[:, qc, :], inverse[:, qc, :], ALU.mult)\
                                .then_inc(heads_used, 1)

                loop(pool, run)


def project_out(nc, sem, layer, t):
    x, y = t["x"], t["norm"]
    stats, moments, rstd, shift, big = t["stats"], t["moments"], t["rstd"], t["shift"], t["big"]
    n = f"o{layer}_"
    arrived = [sem(n + f"arrived{u}") for u in range(2)]
    y_made = sem(n + "y_made")
    y_left = sem(n + "y_left")
    stats_done = sem(n + "stats_done")
    stats_seen = sem(n + "stats_seen")
    moments_done = sem(n + "moments_done")
    std_done = sem(n + "std_done")
    rstd_done = sem(n + "rstd_done")
    shift_done = sem(n + "shift_done")
    y_done = sem(n + "y_done")
    x_done = sem(n + "x_done")
    with nc.sbuf_tensor(n + "heads_in", [P, 2, DC, C], F32) as heads_in, nc.Block() as block:
        @block.sync
        def _(sp):
            with sp.Fori(0, B) as b:
                for u in range(2):
                    sp.wait_ge(y_made, FREE + 4 * b)
                    src = t["o_dram"][bass.ds(b, 1), :, u * C:(u + 1) * C]
                    sp.dma_start(heads_in[:, u], src.rearrange("b (c p) t -> (b p) c t", p=P))\
                        .then_inc(arrived[u], 16)

        @block.tensor
        def _(pe):
            pe.sem_inc(y_made, FREE)
            with pe.Fori(0, B) as b:
                for u in range(2):
                    pe.wait_ge(arrived[u], 16 * (b + 1))
                    pe.wait_ge(y_left, FREE + 4 * b)
                    for s in range(4):
                        for c in range(DC):
                            last = nc.tensor.matmul(big[:, u, s * D:(s + 1) * D],
                                                    heads_in[:, u, c, s * P:(s + 1) * P], t["w_out"][:, layer, c, :],
                                                    start=c == 0, stop=c == DC - 1)
                        if s % 2:
                            last.then_inc(y_made, 1)

        @block.vector
        def _(dve):
            dve.sem_inc(y_left, FREE)
            dve.sem_inc(x_done, FREE)
            with dve.Fori(0, B) as b:
                for u in range(2):
                    k = 2 * b + u
                    for half in range(2):
                        dve.wait_ge(y_made, FREE + 2 * k + half + 1)
                        if half == 0:
                            dve.wait_ge(x_done, FREE + 8 * b)
                        nc.vector.tensor_tensor(
                            y[:, u, 2 * half:2 * half + 2, :],
                            big[:, u, half * C:(half + 1) * C].rearrange("p (s d) -> p s d", d=D),
                            t["b_out"][:, layer:layer + 1, :].to_broadcast([P, 2, D]), ALU.add).then_inc(y_left, 1)
                    dve.wait_ge(y_left, FREE + 2 * k + 2)
                    for s in range(4):
                        nc.vector.bn_stats(stats[:, u, s, :], y[:, u, s, :]).then_inc(stats_done, 1)
                    dve.wait_ge(stats_done, 4 * k + 4)
                    dve.sem_inc(stats_seen, 1)
                    for s in range(4):
                        nc.vector.bn_aggr(moments[:, u, s, :], stats[:, u, s, :]).then_inc(moments_done, 1)
                for u in range(2):
                    k = 2 * b + u
                    dve.wait_ge(std_done, k + 1)
                    nc.vector.reciprocal(rstd[:, u, :], rstd[:, u, :]).then_inc(rstd_done, 1)
                    dve.wait_ge(rstd_done, k + 1)
                    nc.vector.scalar_tensor_tensor(shift[:, u, :], moments[:, u, :, 0], -1.0, rstd[:, u, :],
                                                   ALU.mult, ALU.mult).then_inc(shift_done, 1)
                for u in range(2):
                    k = 2 * b + u
                    for s in range(4):
                        dve.wait_ge(y_done, 4 * k + s + 1)
                        here = x[:, bass.ds(8 * b + 4 * u + s, 1), :]
                        nc.vector.tensor_tensor(here, here, y[:, u, s:s + 1, :], ALU.add).then_inc(x_done, 1)

        @block.scalar
        def _(act):
            with act.Fori(0, B) as b:
                for u in range(2):
                    act.wait_ge(moments_done, 4 * (2 * b + u) + 4)
                    nc.scalar.activation(rstd[:, u, :], moments[:, u, :, 1], ACT.Sqrt, bias=t["eps"][:, 0:1])\
                        .then_inc(std_done, 1)
                for u in range(2):
                    k = 2 * b + u
                    act.wait_ge(shift_done, k + 1)
                    for s in range(4):
                        nc.scalar.activation(y[:, u, s, :], y[:, u, s, :], ACT.Identity,
                                             bias=shift[:, u, s:s + 1], scale=rstd[:, u, s:s + 1])\
                            .then_inc(y_done, 1)


def experts(nc, sem, io, t):
    x, norm, normT, big, ring, accs = t["x"], t["norm"], t["normT"], t["big"], t["ring"], t["accs"]
    stats, moments, rstd, shift = t["stats"], t["moments"], t["rstd"], t["shift"]
    nt = MT_TILES
    with ExitStack() as ctx:
        def sb(name, shape, dt=F32):
            return ctx.enter_context(nc.sbuf_tensor("e_" + name, shape, dt))

        w_in = sb("w_in", [P, 2, DC, 2 * FI])
        w_down = sb("w_down", [FC, 2, 2, D])
        idx = sb("idx", [P, nt, TOPK], I32)
        idx_f = sb("idx_f", [P, nt, TOPK])
        chosen_w = sb("chosen_w", [P, nt, TOPK])
        expert_no = sb("expert_no", [P, NE])
        share = sb("share", [P, nt, TOPK, NE])
        zero = sb("zero", [P, P])
        gated = sb("gated", [P, 2, nt, FI])
        act_in = sb("act_in", [P, 2, nt, FI])
        act_inT = sb("act_inT", [FC, 2, 2, nt * P])
        y = sb("y", [P, nt, D])

        routing = sem("e_routing")
        w_arrived = [sem(f"e_w_arrived{i}") for i in range(2)]
        chain = sem("e_chain")
        moments_done = sem("e_moments_done")
        std_done = sem("e_std_done")
        share_done = sem("e_share_done")
        norm_done = sem("e_norm_done")
        transposed = sem("e_transposed")
        normT_done = sem("e_normT_done")
        in_made = sem("e_in_made")
        gate_done = sem("e_gate_done")
        act_done = sem("e_act_done")
        act_transposed = sem("e_act_transposed")
        actT_done = sem("e_actT_done")
        down_done = sem("e_down_done")
        y_done = sem("e_y_done")
        x_done = sem("e_x_done")

        with nc.Block() as block:
            @block.sync
            def _(sp):
                sp.dma_start(idx[:], io["topk_idx"].rearrange("(n p) k -> p n k", p=P)).then_inc(routing, 16)
                sp.dma_start(chosen_w[:], io["topk_weight"].rearrange("(n p) k -> p n k", p=P)).then_inc(routing, 16)
                sp.dma_start(expert_no[:], io["expert_no"]).then_inc(routing, 16)
                with sp.Fori(0, NE // 2) as i:
                    for e in range(2):
                        sp.wait_ge(down_done, FREE + 2 * i)
                        sp.dma_start(w_in[:, e], io["w_in"][bass.ds(2 * i + e, 1)].rearrange("e p c f -> (e p) c f"))\
                            .then_inc(w_arrived[e], 16)
                        sp.dma_start(w_down[:, e],
                                     io["w_down"][bass.ds(2 * i + e, 1)].rearrange("e p c f -> (e p) c f"))\
                            .then_inc(w_arrived[e], 16)

            @block.vector
            def _(dve):
                dve.sem_inc(act_done, FREE)
                dve.sem_inc(actT_done, FREE)
                steps = [0]

                def link(ins):
                    steps[0] += 1
                    ins.then_inc(chain, 1)
                    dve.wait_ge(chain, steps[0])

                for s in range(nt):
                    link(nc.vector.bn_stats(stats[:, 0, s, :], x[:, s, :]))
                    link(nc.vector.bn_aggr(moments[:, 0, s, :], stats[:, 0, s, :]))
                dve.sem_inc(moments_done, 1)
                dve.wait_ge(std_done, 1)
                link(nc.vector.reciprocal(rstd[:, 0, 0:nt], rstd[:, 0, 0:nt]))
                for s in range(nt):
                    nc.vector.tensor_scalar(norm[:, 0, s, :], x[:, s, :], moments[:, 0, s, 0:1], rstd[:, 0, s:s + 1],
                                            ALU.subtract, ALU.mult).then_inc(norm_done, 1)
                link(nc.vector.memset(zero[:], 0.0))
                dve.wait_ge(routing, 48)
                link(nc.vector.tensor_copy(idx_f[:], idx[:]))
                for s in range(nt):
                    for k in range(TOPK):
                        link(nc.vector.tensor_scalar(share[:, s, k, :], expert_no[:], idx_f[:, s, k:k + 1],
                                                     chosen_w[:, s, k:k + 1], ALU.is_equal, ALU.mult))
                for s in range(nt):
                    for k in range(1, TOPK):
                        link(nc.vector.tensor_tensor(share[:, s, 0, :], share[:, s, 0, :], share[:, s, k, :],
                                                     ALU.add))
                dve.sem_inc(share_done, 1)
                dve.wait_ge(transposed, 1)
                nc.vector.tensor_copy(normT[:, 0, 0:DC * nt * P], big[:, 0, 0:DC * nt * P]).then_inc(normT_done, 1)
                with dve.Fori(0, NE // 2) as i:
                    for e in range(2):
                        dve.wait_ge(gate_done, nt * (2 * i + e) + nt)
                        dve.wait_ge(act_transposed, FREE + 2 * i)
                        for s in range(nt):
                            nc.vector.scalar_tensor_tensor(
                                act_in[:, e, s, :], gated[:, e, s, :], share[:, s, 0, bass.ds(2 * i + e, 1)],
                                big[:, e, s * C + FI:s * C + 2 * FI], ALU.mult, ALU.mult).then_inc(act_done, 1)
                    for e in range(2):
                        dve.wait_ge(act_transposed, FREE + 2 * i + e + 1)
                        dve.wait_ge(down_done, FREE + 2 * i)
                        nc.vector.tensor_copy(act_inT[:, e].rearrange("p c t -> p (c t)"),
                                              ring[0:FC, e, :]).then_inc(actT_done, 1)
                dve.wait_ge(down_done, FREE + NE)
                link(nc.vector.tensor_copy(y[:].rearrange("p s d -> p (s d)"), accs[:, 0, :]))
                for s in range(nt):
                    link(nc.vector.bn_stats(stats[:, 0, s, :], y[:, s, :]))
                    link(nc.vector.bn_aggr(moments[:, 0, s, :], stats[:, 0, s, :]))
                dve.sem_inc(moments_done, 1)
                dve.wait_ge(std_done, 2)
                link(nc.vector.reciprocal(rstd[:, 0, 0:nt], rstd[:, 0, 0:nt]))
                for s in range(nt):
                    link(nc.vector.tensor_scalar(y[:, s, :], y[:, s, :], moments[:, 0, s, 0:1], rstd[:, 0, s:s + 1],
                                                 ALU.subtract, ALU.mult))
                    link(nc.vector.tensor_tensor(x[:, s, :], x[:, s, :], y[:, s, :], ALU.add))

            @block.scalar
            def _(act):
                def root(n):
                    act.wait_ge(moments_done, n)
                    nc.scalar.activation(rstd[:, 0, 0:nt], moments[:, 0, 0:nt, 1], ACT.Sqrt, bias=t["eps"][:, 0:1])\
                        .then_inc(std_done, 1)

                root(1)
                with act.Fori(0, NE // 2) as i:
                    for e in range(2):
                        for s in range(nt):
                            act.wait_ge(in_made, nt * (2 * i + e) + s + 1)
                            act.wait_ge(act_done, FREE + nt * 2 * i)
                            nc.scalar.activation(gated[:, e, s, :], big[:, e, s * C:s * C + FI], ACT.Silu)\
                                .then_inc(gate_done, 1)
                root(2)

            @block.tensor
            def _(pe):
                pe.sem_inc(down_done, FREE)
                pe.sem_inc(act_transposed, FREE)
                pe.wait_ge(norm_done, nt)
                for s in range(nt):
                    for c in range(DC):
                        last = nc.tensor.transpose(big[:, 0, (c * nt + s) * P:(c * nt + s + 1) * P],
                                                   norm[:, 0, s, c * P:(c + 1) * P], t["ident"][:])
                last.then_inc(transposed, 1)
                pe.wait_ge(normT_done, 1)
                pe.wait_ge(share_done, 1)
                nc.tensor.matmul(accs[:, 0, :], zero[:], normT[:, 0, 0:C], start=True, stop=True,
                                 skip_group_check=True)
                with pe.Fori(0, NE // 2) as i:
                    for e in range(2):
                        pe.wait_ge(w_arrived[e], 32 * (i + 1))
                        pe.wait_ge(act_done, FREE + nt * 2 * i)
                        for s in range(nt):
                            for c in range(DC):
                                last = nc.tensor.matmul(big[:, e, s * C:s * C + 2 * FI],
                                                        normT[:, 0, (c * nt + s) * P:(c * nt + s + 1) * P],
                                                        w_in[:, e, c, :], start=c == 0, stop=c == DC - 1)
                            last.then_inc(in_made, 1)
                    for e in range(2):
                        pe.wait_ge(act_done, FREE + nt * (2 * i + e) + nt)
                        pe.wait_ge(actT_done, FREE + 2 * i)
                        for c in range(2):
                            for s in range(nt):
                                last = nc.tensor.transpose(ring[0:FC, e, (c * nt + s) * P:(c * nt + s + 1) * P],
                                                           act_in[:, e, s, c * FC:(c + 1) * FC], t["ident"][:])
                        last.then_inc(act_transposed, 1)
                    for e in range(2):
                        pe.wait_ge(actT_done, FREE + 2 * i + e + 1)
                        for s in range(nt):
                            for c in range(2):
                                last = nc.tensor.matmul(accs[:, 0, s * D:(s + 1) * D],
                                                        act_inT[:, e, c, s * P:(s + 1) * P], w_down[:, e, c, :],
                                                        start=False, stop=True, skip_group_check=True)
                        last.then_inc(down_done, 1)


def linear(nc, sem, io, out, t):
    x, norm, normT, big, ring = t["x"], t["norm"], t["normT"], t["big"], t["ring"]
    stats, moments, rstd, shift = t["stats"], t["moments"], t["rstd"], t["shift"]
    with ExitStack() as ctx:
        def sb(name, shape, dt=F32):
            return ctx.enter_context(nc.sbuf_tensor("l_" + name, shape, dt))

        w = sb("w", [P, DC, D])
        size = sb("size", [P, DC, D])
        alpha = sb("alpha", [P, DC])
        binary = sb("binary", [P, DC, D])
        binaryT = sb("binaryT", [P, DC, D])
        bias = sb("bias", [P, 1, D])
        y = sb("y", [P, 2, 4, D])
        statsy = sb("statsy", [P, 2, 4, 6])
        momentsy = sb("momentsy", [P, 2, 4, 2])
        rstdy = sb("rstdy", [P, 2, 4])

        loaded = sem("l_loaded")
        sizes = sem("l_sizes")
        chain = sem("l_chain")
        binary_done = sem("l_binary_done")
        binary_transposed = sem("l_binary_transposed")
        binaryT_done = sem("l_binaryT_done")
        stats_done = sem("l_stats_done")
        stats_seen = sem("l_stats_seen")
        moments_done = sem("l_moments_done")
        std_done = sem("l_std_done")
        rstd_done = sem("l_rstd_done")
        norm_done = sem("l_norm_done")
        transposed = sem("l_transposed")
        normT_done = sem("l_normT_done")
        y_made = sem("l_y_made")
        y_left = sem("l_y_left")
        statsy_done = sem("l_statsy_done")
        statsy_seen = sem("l_statsy_seen")
        momentsy_done = sem("l_momentsy_done")
        stdy_done = sem("l_stdy_done")
        rstdy_done = sem("l_rstdy_done")
        shift_done = sem("l_shift_done")
        y_done = sem("l_y_done")
        x_done = sem("l_x_done")
        written = sem("l_written")

        with nc.Block() as block:
            @block.sync
            def _(sp):
                sp.dma_start(w[:], io["w_ffn"].rearrange("(c p) i -> p c i", p=P)).then_inc(loaded, 16)
                sp.dma_start(bias[:, 0, :], io["b_ffn"]).then_inc(loaded, 16)
                with sp.Fori(0, B) as b:
                    for u in range(2):
                        sp.wait_ge(x_done, FREE + 8 * b + 4 * u + 4)
                        dst = out[bass.ds(b, 1), u * C:(u + 1) * C, :]
                        sp.dma_start(dst.rearrange("b (s p) d -> p (b s) d", p=P),
                                     x[:, bass.ds(8 * b + 4 * u, 4), :]).then_inc(written, 16)
                sp.wait_ge(written, 16 * 2 * B)

            @block.scalar
            def _(act):
                act.wait_ge(loaded, 32)
                for c in range(DC):
                    nc.scalar.activation(size[:, c, :], w[:, c, :], ACT.Abs, accum_out=alpha[:, c:c + 1])\
                        .then_inc(sizes, 1)
                with act.Fori(0, B) as b:
                    for u in range(2):
                        act.wait_ge(moments_done, 4 * (2 * b + u) + 4)
                        nc.scalar.activation(rstd[:, u, :], moments[:, u, :, 1], ACT.Sqrt, bias=t["eps"][:, 0:1])\
                            .then_inc(std_done, 1)
                    for u in range(2):
                        act.wait_ge(transposed, FREE + 2 * b + u + 1)
                        act.wait_ge(y_made, FREE + 4 * b)
                        nc.scalar.copy(normT[:, u, :], big[:, u, :]).then_inc(normT_done, 1)
                    for u in range(2):
                        act.wait_ge(momentsy_done, 4 * (2 * b + u) + 4)
                        nc.scalar.activation(rstdy[:, u, :], momentsy[:, u, :, 1], ACT.Sqrt, bias=t["eps"][:, 0:1])\
                            .then_inc(stdy_done, 1)
                    for u in range(2):
                        k = 2 * b + u
                        act.wait_ge(shift_done, k + 1)
                        for s in range(4):
                            nc.scalar.activation(y[:, u, s, :], y[:, u, s, :], ACT.Identity,
                                                 bias=shift[:, u, s:s + 1], scale=rstdy[:, u, s:s + 1])\
                                .then_inc(y_done, 1)

            @block.vector
            def _(dve):
                dve.sem_inc(norm_done, FREE)
                dve.sem_inc(y_left, FREE)
                dve.sem_inc(x_done, FREE)
                steps = [0]

                def link(ins):
                    steps[0] += 1
                    ins.then_inc(chain, 1)
                    dve.wait_ge(chain, steps[0])

                dve.wait_ge(sizes, DC)
                link(nc.vector.tensor_scalar(alpha[:], alpha[:], 1.0 / D, None, ALU.mult))
                for c in range(DC):
                    link(nc.vector.tensor_scalar(binary[:, c, :], w[:, c, :], 0.0, 2.0, ALU.is_ge, ALU.mult))
                    link(nc.vector.tensor_scalar(binary[:, c, :], binary[:, c, :], -1.0, alpha[:, c:c + 1],
                                                 ALU.add, ALU.mult))
                    link(nc.vector.tensor_tensor(binary[:, c, :], binary[:, c, :], w[:, c, :], ALU.subtract))
                    link(nc.vector.tensor_tensor(binary[:, c, :], binary[:, c, :], w[:, c, :], ALU.add))
                dve.sem_inc(binary_done, 1)
                dve.wait_ge(binary_transposed, 1)
                nc.vector.tensor_copy(binaryT[:].rearrange("p c o -> p (c o)"), ring[:, 0, :]).then_inc(binaryT_done, 1)
                with dve.Fori(0, B) as b:
                    for u in range(2):
                        k = 2 * b + u
                        dve.wait_ge(norm_done, FREE + 8 * b)
                        for s in range(4):
                            nc.vector.bn_stats(stats[:, u, s, :], x[:, bass.ds(8 * b + 4 * u + s, 1), :])\
                                .then_inc(stats_done, 1)
                        dve.wait_ge(stats_done, 4 * k + 4)
                        dve.sem_inc(stats_seen, 1)
                        for s in range(4):
                            nc.vector.bn_aggr(moments[:, u, s, :], stats[:, u, s, :]).then_inc(moments_done, 1)
                    for u in range(2):
                        k = 2 * b + u
                        dve.wait_ge(std_done, k + 1)
                        nc.vector.reciprocal(rstd[:, u, :], rstd[:, u, :]).then_inc(rstd_done, 1)
                        dve.wait_ge(rstd_done, k + 1)
                        dve.wait_ge(transposed, FREE + 2 * b)
                        for s in range(4):
                            nc.vector.tensor_scalar(norm[:, u, s:s + 1, :], x[:, bass.ds(8 * b + 4 * u + s, 1), :],
                                                    moments[:, u, s, 0:1], rstd[:, u, s:s + 1],
                                                    ALU.subtract, ALU.mult).then_inc(norm_done, 1)
                    for u in range(2):
                        k = 2 * b + u
                        for half in range(2):
                            dve.wait_ge(y_made, FREE + 2 * k + half + 1)
                            if half == 0:
                                dve.wait_ge(x_done, FREE + 8 * b)
                            nc.vector.tensor_tensor(
                                y[:, u, 2 * half:2 * half + 2, :],
                                big[:, u, half * C:(half + 1) * C].rearrange("p (s d) -> p s d", d=D),
                                bias[:].to_broadcast([P, 2, D]), ALU.add).then_inc(y_left, 1)
                        dve.wait_ge(y_left, FREE + 2 * k + 2)
                        for s in range(4):
                            nc.vector.bn_stats(statsy[:, u, s, :], y[:, u, s, :]).then_inc(statsy_done, 1)
                        dve.wait_ge(statsy_done, 4 * k + 4)
                        dve.sem_inc(statsy_seen, 1)
                        for s in range(4):
                            nc.vector.bn_aggr(momentsy[:, u, s, :], statsy[:, u, s, :]).then_inc(momentsy_done, 1)
                    for u in range(2):
                        k = 2 * b + u
                        dve.wait_ge(stdy_done, k + 1)
                        nc.vector.reciprocal(rstdy[:, u, :], rstdy[:, u, :]).then_inc(rstdy_done, 1)
                        dve.wait_ge(rstdy_done, k + 1)
                        nc.vector.scalar_tensor_tensor(shift[:, u, :], momentsy[:, u, :, 0], -1.0, rstdy[:, u, :],
                                                       ALU.mult, ALU.mult).then_inc(shift_done, 1)
                    for u in range(2):
                        k = 2 * b + u
                        for s in range(4):
                            dve.wait_ge(y_done, 4 * k + s + 1)
                            here = x[:, bass.ds(8 * b + 4 * u + s, 1), :]
                            nc.vector.tensor_tensor(here, here, y[:, u, s:s + 1, :], ALU.add).then_inc(x_done, 1)

            @block.tensor
            def _(pe):
                pe.sem_inc(transposed, FREE)
                pe.sem_inc(y_made, FREE)
                pe.wait_ge(binary_done, 1)
                for co in range(DC):
                    for ci in range(DC):
                        last = nc.tensor.transpose(ring[:, 0, ci * D + co * P:ci * D + (co + 1) * P],
                                                   binary[:, co, ci * P:(ci + 1) * P], t["ident"][:])
                last.then_inc(binary_transposed, 1)
                pe.wait_ge(binaryT_done, 1)
                with pe.Fori(0, B) as b:
                    for u in range(2):
                        k = 2 * b + u
                        pe.wait_ge(norm_done, FREE + 4 * k + 4)
                        pe.wait_ge(y_left, FREE + 4 * b)
                        for s in range(4):
                            for c in range(DC):
                                last = nc.tensor.transpose(big[:, u, c * C + s * P:c * C + (s + 1) * P],
                                                           norm[:, u, s, c * P:(c + 1) * P], t["ident"][:])
                        last.then_inc(transposed, 1)
                    for u in range(2):
                        k = 2 * b + u
                        pe.wait_ge(normT_done, k + 1)
                        for s in range(4):
                            for c in range(DC):
                                last = nc.tensor.matmul(big[:, u, s * D:(s + 1) * D],
                                                        normT[:, u, c * C + s * P:c * C + (s + 1) * P],
                                                        binaryT[:, c, :], start=c == 0, stop=c == DC - 1)
                            if s % 2:
                                last.then_inc(y_made, 1)



def three_parts(a):
    bf16 = mybir.dt.np(BF16)
    high = a.astype(bf16)
    rest = a - high.astype(np.float32)
    mid = rest.astype(bf16)
    low = (rest - mid.astype(np.float32)).astype(bf16)
    return [p.astype(np.float32) for p in (high, mid, low)]


def constants():
    bf16 = mybir.dt.np(BF16)
    i = np.arange(P)
    pos = np.arange(S)
    near, far = (pos % P).astype(np.float32), (pos // P * P).astype(np.float32)
    start = 2.0 ** (-2.0 ** (-(np.log2(NH) - 3)))
    slopes = np.array([start * start ** n for n in range(NH)]).astype(np.float32).reshape(NG, GH)
    pos_q = np.zeros((2, NG, POS_ROWS, GH, S), np.float32)
    pos_k = np.zeros((2, NG, POS_ROWS + MAX_ROWS, GH, S), np.float32)
    pos_k[:, :, POS_ROWS:] = 1.0
    for n, part in enumerate(three_parts(slopes)):
        for m, place in enumerate((far, near)):
            row = 4 * n + 2 * m
            pos_q[1, :, row] = part[:, :, None]
            pos_k[1, :, row] = place
            pos_q[1, :, row + 1] = -place
            pos_k[1, :, row + 1] = part[:, :, None]
    return {
        "ident": np.eye(P, dtype=np.float32),
        "ident_b": np.eye(P, dtype=bf16),
        "mask_exp": np.where(i[:, None] > i[None, :], MASKED, 0.0).astype(bf16),
        "mask_max": np.where(i[None, :] > i[:, None], MASKED, 0.0).astype(bf16),
        "spread": (i[:, None] == i[None, :] // VW * VW + HD).astype(np.float32),
        "pos_q": pos_q.astype(bf16),
        "pos_k": pos_k.astype(bf16),
        "expert_no": np.broadcast_to(np.arange(NE, dtype=np.float32), (P, NE)),
    }


def layouts(a):
    order = np.arange(2 * D).reshape(4, 2, GH, HD).transpose(0, 1, 3, 2).reshape(-1)
    order = np.concatenate([order, np.arange(2 * D, 3 * D)])
    w_qkv = np.stack([a["L0_attn_w_qkv"].T, a["L1_attn_w_qkv"]])[:, :, order]
    b_qkv = np.stack([a["L0_attn_b_qkv"], a["L1_attn_b_qkv"]])
    w_out = np.stack([a["L0_attn_w_out"].T, a["L1_attn_w_proj"]])
    rows = (P, 2, D)
    w_in = np.concatenate([a["L0_ffn_gate_weight"], a["L0_ffn_up_weight"]], axis=1)
    return {
        "x": a["L0_attn_x"].reshape(B * S, D),
        "w_qkv": w_qkv.reshape(2, DC, P, 3 * D).transpose(2, 0, 1, 3),
        "b_qk": b_qkv[:, order[:2 * D]].reshape(2, 4, P).transpose(2, 0, 1),
        "b_v": np.broadcast_to(b_qkv[:, 2 * D:], rows),
        "w_out": w_out.reshape(2, DC, P, D).transpose(2, 0, 1, 3),
        "b_out": np.broadcast_to(np.stack([a["L0_attn_b_out"], a["L1_attn_b_proj"]]), rows),
        "w_in": w_in.transpose(0, 2, 1).reshape(NE, DC, P, 2 * FI).transpose(0, 2, 1, 3),
        "w_down": a["L0_ffn_down_weight"].transpose(0, 2, 1).reshape(NE, 2, FC, D).transpose(0, 2, 1, 3),
        "topk_idx": a["L0_ffn_topk_idx"].reshape(MT_TILES * P, TOPK),
        "topk_weight": a["L0_ffn_topk_weight"].reshape(MT_TILES * P, TOPK),
        "w_ffn": a["L1_ffn_weight"],
        "b_ffn": np.broadcast_to(a["L1_ffn_bias"], (P, D)),
    }


def kernel(**inputs):
    import concourse.bacc as bacc
    from concourse.bass_utils import run_bass_kernel_spmd

    nc = bacc.Bacc("TRN2", target_bir_lowering=False, num_devices=1)
    a = {name: np.asarray(v) for name, v in inputs.items()}
    arrays = {name: np.ascontiguousarray(v) for name, v in {**layouts(a), **constants()}.items()}
    io = {name: nc.dram_tensor(f"in_{name}", v.shape, mybir.dt.from_np(v.dtype), kind="ExternalInput").ap()
          for name, v in arrays.items()}
    out = nc.dram_tensor("out_x", (B, S, D), F32, kind="ExternalOutput").ap()
    sandwich(nc, io, out)
    result = run_bass_kernel_spmd(nc, [{f"in_{name}": v for name, v in arrays.items()}], core_ids=[0])
    return result.results[0]["out_x"]
```

```python
from contextlib import ExitStack

import numpy as np

import concourse.bass as bass
from concourse import mybir

F32 = mybir.dt.float32
BF16 = mybir.dt.bfloat16
I32 = mybir.dt.int32
ALU = mybir.AluOpType
ACT = mybir.ActivationFunctionType
AX_X = mybir.AxisListType.X

P = 128
B, S, D = 4, 1024, 256
NH, HD = 16, 16
DC = D // P
NT = B * S // P
TB = S // P
NG = 4
GH = NH // NG
VW = P // GH
C = 512
NE, FI, TOPK = 16, 176, 4
FC = FI // 2
MT_TILES = 2
EPS = 1e-5
MASKED = -1e30
OFFSET = 16.0

PARTS = 3
QK_ROWS = 6 * HD
POS_ROWS = 12
MAX_ROWS = PARTS
K_MAX = QK_ROWS + POS_ROWS
K_EXP = K_MAX + MAX_ROWS
Q_RUNS = [(0, 0, 3), (3, 0, 2), (5, 0, 1)]
K_RUNS = [(0, 0), (1, 0), (2, 0), (3, 1), (4, 1), (5, 2)]
LOADS = len(Q_RUNS) + len(K_RUNS) + 3
SLOTS = 4
LEAD = 11
GROUPS = B * NG
DEPTH = 3
PROBS = 4
FREE = 3


def maximum_units():
    units = []
    for cls in (0, 1):
        for n in range(1, 5):
            per = 4 // n if n < 3 else 1
            for h in range(0, GH, per):
                units.append((cls, list(range(h, h + per)), 4 * cls + n - 1, cls * C, n * P))
    for qb in range(4, 8):
        for h in range(GH):
            units.append((2, [h], qb, 0, C))
    return units


MAX_UNITS = maximum_units()


BLOCKS = [(kb, qc) for kb in range(TB) for qc in range(kb * P // C, S // C)]
DIAGONAL = [BLOCKS.index((kb, kb * P // C)) for kb in range(TB)]
ORDER = ("EEEMMEEMEMEEMEVEEEMMEMEEMEMEMEMVEEEMMEEMEMVEEMEMEMVEEEMMEMVE"
         "EEMMEMVEEEMMEMMVEEMEMEMVEEEVEMMVMMMVMVMM")


def attention_steps():
    ahead = []
    for g in range(GROUPS + 2):
        units = [("M", g, i) for i in range(len(MAX_UNITS))]
        ahead += units[:3] + [("T", g - 1)] + units[3:] + [("F", g)]
    per_group = len(MAX_UNITS) + 2
    assert ORDER.count("M") == per_group

    def real(steps):
        return [s for s in steps if 0 <= s[1] < GROUPS]

    at = per_group + LEAD
    before, groups = real(ahead[:at]), []
    for g in range(GROUPS):
        own = {"E": iter([("E", g, n, h) for n in range(len(BLOCKS)) for h in range(GH)]),
               "V": iter([("V", g, n) for n in range(len(BLOCKS))]),
               "M": iter(ahead[at:at + per_group])}
        at += per_group
        steps = []
        for kind in ORDER:
            steps.append(next(own[kind]))
            if kind == "V" and BLOCKS[steps[-1][2]] in ((3, 0), (7, 1)):
                steps.append(("O", g, BLOCKS[steps[-1][2]][1]))
        assert all(next(i, None) is None for i in own.values())
        groups.append(real(steps))
    return before, groups


def relative(groups, it):
    return [(s[0], s[1] - NG * it, *s[2:]) for group in groups[NG * it:NG * (it + 1)] for s in group]


BEFORE, STEPS = attention_steps()
BODY = relative(STEPS, 0)
LAST = relative(STEPS, B - 1)
assert BODY == relative(STEPS, 1) == relative(STEPS, B - 2)


def banks(steps):
    return sum(s[0] in "MT" for s in steps)


def sandwich(nc, io, out):
    with ExitStack() as ctx:
        def sb(name, shape, dt=F32):
            return ctx.enter_context(nc.sbuf_tensor(name, shape, dt))

        in_use = []

        def sem(name):
            in_use.append(nc.alloc_semaphore(name))
            return in_use[-1]

        def stage_ends():
            nc.clear_and_free_semaphores(in_use)
            nc.all_engine_barrier()
            in_use.clear()

        q_dram = nc.dram_tensor("q_parts", [B, NG, PARTS, HD, GH, S], BF16).ap()
        k_dram = nc.dram_tensor("k_parts", [B, NG, PARTS, HD, GH, S], BF16).ap()
        v_dram = nc.dram_tensor("values", [B, NG, P, TB, P], F32).ap()
        o_dram = nc.dram_tensor("heads", [B, NG, P, S], F32).ap()
        i_dram = nc.dram_tensor("inverses", [B * NH, S], F32).ap()

        x = sb("x", [P, NT, D])
        w_qkv = sb("w_qkv", [P, 2, DC, 3 * D])
        b_qk = sb("b_qk", [P, 2, 4])
        b_v = sb("b_v", [P, 2, D])
        w_out = sb("w_out", [P, 2, DC, D])
        b_out = sb("b_out", [P, 2, D])
        ident = sb("ident", [P, P])
        ident_b = sb("ident_b", [P, P], BF16)
        mask_max = sb("mask_max", [P, P], BF16)
        eps = sb("eps", [P, 1])
        stats = sb("stats", [P, 2, 4, 6])
        moments = sb("moments", [P, 2, 4, 2])
        rstd = sb("rstd", [P, 2, 4])
        shift = sb("shift", [P, 2, 4])
        norm = sb("norm", [P, 2, 4, D])
        normT = sb("normT", [P, 2, DC * C])

        psum = ctx.enter_context(nc.psum_tensor("psum", [P, 8, C], F32))
        big = psum[:, 0:4, :].rearrange("p (u h) c -> p u (h c)", u=2)
        ring, accs = psum[:, 4:6, :], psum[:, 6:8, :]

        loaded, weights_loaded, rest_loaded, eps_set = (sem(name) for name in (
            "loaded", "weights_loaded", "rest_loaded", "eps_set"))
        small = [(ident[:], io["ident"]), (b_qk[:], io["b_qk"]), (b_v[:], io["b_v"])]
        later = [(w_qkv[:, 1], io["w_qkv"][:, 1]), (w_out[:], io["w_out"]), (b_out[:], io["b_out"]), (ident_b[:], io["ident_b"]),
                 (mask_max[:], io["mask_max"])]
        with nc.Block() as block:
            @block.sync
            def _(sp):
                for dst, src in small:
                    sp.dma_start(dst, src).then_inc(loaded, 16)
                sp.dma_start(w_qkv[:, 0], io["w_qkv"][:, 0]).then_inc(weights_loaded, 16)
                for dst, src in later:
                    sp.dma_start(dst, src).then_inc(rest_loaded, 16)

            @block.vector
            def _(dve):
                nc.vector.memset(eps[:], EPS).then_inc(eps_set, 1)

        for layer in range(2):
            project_qkv(nc, sem, layer, dict(
                x=x, w_qkv=w_qkv, b_qk=b_qk, b_v=b_v, ident=ident, eps=eps, stats=stats, moments=moments, rstd=rstd,
                norm=norm, normT=normT, big=big, ring=ring, accs=accs,
                q_dram=q_dram, k_dram=k_dram, v_dram=v_dram, x_dram=io["x"], loaded=loaded, loads=len(small),
                weights_loaded=weights_loaded, rest_loaded=rest_loaded, rest_loads=len(later), eps_set=eps_set))
            stage_ends()
            attend(nc, sem, layer, dict(
                ident_b=ident_b, mask_max=mask_max, psum=psum,
                q_dram=q_dram, k_dram=k_dram, v_dram=v_dram, o_dram=o_dram, pos_q=io["pos_q"], pos_k=io["pos_k"]))
            stage_ends()
            project_out(nc, sem, layer, dict(
                x=x, w_out=w_out, b_out=b_out, eps=eps, stats=stats, moments=moments, rstd=rstd, shift=shift, norm=norm, big=big, o_dram=o_dram, i_dram=i_dram))
            stage_ends()
            if layer == 0:
                experts(nc, sem, io, dict(
                    x=x, ident=ident, eps=eps, stats=stats, moments=moments, rstd=rstd, shift=shift, norm=norm, normT=normT,
                    big=big, ring=ring, accs=accs))
                stage_ends()
        linear(nc, sem, io, out, dict(
            x=x, ident=ident, eps=eps, stats=stats, moments=moments, rstd=rstd, shift=shift, norm=norm, normT=normT,
            big=big, ring=ring))


def project_qkv(nc, sem, layer, t):
    x, norm, normT = t["x"], t["norm"], t["normT"]
    stats, moments, rstd = t["stats"], t["moments"], t["rstd"]
    big, ring, accs = t["big"], t["ring"], t["accs"]
    scale = (0.25, 0.0625)[layer]
    n = f"p{layer}_"
    stats_done = sem(n + "stats_done")
    stats_seen = sem(n + "stats_seen")
    moments_done = sem(n + "moments_done")
    std_done = sem(n + "std_done")
    rstd_done = sem(n + "rstd_done")
    norm_done = sem(n + "norm_done")
    transposed = sem(n + "transposed")
    normT_done = sem(n + "normT_done")
    qk_made = sem(n + "qk_made")
    qk_left = sem(n + "qk_left")
    rest_done = sem(n + "rest_done")
    mid_done = sem(n + "mid_done")
    low_done = sem(n + "low_done")
    v_made = sem(n + "v_made")
    v_left = sem(n + "v_left")
    stored = [sem(n + f"stored{u}") for u in range(2)]
    ones_set = sem(n + "ones_set")
    stores = 4 * 2 + NG
    if layer == 0:
        x_arrived = sem(n + "x_arrived")
        bias_scaled = sem(n + "bias_scaled")

    with (nc.sbuf_tensor(n + "qk32", [P, 4, C], F32) as qk32,
          nc.sbuf_tensor(n + "parts", [P, 2, 4, PARTS, C], BF16) as parts,
          nc.sbuf_tensor(n + "values", [P, 2, 4, NG, P], F32) as values,
          nc.Block() as block):
        @block.gpsimd
        def _(pool):
            nc.gpsimd.memset(values[:], 1.0).then_inc(ones_set, 1)
            if layer == 0:
                with pool.Fori(0, B) as b:
                    pool.dma_start(x[:, bass.ds(TB * b, TB), :],
                                   t["x_dram"][bass.ds(S * b, S), :].rearrange("(t p) d -> p t d", p=P))\
                        .then_inc(x_arrived, 16)
                    pool.wait_ge(x_arrived, 16 * (b + 1))

        @block.sync
        def _(sp):
            sp.sem_inc(stored[0], FREE)
            sp.sem_inc(stored[1], FREE)
            with sp.Fori(0, B) as b:
                for u in range(2):
                    k = 2 * b + u
                    for m in range(4):
                        sp.wait_ge(low_done, FREE + 4 * k + m + 1)
                        dram = (t["q_dram"], t["k_dram"])[m // 2]
                        for g in range(2):
                            dst = dram[bass.ds(b, 1), 2 * (m % 2) + g, :, :, :, u * C:(u + 1) * C]
                            sp.dma_start(dst.rearrange("b part r j t -> (b r j) part t"),
                                         parts[64 * g:64 * g + 64, u, m]).then_inc(stored[u], 16)
                    sp.wait_ge(v_left, FREE + 4 * k + 4)
                    for g in range(NG):
                        dst = t["v_dram"][bass.ds(b, 1), g, :, 4 * u:4 * u + 4, :]
                        sp.dma_start(dst.rearrange("b p s c -> (b p) s c"),
                                     values[:, u, :, g, :]).then_inc(stored[u], 16)
            for u in range(2):
                sp.wait_ge(stored[u], FREE + 16 * stores * B)
            if layer == 0:
                sp.wait_ge(t["rest_loaded"], 16 * t["rest_loads"])

        @block.vector
        def _(dve):
            dve.sem_inc(norm_done, FREE)
            dve.sem_inc(low_done, FREE)
            dve.sem_inc(v_left, FREE)

            def statistics(b, u):
                k = 2 * b + u
                if layer == 0:
                    dve.wait_ge(x_arrived, 16 * (b + 1))
                dve.wait_ge(norm_done, FREE + 8 * b)
                for s in range(4):
                    nc.vector.bn_stats(stats[:, u, s, :], x[:, bass.ds(8 * b + 4 * u + s, 1), :])\
                        .then_inc(stats_done, 1)
                dve.wait_ge(stats_done, 4 * k + 4)
                dve.sem_inc(stats_seen, 1)
                for s in range(4):
                    nc.vector.bn_aggr(moments[:, u, s, :], stats[:, u, s, :]).then_inc(moments_done, 1)

            def normalise(b, u):
                k = 2 * b + u
                dve.wait_ge(std_done, k + 1)
                nc.vector.reciprocal(rstd[:, u, :], rstd[:, u, :]).then_inc(rstd_done, 1)
                dve.wait_ge(rstd_done, k + 1)
                dve.wait_ge(transposed, FREE + 2 * b)
                for s in range(4):
                    nc.vector.tensor_scalar(norm[:, u, s:s + 1, :], x[:, bass.ds(8 * b + 4 * u + s, 1), :],
                                            moments[:, u, s, 0:1], rstd[:, u, s:s + 1],
                                            ALU.subtract, ALU.mult).then_inc(norm_done, 1)

            def split(b, u, m):
                k = 2 * b + u
                dve.wait_ge(qk_left, FREE + 2 * (4 * k + m) + 2)
                nc.vector.tensor_tensor(qk32[:, m, :], qk32[:, m, :], parts[:, u, m, 0, :], ALU.subtract)\
                    .then_inc(rest_done, 1)
                dve.wait_ge(rest_done, 4 * k + m + 1)
                nc.vector.tensor_copy(parts[:, u, m, 1, :], qk32[:, m, :]).then_inc(mid_done, 1)
                dve.wait_ge(mid_done, 4 * k + m + 1)
                nc.vector.tensor_tensor(parts[:, u, m, 2, :], qk32[:, m, :], parts[:, u, m, 1, :],
                                        ALU.subtract).then_inc(low_done, 1)

            def value(b, u, s):
                dve.wait_ge(v_made, FREE + 2 * (2 * b + u) + s // 2 + 1)
                if s == 0:
                    dve.wait_ge(stored[u], FREE + 16 * stores * b)
                dst = values[:, u, s].rearrange("p g (j c) -> p (g j) c", c=VW)[:, :, 0:HD]
                nc.vector.tensor_tensor(
                    dst, accs[:, s // 2, s % 2 * D:s % 2 * D + D].rearrange("p (h d) -> p h d", d=HD),
                    t["b_v"][:, layer, :].rearrange("p (h d) -> p h d", d=HD), ALU.add).then_inc(v_left, 1)

            def chunk(b, u, more):
                if more:
                    statistics(b + 1, u)
                split(b, u, 0)
                if more:
                    normalise(b + 1, u)
                for m in range(1, 4):
                    split(b, u, m)
                for s in range(4):
                    value(b, u, s)

            for u in range(2):
                statistics(0, u)
            for u in range(2):
                normalise(0, u)
            dve.wait_ge(ones_set, 1)
            if layer == 0:
                dve.wait_ge(t["loaded"], 16 * t["loads"])
                for other in range(2):
                    nc.vector.tensor_scalar(t["b_qk"][:, other, 0:2], t["b_qk"][:, other, 0:2], (0.25, 0.0625)[other],
                                            None, ALU.mult).then_inc(bias_scaled, 1)
            with dve.Fori(0, B - 1) as b:
                for u in range(2):
                    chunk(b, u, True)
            for u in range(2):
                chunk(B - 1, u, False)

        @block.scalar
        def _(act):
            act.sem_inc(normT_done, FREE)
            act.sem_inc(qk_left, FREE)

            def root(b, u):
                act.wait_ge(moments_done, 4 * (2 * b + u) + 4)
                nc.scalar.activation(rstd[:, u, :], moments[:, u, :, 1], ACT.Sqrt, bias=t["eps"][:, 0:1])\
                    .then_inc(std_done, 1)

            def copy(b, u):
                act.wait_ge(transposed, FREE + 2 * b + u + 1)
                act.wait_ge(v_made, FREE + 2 * (2 * b + u - 1))
                nc.scalar.copy(normT[:, u, :], big[:, u, :]).then_inc(normT_done, 1)

            def evacuate(b, u, m):
                k = 2 * b + u
                act.wait_ge(qk_made, 4 * k + m + 1)
                act.wait_ge(low_done, FREE + 4 * k)
                for dst in (qk32[:, m, :], parts[:, u, m, 0, :]):
                    nc.scalar.activation(dst, ring[:, m % 2, :], ACT.Identity, bias=t["b_qk"][:, layer, m:m + 1],
                                         scale=scale if m < 2 else 1.0).then_inc(qk_left, 1)

            def chunk(b, u, more):
                act.wait_ge(stored[u], FREE + 16 * stores * b)
                evacuate(b, u, 0)
                if more:
                    root(b + 1, u)
                for m in range(1, 4):
                    evacuate(b, u, m)
                if more:
                    copy(b + 1, u)

            if layer == 0:
                act.wait_ge(t["eps_set"], 1)
            for u in range(2):
                root(0, u)
            for u in range(2):
                copy(0, u)
            if layer == 0:
                act.wait_ge(bias_scaled, 2)
            with act.Fori(0, B - 1) as b:
                for u in range(2):
                    chunk(b, u, True)
            for u in range(2):
                chunk(B - 1, u, False)

        @block.tensor
        def _(pe):
            pe.sem_inc(transposed, FREE)
            pe.sem_inc(v_made, FREE)

            def transpose(b, u):
                pe.wait_ge(norm_done, FREE + 4 * (2 * b + u) + 4)
                pe.wait_ge(normT_done, FREE + 2 * b)
                for s in range(4):
                    for c in range(DC):
                        last = nc.tensor.transpose(big[:, u, c * C + s * P:c * C + (s + 1) * P],
                                                   norm[:, u, s, c * P:(c + 1) * P], t["ident"][:])
                last.then_inc(transposed, 1)

            def products(b, u):
                k = 2 * b + u
                pe.wait_ge(normT_done, FREE + k + 1)
                for m in range(4):
                    if u or m >= 2:
                        pe.wait_ge(qk_left, FREE + 2 * (4 * k + m - 1))
                    else:
                        pe.wait_ge(qk_left, FREE + 16 * b)
                    for c in range(DC):
                        last = nc.tensor.matmul(ring[:, m % 2, :],
                                                t["w_qkv"][:, layer, c, m * P:(m + 1) * P],
                                                normT[:, u, c * C:(c + 1) * C], start=c == 0, stop=c == DC - 1)
                    last.then_inc(qk_made, 1)
                for s in range(4):
                    if s % 2 == 0:
                        pe.wait_ge(v_left, FREE + 4 * k)
                    for c in range(DC):
                        last = nc.tensor.matmul(accs[:, s // 2, s % 2 * D:s % 2 * D + D],
                                                normT[:, u, c * C + s * P:c * C + (s + 1) * P],
                                                t["w_qkv"][:, layer, c, 2 * D:3 * D],
                                                start=c == 0, stop=c == DC - 1)
                    if s % 2:
                        last.then_inc(v_made, 1)

            if layer == 0:
                pe.wait_ge(t["loaded"], 16 * t["loads"])
            for u in range(2):
                transpose(0, u)
            if layer == 0:
                pe.wait_ge(t["weights_loaded"], 16)
            with pe.Fori(0, B - 1) as b:
                for u in range(2):
                    products(b, u)
                    transpose(b + 1, u)
            for u in range(2):
                products(B - 1, u)


def attend(nc, sem, layer, t):
    scores, ring, accs = t["psum"][:, 0:DEPTH, :], t["psum"][:, DEPTH:2 * DEPTH, :], t["psum"][:, 6:8, :]
    n = f"a{layer}_"
    with ExitStack() as ctx:
        def sb(name, shape, dt=F32):
            return ctx.enter_context(nc.sbuf_tensor(n + name, shape, dt))

        qT = sb("qT", [P, SLOTS, GH, S], BF16)
        kT = sb("kT", [P, SLOTS, GH, S], BF16)
        val = sb("val", [P, SLOTS, TB, P])
        prob = sb("prob", [P, PROBS, GH, C])
        tops = sb("tops", [P, SLOTS, 3, 4, GH])
        rest = sb("rest", [P, SLOTS, 2 * 4 * GH])
        topp = sb("topp", [P, SLOTS, PARTS, GH, 8], BF16)
        topT = sb("topT", [PARTS * GH * 8, SLOTS, P], BF16)
        heads = sb("heads", [P, 2, C])

        arrived = [sem(n + f"arrived{i}") for i in range(SLOTS)]
        toprows = [sem(n + f"toprows{i}") for i in range(SLOTS)]
        ring_made = sem(n + "ring_made")
        ring_free = sem(n + "ring_free")
        scores_made = sem(n + "scores_made")
        scores_free = sem(n + "scores_free")
        prob_used = sem(n + "prob_used")
        heads_left = sem(n + "heads_left")
        top_merged = sem(n + "top_merged")
        top_high = sem(n + "top_high")
        top_rest = sem(n + "top_rest")
        top_mid = sem(n + "top_mid")
        top_low = sem(n + "top_low")
        stored = [sem(n + f"stored{i}") for i in range(2)]

        def loop(eng, run):
            run(BEFORE, 0, 0)
            with eng.Fori(0, B - 1) as it:
                run(BODY, it, banks(BEFORE))
            run(LAST, B - 1, banks(BEFORE))

        n_blocks = len(BLOCKS)
        causal = sem(n + "causal")
        exps_seen = sem(n + "exps_seen")

        def where(g):
            return g % SLOTS, g // SLOTS

        with nc.Block() as block:
            @block.sync
            def _(sp):
                def load(it, g):
                    s, more = where(g)
                    b = bass.ds(it + more, 1)
                    for block0, part, count in Q_RUNS:
                        sp.dma_start(qT[block0 * HD:(block0 + count) * HD, s],
                                     t["q_dram"][b, s, part:part + count].rearrange("b a r j t -> (b a r) j t"))\
                            .then_inc(arrived[s], 16)
                    for block0, part in K_RUNS:
                        sp.dma_start(kT[block0 * HD:(block0 + 1) * HD, s],
                                     t["k_dram"][b, s, part].rearrange("b r j t -> (b r) j t"))\
                            .then_inc(arrived[s], 16)
                    sp.dma_start(qT[QK_ROWS:K_MAX, s], t["pos_q"][layer, s]).then_inc(arrived[s], 16)
                    sp.dma_start(kT[QK_ROWS:K_EXP, s], t["pos_k"][layer, s]).then_inc(arrived[s], 16)
                    sp.dma_start(val[:, s], t["v_dram"][b, s].rearrange("b p k c -> (b p) k c"))\
                        .then_inc(arrived[s], 16)

                def run(steps, it, first):
                    r = 0
                    for step in steps:
                        g = step[1]
                        s, more = where(g)
                        if step[0] in "MT":
                            made = first + r + it * banks(BODY)
                            r += 1
                        if step[0] == "T":
                            sp.wait_ge(ring_free, DEPTH + made + 1)
                            for part in range(PARTS):
                                rows = slice(part * GH * 8, (part + 1) * GH * 8)
                                sp.dma_start(qT[K_MAX + part:K_MAX + part + 1, s],
                                             topT[rows, s, :]).then_inc(toprows[s], 16)
                        if step[0] == "O":
                            qc = step[2]
                            sp.wait_ge(heads_left, 2 + 2 * (NG * it + g) + qc + 1)
                            dst = t["o_dram"][bass.ds(it, 1), g, :, qc * C:(qc + 1) * C]
                            sp.dma_start(dst.rearrange("b r t -> (b r) t"), heads[:, qc, :])\
                                .then_inc(stored[qc], 16)
                            if qc and steps is not LAST:
                                sp.wait_ge(prob_used, PROBS + n_blocks * (NG * it + g + 1))
                                load(it, g + SLOTS)

                for i in range(SLOTS):
                    sp.sem_inc(toprows[i], FREE)
                for qc in range(2):
                    sp.sem_inc(stored[qc], FREE)
                for g in range(SLOTS):
                    load(0, g)
                loop(sp, run)
                for qc in range(2):
                    sp.wait_ge(stored[qc], FREE + 16 * GROUPS)

            @block.tensor
            def _(pe):
                pe.sem_inc(prob_used, PROBS)

                def run(steps, it, first):
                    r = 0
                    for step in steps:
                        g = step[1]
                        s, more = where(g)
                        G = NG * it + g
                        if step[0] in "MT":
                            bank = (first + r) % DEPTH
                            made = first + r + it * banks(BODY)
                            r += 1
                        if step[0] == "M":
                            cls, hs, qb, k0, keys = MAX_UNITS[step[2]]
                            if step[2] == 0:
                                pe.wait_ge(arrived[s], 16 * LOADS * (it + more + 1))
                            pe.wait_ge(ring_free, made + 1)
                            for i, h in enumerate(hs):
                                cols = ring[:, bank, i * keys:(i + 1) * keys]
                                last = nc.tensor.matmul(cols, qT[0:K_MAX, s, h, qb * P:(qb + 1) * P],
                                                        kT[0:K_MAX, s, h, k0:k0 + keys],
                                                        start=i == 0, stop=cls == 2, skip_group_check=True)
                                if cls < 2:
                                    last = nc.tensor.matmul(cols[:, keys - P:keys], t["ident_b"][:], t["mask_max"][:],
                                                            start=False, stop=True, skip_group_check=True)
                            last.then_inc(ring_made, 1)
                        if step[0] == "T":
                            pe.wait_ge(top_low, G + 1)
                            pe.wait_ge(ring_free, made + 1)
                            nc.tensor.transpose(ring[:, bank, 0:P // 2].bitcast(BF16)[0:PARTS * GH * 8, :],
                                                topp[:, s].rearrange("p a h q -> p (a h q)"), t["ident_b"][:])\
                                .then_inc(ring_made, 1)
                        if step[0] == "E":
                            _, _, n, h = step
                            kb, qc = BLOCKS[n]
                            e = GH * (n_blocks * G + n) + h
                            slot = (GH * (n_blocks * g + n) + h) % DEPTH
                            if n == 0 and h == 0:
                                pe.wait_ge(toprows[s], FREE + 16 * PARTS * (it + more + 1))
                            pe.wait_ge(scores_free, e + 1)
                            q0, q1 = max(kb * P, qc * C), (qc + 1) * C
                            last = nc.tensor.matmul(scores[:, slot, 0:q1 - q0],
                                                    kT[0:K_EXP, s, h, kb * P:(kb + 1) * P],
                                                    qT[0:K_EXP, s, h, q0:q1],
                                                    start=True, stop=True)
                            last.then_inc(scores_made, 1)
                        if step[0] == "V":
                            n = step[2]
                            kb, qc = BLOCKS[n]
                            v = n_blocks * G + n
                            if n in DIAGONAL:
                                pe.wait_ge(causal, TB * G + DIAGONAL.index(n) + 1)
                            else:
                                pe.wait_ge(scores_free, DEPTH + GH * (v + 1))
                            if kb == 0:
                                pe.wait_ge(heads_left, 2 * G + qc + 1)
                            q0, q1 = max(kb * P, qc * C), (qc + 1) * C
                            for h in range(GH):
                                last = nc.tensor.matmul(accs[h * VW:(h + 1) * VW, qc, q0 - qc * C:C],
                                                        val[:, s, kb, h * VW:(h + 1) * VW],
                                                        prob[:, n % PROBS, h, 0:q1 - q0],
                                                        start=kb == 0, stop=kb == 4 * qc + 3,
                                                        skip_group_check=True)
                            last.then_inc(prob_used, 1)

                loop(pe, run)

            @block.scalar
            def _(act):
                act.sem_inc(scores_free, DEPTH)
                act.sem_inc(heads_left, 2)

                def run(steps, it, _):
                    for step in steps:
                        G = NG * it + step[1]
                        if step[0] == "E":
                            _, _, n, h = step
                            kb, qc = BLOCKS[n]
                            e = GH * (n_blocks * G + n) + h
                            slot = (GH * (n_blocks * step[1] + n) + h) % DEPTH
                            width = (qc + 1) * C - max(kb * P, qc * C)
                            act.wait_ge(scores_made, e + 1)
                            if h == 0:
                                act.wait_ge(prob_used, n_blocks * G + n + 1)
                            nc.scalar.activation(prob[:, n % PROBS, h, 0:width], scores[:, slot, 0:width], ACT.Exp)\
                                .then_inc(scores_free, 1)
                        if step[0] == "O":
                            qc = step[2]
                            act.wait_ge(prob_used, PROBS + n_blocks * G + BLOCKS.index((4 * qc + 3, qc)) + 1)
                            act.wait_ge(stored[qc], FREE + 16 * G)
                            nc.scalar.copy(heads[:, qc, :], accs[:, qc, :]).then_inc(heads_left, 1)

                loop(act, run)

            @block.vector
            def _(dve):
                dve.sem_inc(ring_free, DEPTH)

                def run(steps, it, first):
                    r = 0
                    for step in steps:
                        g = step[1]
                        s, more = where(g)
                        G = NG * it + g
                        if step[0] in "MT":
                            bank = (first + r) % DEPTH
                            made = first + r + it * banks(BODY)
                            r += 1
                            dve.wait_ge(ring_made, made + 1)
                        if step[0] == "M":
                            cls, hs, qb, _, keys = MAX_UNITS[step[2]]
                            nc.vector.reduce_max(
                                tops[:, s, cls, qb % 4, hs[0]:hs[-1] + 1],
                                ring[:, bank, 0:len(hs) * keys].rearrange("p (h k) -> p h k", k=keys),
                                axis=AX_X).then_inc(ring_free, 1)
                        if step[0] == "F":
                            dve.wait_ge(ring_free, DEPTH + first + r + it * banks(BODY))
                            nc.vector.tensor_tensor(tops[:, s, 1], tops[:, s, 1], tops[:, s, 2], ALU.max)\
                                .then_inc(top_merged, 1)
                            top = tops[:, s, 0:2].rearrange("p c q h -> p (c q) h")
                            left = rest[:, s].rearrange("p (q h) -> p q h", h=GH)

                            def part(i):
                                return topp[:, s, i].rearrange("p h q -> p q h")

                            dve.wait_ge(top_merged, G + 1)
                            nc.vector.tensor_scalar(part(0), top, OFFSET, -1.0, ALU.add, ALU.mult)\
                                .then_inc(top_high, 1)
                            dve.wait_ge(top_high, G + 1)
                            nc.vector.scalar_tensor_tensor(left, top, OFFSET, part(0), ALU.add, ALU.add)\
                                .then_inc(top_rest, 1)
                            dve.wait_ge(top_rest, G + 1)
                            nc.vector.tensor_scalar(part(1), left, -1.0, None, ALU.mult).then_inc(top_mid, 1)
                            dve.wait_ge(top_mid, G + 1)
                            nc.vector.scalar_tensor_tensor(part(2), left, -1.0, part(1), ALU.mult, ALU.subtract)\
                                .then_inc(top_low, 1)
                        if step[0] == "T":
                            dve.wait_ge(toprows[s], FREE + 16 * PARTS * (it + more))
                            nc.vector.tensor_copy(topT[:, s, :],
                                                  ring[:, bank, 0:P // 2].bitcast(BF16)[0:PARTS * GH * 8, :])\
                                .then_inc(ring_free, 1)

                loop(dve, run)

            @block.gpsimd
            def _(pool):
                def run(steps, it, _):
                    for step in steps:
                        if step[0] == "E" and step[2] in DIAGONAL and step[3] == GH - 1:
                            G, n = NG * it + step[1], step[2]
                            pool.wait_ge(scores_free, DEPTH + GH * (n_blocks * G + n + 1))
                            pool.sem_inc(exps_seen, 1)
                            own = prob[:, n % PROBS, :, 0:P]
                            nc.gpsimd.affine_select(out=own, in_=own, compare_op=ALU.is_ge, fill=0.0, base=0,
                                                    pattern=[[0, GH], [1, P]], channel_multiplier=-1)\
                                .then_inc(causal, 1)

                loop(pool, run)


def project_out(nc, sem, layer, t):
    x, y = t["x"], t["norm"]
    stats, moments, rstd, shift, big = t["stats"], t["moments"], t["rstd"], t["shift"], t["big"]
    n = f"o{layer}_"
    arrived = [sem(n + f"arrived{u}") for u in range(2)]
    den_loaded = sem(n + "den_loaded")
    den_inverted = sem(n + "den_inverted")
    inv_stored = sem(n + "inv_stored")
    scaled = sem(n + "scaled")
    y_made = sem(n + "y_made")
    y_left = sem(n + "y_left")
    stats_done = sem(n + "stats_done")
    stats_seen = sem(n + "stats_seen")
    moments_done = sem(n + "moments_done")
    std_done = sem(n + "std_done")
    rstd_done = sem(n + "rstd_done")
    shift_done = sem(n + "shift_done")
    y_done = sem(n + "y_done")
    x_done = sem(n + "x_done")
    with (nc.sbuf_tensor(n + "heads_in", [P, 2, DC, C], F32) as heads_in,
          nc.sbuf_tensor(n + "inverse", [P, 2, DC, C], F32) as inverse,
          nc.sbuf_tensor(n + "denominators", [P, C], F32) as den, nc.Block() as block):
        rows = t["o_dram"].rearrange("b g (j r) t -> (b g j) r t", r=VW)
        halves = t["i_dram"].rearrange("h (u t) -> (h u) t", u=2)

        @block.sync
        def _(sp):
            sp.dma_start(den[:], rows[:, HD, :].rearrange("h (u t) -> h u t", u=2)).then_inc(den_loaded, 16)
            sp.wait_ge(den_inverted, 1)
            sp.dma_start(halves, den[:]).then_inc(inv_stored, 16)
            sp.wait_ge(inv_stored, 16)
            with sp.Fori(0, B) as b:
                for u in range(2):
                    sp.wait_ge(y_made, FREE + 4 * b)
                    for c in range(DC):
                        heads = bass.ds(NH * b + c * NH // 2, NH // 2)
                        sp.dma_start(heads_in[:, u, c], rows[heads, 0:HD, u * C:(u + 1) * C])\
                            .then_inc(arrived[u], 16)
                        src = t["i_dram"][heads, u * C:(u + 1) * C].rearrange("h (o t) -> h o t", o=1)
                        sp.dma_start(inverse[:, u, c], src.to_broadcast([NH // 2, HD, C])).then_inc(arrived[u], 16)

        @block.gpsimd
        def _(pool):
            with pool.Fori(0, B) as b:
                for u in range(2):
                    pool.wait_ge(arrived[u], 16 * 2 * DC * (b + 1))
                    nc.gpsimd.tensor_tensor(heads_in[:, u], heads_in[:, u], inverse[:, u], ALU.mult)\
                        .then_inc(scaled, 1)

        @block.tensor
        def _(pe):
            pe.sem_inc(y_made, FREE)
            with pe.Fori(0, B) as b:
                for u in range(2):
                    pe.wait_ge(scaled, 2 * b + u + 1)
                    pe.wait_ge(y_left, FREE + 4 * b)
                    for s in range(4):
                        for c in range(DC):
                            last = nc.tensor.matmul(big[:, u, s * D:(s + 1) * D],
                                                    heads_in[:, u, c, s * P:(s + 1) * P], t["w_out"][:, layer, c, :],
                                                    start=c == 0, stop=c == DC - 1)
                        if s % 2:
                            last.then_inc(y_made, 1)

        @block.vector
        def _(dve):
            dve.sem_inc(y_left, FREE)
            dve.sem_inc(x_done, FREE)
            dve.wait_ge(den_loaded, 16)
            nc.vector.reciprocal(den[:], den[:]).then_inc(den_inverted, 1)
            with dve.Fori(0, B) as b:
                for u in range(2):
                    k = 2 * b + u
                    for half in range(2):
                        dve.wait_ge(y_made, FREE + 2 * k + half + 1)
                        if half == 0:
                            dve.wait_ge(x_done, FREE + 8 * b)
                        nc.vector.tensor_tensor(
                            y[:, u, 2 * half:2 * half + 2, :],
                            big[:, u, half * C:(half + 1) * C].rearrange("p (s d) -> p s d", d=D),
                            t["b_out"][:, layer:layer + 1, :].to_broadcast([P, 2, D]), ALU.add).then_inc(y_left, 1)
                    dve.wait_ge(y_left, FREE + 2 * k + 2)
                    for s in range(4):
                        nc.vector.bn_stats(stats[:, u, s, :], y[:, u, s, :]).then_inc(stats_done, 1)
                    dve.wait_ge(stats_done, 4 * k + 4)
                    dve.sem_inc(stats_seen, 1)
                    for s in range(4):
                        nc.vector.bn_aggr(moments[:, u, s, :], stats[:, u, s, :]).then_inc(moments_done, 1)
                for u in range(2):
                    k = 2 * b + u
                    dve.wait_ge(std_done, k + 1)
                    nc.vector.reciprocal(rstd[:, u, :], rstd[:, u, :]).then_inc(rstd_done, 1)
                    dve.wait_ge(rstd_done, k + 1)
                    nc.vector.scalar_tensor_tensor(shift[:, u, :], moments[:, u, :, 0], -1.0, rstd[:, u, :],
                                                   ALU.mult, ALU.mult).then_inc(shift_done, 1)
                for u in range(2):
                    k = 2 * b + u
                    for s in range(4):
                        dve.wait_ge(y_done, 4 * k + s + 1)
                        here = x[:, bass.ds(8 * b + 4 * u + s, 1), :]
                        nc.vector.tensor_tensor(here, here, y[:, u, s:s + 1, :], ALU.add).then_inc(x_done, 1)

        @block.scalar
        def _(act):
            with act.Fori(0, B) as b:
                for u in range(2):
                    act.wait_ge(moments_done, 4 * (2 * b + u) + 4)
                    nc.scalar.activation(rstd[:, u, :], moments[:, u, :, 1], ACT.Sqrt, bias=t["eps"][:, 0:1])\
                        .then_inc(std_done, 1)
                for u in range(2):
                    k = 2 * b + u
                    act.wait_ge(shift_done, k + 1)
                    for s in range(4):
                        nc.scalar.activation(y[:, u, s, :], y[:, u, s, :], ACT.Identity,
                                             bias=shift[:, u, s:s + 1], scale=rstd[:, u, s:s + 1])\
                            .then_inc(y_done, 1)


def experts(nc, sem, io, t):
    x, norm, normT, big, ring, accs = t["x"], t["norm"], t["normT"], t["big"], t["ring"], t["accs"]
    stats, moments, rstd, shift = t["stats"], t["moments"], t["rstd"], t["shift"]
    nt = MT_TILES
    with ExitStack() as ctx:
        def sb(name, shape, dt=F32):
            return ctx.enter_context(nc.sbuf_tensor("e_" + name, shape, dt))

        w_in = sb("w_in", [P, 2, DC, 2 * FI])
        w_down = sb("w_down", [FC, 2, 2, D])
        idx = sb("idx", [P, nt, TOPK], I32)
        idx_f = sb("idx_f", [P, nt, TOPK])
        chosen_w = sb("chosen_w", [P, nt, TOPK])
        expert_no = sb("expert_no", [P, NE])
        share = sb("share", [P, nt, TOPK, NE])
        zero = sb("zero", [P, P])
        gated = sb("gated", [P, 2, nt, FI])
        act_in = sb("act_in", [P, 2, nt, FI])
        act_inT = sb("act_inT", [FC, 2, 2, nt * P])
        y = sb("y", [P, nt, D])

        routing = sem("e_routing")
        w_arrived = [sem(f"e_w_arrived{i}") for i in range(2)]
        chain = sem("e_chain")
        moments_done = sem("e_moments_done")
        std_done = sem("e_std_done")
        share_done = sem("e_share_done")
        norm_done = sem("e_norm_done")
        transposed = sem("e_transposed")
        normT_done = sem("e_normT_done")
        in_made = sem("e_in_made")
        gate_done = sem("e_gate_done")
        act_done = sem("e_act_done")
        act_transposed = sem("e_act_transposed")
        actT_done = sem("e_actT_done")
        down_done = sem("e_down_done")
        y_done = sem("e_y_done")
        x_done = sem("e_x_done")

        with nc.Block() as block:
            @block.sync
            def _(sp):
                sp.dma_start(idx[:], io["topk_idx"].rearrange("(n p) k -> p n k", p=P)).then_inc(routing, 16)
                sp.dma_start(chosen_w[:], io["topk_weight"].rearrange("(n p) k -> p n k", p=P)).then_inc(routing, 16)
                sp.dma_start(expert_no[:], io["expert_no"]).then_inc(routing, 16)
                with sp.Fori(0, NE // 2) as i:
                    for e in range(2):
                        sp.wait_ge(down_done, FREE + 2 * i)
                        sp.dma_start(w_in[:, e], io["w_in"][bass.ds(2 * i + e, 1)].rearrange("e p c f -> (e p) c f"))\
                            .then_inc(w_arrived[e], 16)
                        sp.dma_start(w_down[:, e],
                                     io["w_down"][bass.ds(2 * i + e, 1)].rearrange("e p c f -> (e p) c f"))\
                            .then_inc(w_arrived[e], 16)

            @block.vector
            def _(dve):
                dve.sem_inc(act_done, FREE)
                dve.sem_inc(actT_done, FREE)
                steps = [0]

                def link(ins):
                    steps[0] += 1
                    ins.then_inc(chain, 1)
                    dve.wait_ge(chain, steps[0])

                for s in range(nt):
                    link(nc.vector.bn_stats(stats[:, 0, s, :], x[:, s, :]))
                    link(nc.vector.bn_aggr(moments[:, 0, s, :], stats[:, 0, s, :]))
                dve.sem_inc(moments_done, 1)
                dve.wait_ge(std_done, 1)
                link(nc.vector.reciprocal(rstd[:, 0, 0:nt], rstd[:, 0, 0:nt]))
                for s in range(nt):
                    nc.vector.tensor_scalar(norm[:, 0, s, :], x[:, s, :], moments[:, 0, s, 0:1], rstd[:, 0, s:s + 1],
                                            ALU.subtract, ALU.mult).then_inc(norm_done, 1)
                link(nc.vector.memset(zero[:], 0.0))
                dve.wait_ge(routing, 48)
                link(nc.vector.tensor_copy(idx_f[:], idx[:]))
                for s in range(nt):
                    for k in range(TOPK):
                        link(nc.vector.tensor_scalar(share[:, s, k, :], expert_no[:], idx_f[:, s, k:k + 1],
                                                     chosen_w[:, s, k:k + 1], ALU.is_equal, ALU.mult))
                for s in range(nt):
                    for k in range(1, TOPK):
                        link(nc.vector.tensor_tensor(share[:, s, 0, :], share[:, s, 0, :], share[:, s, k, :],
                                                     ALU.add))
                dve.sem_inc(share_done, 1)
                dve.wait_ge(transposed, 1)
                nc.vector.tensor_copy(normT[:, 0, 0:DC * nt * P], big[:, 0, 0:DC * nt * P]).then_inc(normT_done, 1)
                with dve.Fori(0, NE // 2) as i:
                    for e in range(2):
                        dve.wait_ge(gate_done, nt * (2 * i + e) + nt)
                        dve.wait_ge(act_transposed, FREE + 2 * i)
                        for s in range(nt):
                            nc.vector.scalar_tensor_tensor(
                                act_in[:, e, s, :], gated[:, e, s, :], share[:, s, 0, bass.ds(2 * i + e, 1)],
                                big[:, e, s * C + FI:s * C + 2 * FI], ALU.mult, ALU.mult).then_inc(act_done, 1)
                    for e in range(2):
                        dve.wait_ge(act_transposed, FREE + 2 * i + e + 1)
                        dve.wait_ge(down_done, FREE + 2 * i)
                        nc.vector.tensor_copy(act_inT[:, e].rearrange("p c t -> p (c t)"),
                                              ring[0:FC, e, :]).then_inc(actT_done, 1)
                dve.wait_ge(down_done, FREE + NE)
                link(nc.vector.tensor_copy(y[:].rearrange("p s d -> p (s d)"), accs[:, 0, :]))
                for s in range(nt):
                    link(nc.vector.bn_stats(stats[:, 0, s, :], y[:, s, :]))
                    link(nc.vector.bn_aggr(moments[:, 0, s, :], stats[:, 0, s, :]))
                dve.sem_inc(moments_done, 1)
                dve.wait_ge(std_done, 2)
                link(nc.vector.reciprocal(rstd[:, 0, 0:nt], rstd[:, 0, 0:nt]))
                for s in range(nt):
                    link(nc.vector.tensor_scalar(y[:, s, :], y[:, s, :], moments[:, 0, s, 0:1], rstd[:, 0, s:s + 1],
                                                 ALU.subtract, ALU.mult))
                    link(nc.vector.tensor_tensor(x[:, s, :], x[:, s, :], y[:, s, :], ALU.add))

            @block.scalar
            def _(act):
                def root(n):
                    act.wait_ge(moments_done, n)
                    nc.scalar.activation(rstd[:, 0, 0:nt], moments[:, 0, 0:nt, 1], ACT.Sqrt, bias=t["eps"][:, 0:1])\
                        .then_inc(std_done, 1)

                root(1)
                with act.Fori(0, NE // 2) as i:
                    for e in range(2):
                        for s in range(nt):
                            act.wait_ge(in_made, nt * (2 * i + e) + s + 1)
                            act.wait_ge(act_done, FREE + nt * 2 * i)
                            nc.scalar.activation(gated[:, e, s, :], big[:, e, s * C:s * C + FI], ACT.Silu)\
                                .then_inc(gate_done, 1)
                root(2)

            @block.tensor
            def _(pe):
                pe.sem_inc(down_done, FREE)
                pe.sem_inc(act_transposed, FREE)
                pe.wait_ge(norm_done, nt)
                for s in range(nt):
                    for c in range(DC):
                        last = nc.tensor.transpose(big[:, 0, (c * nt + s) * P:(c * nt + s + 1) * P],
                                                   norm[:, 0, s, c * P:(c + 1) * P], t["ident"][:])
                last.then_inc(transposed, 1)
                pe.wait_ge(normT_done, 1)
                pe.wait_ge(share_done, 1)
                nc.tensor.matmul(accs[:, 0, :], zero[:], normT[:, 0, 0:C], start=True, stop=True,
                                 skip_group_check=True)
                with pe.Fori(0, NE // 2) as i:
                    for e in range(2):
                        pe.wait_ge(w_arrived[e], 32 * (i + 1))
                        pe.wait_ge(act_done, FREE + nt * 2 * i)
                        for s in range(nt):
                            for c in range(DC):
                                last = nc.tensor.matmul(big[:, e, s * C:s * C + 2 * FI],
                                                        normT[:, 0, (c * nt + s) * P:(c * nt + s + 1) * P],
                                                        w_in[:, e, c, :], start=c == 0, stop=c == DC - 1)
                            last.then_inc(in_made, 1)
                    for e in range(2):
                        pe.wait_ge(act_done, FREE + nt * (2 * i + e) + nt)
                        pe.wait_ge(actT_done, FREE + 2 * i)
                        for c in range(2):
                            for s in range(nt):
                                last = nc.tensor.transpose(ring[0:FC, e, (c * nt + s) * P:(c * nt + s + 1) * P],
                                                           act_in[:, e, s, c * FC:(c + 1) * FC], t["ident"][:])
                        last.then_inc(act_transposed, 1)
                    for e in range(2):
                        pe.wait_ge(actT_done, FREE + 2 * i + e + 1)
                        for s in range(nt):
                            for c in range(2):
                                last = nc.tensor.matmul(accs[:, 0, s * D:(s + 1) * D],
                                                        act_inT[:, e, c, s * P:(s + 1) * P], w_down[:, e, c, :],
                                                        start=False, stop=True, skip_group_check=True)
                        last.then_inc(down_done, 1)


def linear(nc, sem, io, out, t):
    x, norm, normT, big, ring = t["x"], t["norm"], t["normT"], t["big"], t["ring"]
    stats, moments, rstd, shift = t["stats"], t["moments"], t["rstd"], t["shift"]
    with ExitStack() as ctx:
        def sb(name, shape, dt=F32):
            return ctx.enter_context(nc.sbuf_tensor("l_" + name, shape, dt))

        w = sb("w", [P, DC, D])
        size = sb("size", [P, DC, D])
        alpha = sb("alpha", [P, DC])
        binary = sb("binary", [P, DC, D])
        binaryT = sb("binaryT", [P, DC, D])
        bias = sb("bias", [P, 1, D])
        y = sb("y", [P, 2, 4, D])
        statsy = sb("statsy", [P, 2, 4, 6])
        momentsy = sb("momentsy", [P, 2, 4, 2])
        rstdy = sb("rstdy", [P, 2, 4])

        loaded = sem("l_loaded")
        sizes = sem("l_sizes")
        chain = sem("l_chain")
        binary_done = sem("l_binary_done")
        binary_transposed = sem("l_binary_transposed")
        binaryT_done = sem("l_binaryT_done")
        stats_done = sem("l_stats_done")
        stats_seen = sem("l_stats_seen")
        moments_done = sem("l_moments_done")
        std_done = sem("l_std_done")
        rstd_done = sem("l_rstd_done")
        norm_done = sem("l_norm_done")
        transposed = sem("l_transposed")
        normT_done = sem("l_normT_done")
        y_made = sem("l_y_made")
        y_left = sem("l_y_left")
        statsy_done = sem("l_statsy_done")
        statsy_seen = sem("l_statsy_seen")
        momentsy_done = sem("l_momentsy_done")
        stdy_done = sem("l_stdy_done")
        rstdy_done = sem("l_rstdy_done")
        shift_done = sem("l_shift_done")
        y_done = sem("l_y_done")
        x_done = sem("l_x_done")
        written = sem("l_written")

        with nc.Block() as block:
            @block.sync
            def _(sp):
                sp.dma_start(w[:], io["w_ffn"].rearrange("(c p) i -> p c i", p=P)).then_inc(loaded, 16)
                sp.dma_start(bias[:, 0, :], io["b_ffn"]).then_inc(loaded, 16)
                with sp.Fori(0, B) as b:
                    for u in range(2):
                        sp.wait_ge(x_done, FREE + 8 * b + 4 * u + 4)
                        dst = out[bass.ds(b, 1), u * C:(u + 1) * C, :]
                        sp.dma_start(dst.rearrange("b (s p) d -> p (b s) d", p=P),
                                     x[:, bass.ds(8 * b + 4 * u, 4), :]).then_inc(written, 16)
                sp.wait_ge(written, 16 * 2 * B)

            @block.scalar
            def _(act):
                act.wait_ge(loaded, 32)
                for c in range(DC):
                    nc.scalar.activation(size[:, c, :], w[:, c, :], ACT.Abs, accum_out=alpha[:, c:c + 1])\
                        .then_inc(sizes, 1)
                with act.Fori(0, B) as b:
                    for u in range(2):
                        act.wait_ge(moments_done, 4 * (2 * b + u) + 4)
                        nc.scalar.activation(rstd[:, u, :], moments[:, u, :, 1], ACT.Sqrt, bias=t["eps"][:, 0:1])\
                            .then_inc(std_done, 1)
                    for u in range(2):
                        act.wait_ge(transposed, FREE + 2 * b + u + 1)
                        act.wait_ge(y_made, FREE + 4 * b)
                        nc.scalar.copy(normT[:, u, :], big[:, u, :]).then_inc(normT_done, 1)
                    for u in range(2):
                        act.wait_ge(momentsy_done, 4 * (2 * b + u) + 4)
                        nc.scalar.activation(rstdy[:, u, :], momentsy[:, u, :, 1], ACT.Sqrt, bias=t["eps"][:, 0:1])\
                            .then_inc(stdy_done, 1)
                    for u in range(2):
                        k = 2 * b + u
                        act.wait_ge(shift_done, k + 1)
                        for s in range(4):
                            nc.scalar.activation(y[:, u, s, :], y[:, u, s, :], ACT.Identity,
                                                 bias=shift[:, u, s:s + 1], scale=rstdy[:, u, s:s + 1])\
                                .then_inc(y_done, 1)

            @block.vector
            def _(dve):
                dve.sem_inc(norm_done, FREE)
                dve.sem_inc(y_left, FREE)
                dve.sem_inc(x_done, FREE)
                steps = [0]

                def link(ins):
                    steps[0] += 1
                    ins.then_inc(chain, 1)
                    dve.wait_ge(chain, steps[0])

                dve.wait_ge(sizes, DC)
                link(nc.vector.tensor_scalar(alpha[:], alpha[:], 1.0 / D, None, ALU.mult))
                for c in range(DC):
                    link(nc.vector.tensor_scalar(binary[:, c, :], w[:, c, :], 0.0, 2.0, ALU.is_ge, ALU.mult))
                    link(nc.vector.tensor_scalar(binary[:, c, :], binary[:, c, :], -1.0, alpha[:, c:c + 1],
                                                 ALU.add, ALU.mult))
                    link(nc.vector.tensor_tensor(binary[:, c, :], binary[:, c, :], w[:, c, :], ALU.subtract))
                    link(nc.vector.tensor_tensor(binary[:, c, :], binary[:, c, :], w[:, c, :], ALU.add))
                dve.sem_inc(binary_done, 1)
                dve.wait_ge(binary_transposed, 1)
                nc.vector.tensor_copy(binaryT[:].rearrange("p c o -> p (c o)"), ring[:, 0, :]).then_inc(binaryT_done, 1)
                with dve.Fori(0, B) as b:
                    for u in range(2):
                        k = 2 * b + u
                        dve.wait_ge(norm_done, FREE + 8 * b)
                        for s in range(4):
                            nc.vector.bn_stats(stats[:, u, s, :], x[:, bass.ds(8 * b + 4 * u + s, 1), :])\
                                .then_inc(stats_done, 1)
                        dve.wait_ge(stats_done, 4 * k + 4)
                        dve.sem_inc(stats_seen, 1)
                        for s in range(4):
                            nc.vector.bn_aggr(moments[:, u, s, :], stats[:, u, s, :]).then_inc(moments_done, 1)
                    for u in range(2):
                        k = 2 * b + u
                        dve.wait_ge(std_done, k + 1)
                        nc.vector.reciprocal(rstd[:, u, :], rstd[:, u, :]).then_inc(rstd_done, 1)
                        dve.wait_ge(rstd_done, k + 1)
                        dve.wait_ge(transposed, FREE + 2 * b)
                        for s in range(4):
                            nc.vector.tensor_scalar(norm[:, u, s:s + 1, :], x[:, bass.ds(8 * b + 4 * u + s, 1), :],
                                                    moments[:, u, s, 0:1], rstd[:, u, s:s + 1],
                                                    ALU.subtract, ALU.mult).then_inc(norm_done, 1)
                    for u in range(2):
                        k = 2 * b + u
                        for half in range(2):
                            dve.wait_ge(y_made, FREE + 2 * k + half + 1)
                            if half == 0:
                                dve.wait_ge(x_done, FREE + 8 * b)
                            nc.vector.tensor_tensor(
                                y[:, u, 2 * half:2 * half + 2, :],
                                big[:, u, half * C:(half + 1) * C].rearrange("p (s d) -> p s d", d=D),
                                bias[:].to_broadcast([P, 2, D]), ALU.add).then_inc(y_left, 1)
                        dve.wait_ge(y_left, FREE + 2 * k + 2)
                        for s in range(4):
                            nc.vector.bn_stats(statsy[:, u, s, :], y[:, u, s, :]).then_inc(statsy_done, 1)
                        dve.wait_ge(statsy_done, 4 * k + 4)
                        dve.sem_inc(statsy_seen, 1)
                        for s in range(4):
                            nc.vector.bn_aggr(momentsy[:, u, s, :], statsy[:, u, s, :]).then_inc(momentsy_done, 1)
                    for u in range(2):
                        k = 2 * b + u
                        dve.wait_ge(stdy_done, k + 1)
                        nc.vector.reciprocal(rstdy[:, u, :], rstdy[:, u, :]).then_inc(rstdy_done, 1)
                        dve.wait_ge(rstdy_done, k + 1)
                        nc.vector.scalar_tensor_tensor(shift[:, u, :], momentsy[:, u, :, 0], -1.0, rstdy[:, u, :],
                                                       ALU.mult, ALU.mult).then_inc(shift_done, 1)
                    for u in range(2):
                        k = 2 * b + u
                        for s in range(4):
                            dve.wait_ge(y_done, 4 * k + s + 1)
                            here = x[:, bass.ds(8 * b + 4 * u + s, 1), :]
                            nc.vector.tensor_tensor(here, here, y[:, u, s:s + 1, :], ALU.add).then_inc(x_done, 1)

            @block.tensor
            def _(pe):
                pe.sem_inc(transposed, FREE)
                pe.sem_inc(y_made, FREE)
                pe.wait_ge(binary_done, 1)
                for co in range(DC):
                    for ci in range(DC):
                        last = nc.tensor.transpose(ring[:, 0, ci * D + co * P:ci * D + (co + 1) * P],
                                                   binary[:, co, ci * P:(ci + 1) * P], t["ident"][:])
                last.then_inc(binary_transposed, 1)
                pe.wait_ge(binaryT_done, 1)
                with pe.Fori(0, B) as b:
                    for u in range(2):
                        k = 2 * b + u
                        pe.wait_ge(norm_done, FREE + 4 * k + 4)
                        pe.wait_ge(y_left, FREE + 4 * b)
                        for s in range(4):
                            for c in range(DC):
                                last = nc.tensor.transpose(big[:, u, c * C + s * P:c * C + (s + 1) * P],
                                                           norm[:, u, s, c * P:(c + 1) * P], t["ident"][:])
                        last.then_inc(transposed, 1)
                    for u in range(2):
                        k = 2 * b + u
                        pe.wait_ge(normT_done, k + 1)
                        for s in range(4):
                            for c in range(DC):
                                last = nc.tensor.matmul(big[:, u, s * D:(s + 1) * D],
                                                        normT[:, u, c * C + s * P:c * C + (s + 1) * P],
                                                        binaryT[:, c, :], start=c == 0, stop=c == DC - 1)
                            if s % 2:
                                last.then_inc(y_made, 1)



def three_parts(a):
    bf16 = mybir.dt.np(BF16)
    high = a.astype(bf16)
    rest = a - high.astype(np.float32)
    mid = rest.astype(bf16)
    low = (rest - mid.astype(np.float32)).astype(bf16)
    return [p.astype(np.float32) for p in (high, mid, low)]


def constants():
    bf16 = mybir.dt.np(BF16)
    i = np.arange(P)
    pos = np.arange(S)
    near, far = (pos % P).astype(np.float32), (pos // P * P).astype(np.float32)
    start = 2.0 ** (-2.0 ** (-(np.log2(NH) - 3)))
    slopes = np.array([start * start ** n for n in range(NH)]).astype(np.float32).reshape(NG, GH)
    pos_q = np.zeros((2, NG, POS_ROWS, GH, S), np.float32)
    pos_k = np.zeros((2, NG, POS_ROWS + MAX_ROWS, GH, S), np.float32)
    pos_k[:, :, POS_ROWS:] = 1.0
    for n, part in enumerate(three_parts(slopes)):
        for m, place in enumerate((far, near)):
            row = 4 * n + 2 * m
            pos_q[1, :, row] = part[:, :, None]
            pos_k[1, :, row] = place
            pos_q[1, :, row + 1] = -place
            pos_k[1, :, row + 1] = part[:, :, None]
    return {
        "ident": np.eye(P, dtype=np.float32),
        "ident_b": np.eye(P, dtype=bf16),
        "mask_max": np.where(i[None, :] > i[:, None], MASKED, 0.0).astype(bf16),
        "pos_q": pos_q.astype(bf16),
        "pos_k": pos_k.astype(bf16),
        "expert_no": np.broadcast_to(np.arange(NE, dtype=np.float32), (P, NE)),
    }


def layouts(a):
    order = np.arange(2 * D).reshape(4, 2, GH, HD).transpose(0, 1, 3, 2).reshape(-1)
    order = np.concatenate([order, np.arange(2 * D, 3 * D)])
    w_qkv = np.stack([a["L0_attn_w_qkv"].T, a["L1_attn_w_qkv"]])[:, :, order]
    b_qkv = np.stack([a["L0_attn_b_qkv"], a["L1_attn_b_qkv"]])
    w_out = np.stack([a["L0_attn_w_out"].T, a["L1_attn_w_proj"]])
    rows = (P, 2, D)
    w_in = np.concatenate([a["L0_ffn_gate_weight"], a["L0_ffn_up_weight"]], axis=1)
    return {
        "x": a["L0_attn_x"].reshape(B * S, D),
        "w_qkv": w_qkv.reshape(2, DC, P, 3 * D).transpose(2, 0, 1, 3),
        "b_qk": b_qkv[:, order[:2 * D]].reshape(2, 4, P).transpose(2, 0, 1),
        "b_v": np.broadcast_to(b_qkv[:, 2 * D:], rows),
        "w_out": w_out.reshape(2, DC, P, D).transpose(2, 0, 1, 3),
        "b_out": np.broadcast_to(np.stack([a["L0_attn_b_out"], a["L1_attn_b_proj"]]), rows),
        "w_in": w_in.transpose(0, 2, 1).reshape(NE, DC, P, 2 * FI).transpose(0, 2, 1, 3),
        "w_down": a["L0_ffn_down_weight"].transpose(0, 2, 1).reshape(NE, 2, FC, D).transpose(0, 2, 1, 3),
        "topk_idx": a["L0_ffn_topk_idx"].reshape(MT_TILES * P, TOPK),
        "topk_weight": a["L0_ffn_topk_weight"].reshape(MT_TILES * P, TOPK),
        "w_ffn": a["L1_ffn_weight"],
        "b_ffn": np.broadcast_to(a["L1_ffn_bias"], (P, D)),
    }


def kernel(**inputs):
    import concourse.bacc as bacc
    from concourse.bass_utils import run_bass_kernel_spmd

    nc = bacc.Bacc("TRN2", target_bir_lowering=False, num_devices=1)
    a = {name: np.asarray(v) for name, v in inputs.items()}
    arrays = {name: np.ascontiguousarray(v) for name, v in {**layouts(a), **constants()}.items()}
    io = {name: nc.dram_tensor(f"in_{name}", v.shape, mybir.dt.from_np(v.dtype), kind="ExternalInput").ap()
          for name, v in arrays.items()}
    out = nc.dram_tensor("out_x", (B, S, D), F32, kind="ExternalOutput").ap()
    sandwich(nc, io, out)
    result = run_bass_kernel_spmd(nc, [{f"in_{name}": v for name, v in arrays.items()}], core_ids=[0])
    return result.results[0]["out_x"]
```

```python
from contextlib import ExitStack

import numpy as np

import concourse.bass as bass
from concourse import mybir

F32 = mybir.dt.float32
BF16 = mybir.dt.bfloat16
I32 = mybir.dt.int32
ALU = mybir.AluOpType
ACT = mybir.ActivationFunctionType
AX_X = mybir.AxisListType.X

P = 128
B, S, D = 4, 1024, 256
NH, HD = 16, 16
DC = D // P
NT = B * S // P
TB = S // P
NG = 4
GH = NH // NG
VW = P // GH
C = 512
NE, FI, TOPK = 16, 176, 4
FC = FI // 2
MT_TILES = 2
EPS = 1e-5
MASKED = -1e30
OFFSET = 16.0

PARTS = 3
BIAS_ROWS = 32 * (PARTS - 1) + 1
QK_ROWS = 6 * HD
POS_ROWS = 12
MAX_ROWS = PARTS
K_MAX = QK_ROWS + POS_ROWS
K_EXP = K_MAX + MAX_ROWS
Q_RUNS = [(0, 0, 3), (3, 0, 2), (5, 0, 1)]
K_RUNS = [(0, 0), (1, 0), (2, 0), (3, 1), (4, 1), (5, 2)]
LOADS = len(Q_RUNS) + len(K_RUNS) + 2
SLOTS = 4
LEAD = 12
GROUPS = B * NG
DEPTH = 3
PROBS = 4
FREE = 16


def maximum_units():
    units, full = [], []
    for cls in (0, 1):
        for n in range(1, 5):
            per = 4 // n if n < 3 else 1
            for h in range(0, GH, per):
                units.append((cls, list(range(h, h + per)), 4 * cls + n - 1, cls * C, n * P))
    for qb in range(4, 8):
        for h in range(GH):
            full.append((2, [h], qb, 0, C))
    counts, turns = (len(units), len(full)), []
    while units or full:
        turns.append((units if len(units) * counts[1] >= len(full) * counts[0] else full).pop(0))
    return turns


MAX_UNITS = maximum_units()



BLOCKS = [(kb, qc) for kb in range(TB) for qc in range(kb * P // C, S // C)]
DIAGONAL = [BLOCKS.index((kb, kb * P // C)) for kb in range(TB)]
ORDER = ("EMEEMMEEMEMEMEVEMEMEEMEMEMEVMMEEMEVEMEEMEMEMEMEVEMEMVMEEMEME"
         "MEVMEMEMMEEVMMEEVEEVMEMEMEMEEVEEMEMMVMVM")


def attention_steps():
    ahead = []
    for g in range(GROUPS + 2):
        units = [("M", g, i) for i in range(len(MAX_UNITS))]
        ahead += units[:3] + [("T", g - 1)] + units[3:] + [("F", g)]
    per_group = len(MAX_UNITS) + 2
    assert ORDER.count("M") == per_group

    def real(steps):
        return [s for s in steps if 0 <= s[1] < GROUPS]

    at = per_group + LEAD
    before, groups = real(ahead[:at]), []
    for g in range(GROUPS):
        own = {"E": iter([("E", g, n, h) for n in range(len(BLOCKS)) for h in range(GH)]),
               "V": iter([("V", g, n) for n in range(len(BLOCKS))]),
               "M": iter(ahead[at:at + per_group])}
        at += per_group
        steps = []
        for kind in ORDER:
            steps.append(next(own[kind]))
            if kind == "V" and BLOCKS[steps[-1][2]] in ((3, 0), (7, 1)):
                steps.append(("O", g, BLOCKS[steps[-1][2]][1]))
        assert all(next(i, None) is None for i in own.values())
        groups.append(real(steps))
    return before, groups


def relative(groups, it):
    return [(s[0], s[1] - NG * it, *s[2:]) for group in groups[NG * it:NG * (it + 1)] for s in group]


BEFORE, STEPS = attention_steps()
BODY = relative(STEPS, 0)
LAST = relative(STEPS, B - 1)
assert BODY == relative(STEPS, 1) == relative(STEPS, B - 2)
for position, kind in ((2, "D"), (25, "R"), (40, "W"), (60, "H")):
    LAST.insert(LAST.index(("E", NG - 1, 0, 0)) + position, (kind, 0))


def banks(steps):
    return sum(s[0] in "MT" for s in steps)


def sandwich(nc, io, out):
    with ExitStack() as ctx:
        def sb(name, shape, dt=F32):
            return ctx.enter_context(nc.sbuf_tensor(name, shape, dt))

        in_use = []

        def sem(name):
            in_use.append(nc.alloc_semaphore(name))
            return in_use[-1]

        def stage_ends():
            nc.clear_and_free_semaphores(in_use)
            nc.all_engine_barrier()
            in_use.clear()

        q_dram = nc.dram_tensor("q_parts", [B, NG, PARTS, HD, GH, S], BF16).ap()
        k_dram = nc.dram_tensor("k_parts", [B, NG, PARTS, HD, GH, S], BF16).ap()
        v_dram = nc.dram_tensor("values", [B, NG, P, TB, P], F32).ap()
        o_dram = nc.dram_tensor("heads", [B, NG, P, S], F32).ap()
        i_dram = nc.dram_tensor("inverses", [B * NH, S], F32).ap()

        x = sb("x", [P, NT, D])
        w_qkv = sb("w_qkv", [P, 2, DC, 3 * D])
        b_qk = sb("b_qk", [P, 2, 4])
        b_v = sb("b_v", [P, 2, D])
        w_out = sb("w_out", [P, 2, DC, D])
        b_out = sb("b_out", [P, 2, D])
        ident = sb("ident", [P, P])
        ident_b = sb("ident_b", [P, P], BF16)
        binaryT = sb("binaryT", [P, DC, D])
        w_ffn = sb("w_ffn", [P, DC, D])
        b_ffn = sb("b_ffn", [P, 1, D])
        bias_rows = sb("bias_rows", [BIAS_ROWS, 3, D], BF16)
        ones_b = sb("ones_b", [BIAS_ROWS, P], BF16)
        mask_row = sb("mask_row", [P, C])
        eps = sb("eps", [P, 1])
        stats = sb("stats", [P, 2, 4, 6])
        moments = sb("moments", [P, 2, 4, 2])
        rstd = sb("rstd", [P, 2, 4])
        shift = sb("shift", [P, 2, 4])
        norm = sb("norm", [P, 2, 4, D])
        normT = sb("normT", [P, 2, DC * C])

        psum = ctx.enter_context(nc.psum_tensor("psum", [P, 8, C], F32))
        big = psum[:, 0:4, :].rearrange("p (u h) c -> p u (h c)", u=2)
        ring, accs = psum[:, 4:6, :], psum[:, 6:8, :]

        loaded, weights_loaded, rest_loaded, eps_set, rows_set = (sem(name) for name in (
            "loaded", "weights_loaded", "rest_loaded", "eps_set", "rows_set"))
        small = [(ident[:], io["ident"]), (b_qk[:], io["b_qk"])]
        later = [(w_qkv[:, 1], io["w_qkv"][:, 1]), (w_out[:], io["w_out"]), (b_out[:], io["b_out"]),
                 (w_ffn[:], io["w_ffn"].rearrange("(c p) i -> p c i", p=P)), (b_ffn[:, 0, :], io["b_ffn"]),
                 (ident_b[:], io["ident_b"]),
                 (mask_row[:], io["mask_row"])]
        x_first = [sem(f"x_first{k}") for k in range(2)]
        with nc.Block() as block:
            @block.sync
            def _(sp):
                def load_x(k):
                    sp.dma_start(x[:, 4 * k:4 * k + 4, :],
                                 io["x"][C * k:C * (k + 1), :].rearrange("(t p) d -> p t d", p=P))\
                        .then_inc(x_first[k], 16)

                load_x(0)
                for dst, src in small:
                    sp.dma_start(dst, src).then_inc(loaded, 16)
                load_x(1)
                sp.dma_start(w_qkv[:, 0], io["w_qkv"][:, 0]).then_inc(weights_loaded, 16)
                sp.dma_start(b_v[:], io["b_v"]).then_inc(weights_loaded, 16)
                for dst, src in later:
                    sp.dma_start(dst, src).then_inc(rest_loaded, 16)

            @block.vector
            def _(dve):
                nc.vector.memset(eps[:], EPS).then_inc(eps_set, 1)
                nc.vector.memset(bias_rows[:], 0.0).then_inc(rows_set, 1)
                nc.vector.memset(ones_b[:], 1.0).then_inc(rows_set, 1)
                dve.wait_ge(rows_set, 2)

        for layer in range(2):
            with (nc.sbuf_tensor(f"qT{layer}", [P, SLOTS, GH, S], BF16) as qT,
                  nc.sbuf_tensor(f"kT{layer}", [P, SLOTS, GH, S], BF16) as kT):
                head_slot = normT[:].rearrange("p n (c t) -> p n c t", t=C)
                head_arrived = nc.alloc_semaphore(f"o{layer}_head_arrived")
                operands = dict(
                    qT=qT, kT=kT, arrived=[nc.alloc_semaphore(f"a{layer}_arrived{s}") for s in range(SLOTS)],
                    q_dram=q_dram, k_dram=k_dram, v_dram=v_dram, pos_q=io["pos_q"], pos_k=io["pos_k"])
                project_qkv(nc, sem, layer, operands, dict(
                    x=x, w_qkv=w_qkv, b_qk=b_qk, b_v=b_v, ident=ident, eps=eps, stats=stats, moments=moments,
                    rstd=rstd, norm=norm, normT=normT, big=big, ring=ring, accs=accs,
                    q_dram=q_dram, k_dram=k_dram, v_dram=v_dram, x_dram=io["x"], loaded=loaded, loads=len(small),
                    x_first=x_first, weights_loaded=weights_loaded, rest_loaded=rest_loaded,
                    rest_loads=len(later), eps_set=eps_set))
                stage_ends()
                in_use.extend(operands["arrived"])
                attend(nc, sem, layer, dict(
                    ident_b=ident_b, mask_row=mask_row, eps=eps, bias_rows=bias_rows,
                    biases=(b_out[0:BIAS_ROWS, 0, :], b_out[0:BIAS_ROWS, 1, :], b_ffn[0:BIAS_ROWS, 0, :]),
                    head_slot=head_slot, head_arrived=head_arrived, psum=psum, o_dram=o_dram, i_dram=i_dram,
                    **operands))
                stage_ends()
            in_use.append(head_arrived)
            project_out(nc, sem, layer, dict(
                head_slot=head_slot, head_arrived=head_arrived,
                bias_rows=bias_rows, ones_b=ones_b, slots=psum[:].rearrange("p (k h) c -> p k (h c)", h=2),
                w_ffn=w_ffn, binaryT=binaryT, ident=ident, x=x, w_out=w_out, eps=eps, stats=stats,
                moments=moments, rstd=rstd, shift=shift, norm=norm, o_dram=o_dram, i_dram=i_dram))
            stage_ends()
            if layer == 0:
                experts(nc, sem, io, dict(
                    x=x, ident=ident, eps=eps, stats=stats, moments=moments, rstd=rstd, shift=shift, norm=norm, normT=normT,
                    big=big, ring=ring, accs=accs))
                stage_ends()
        linear(nc, sem, io, out, dict(
            x=x, ident=ident, eps=eps, stats=stats, moments=moments, rstd=rstd, shift=shift, norm=norm, normT=normT,
            big=big, binaryT=binaryT, bias_rows=bias_rows, ones_b=ones_b, turned=psum[:, 4:8, :].rearrange("p (u h) c -> p u (h c)", u=2)))


def project_qkv(nc, sem, layer, operands, t):
    x, norm, normT = t["x"], t["norm"], t["normT"]
    stats, moments, rstd = t["stats"], t["moments"], t["rstd"]
    big, ring, accs = t["big"], t["ring"], t["accs"]
    scale = (0.25, 0.0625)[layer]
    n = f"p{layer}_"
    stats_done = sem(n + "stats_done")
    stats_seen = sem(n + "stats_seen")
    moments_done = sem(n + "moments_done")
    std_done = sem(n + "std_done")
    rstd_done = sem(n + "rstd_done")
    norm_done = sem(n + "norm_done")
    transposed = sem(n + "transposed")
    normT_done = sem(n + "normT_done")
    qk_made = sem(n + "qk_made")
    qk_left = sem(n + "qk_left")
    rest_done = sem(n + "rest_done")
    mid_done = sem(n + "mid_done")
    low_done = sem(n + "low_done")
    v_made = sem(n + "v_made")
    v_left = sem(n + "v_left")
    stored = [sem(n + f"stored{u}") for u in range(2)]
    ones_set = sem(n + "ones_set")
    stores = 4 * 2 + NG
    if layer == 0:
        x_arrived = sem(n + "x_arrived")
        bias_scaled = sem(n + "bias_scaled")

    with (nc.sbuf_tensor(n + "qk32", [P, 4, C], F32) as qk32,
          nc.sbuf_tensor(n + "parts", [P, 2, 4, PARTS, C], BF16) as parts,
          nc.sbuf_tensor(n + "values", [P, 2, 4, NG, P], F32) as values,
          nc.Block() as block):
        @block.gpsimd
        def _(pool):
            def load_x(k):
                pool.dma_start(x[:, bass.ds(4 * k, 4), :],
                               t["x_dram"][bass.ds(C * k, C), :].rearrange("(t p) d -> p t d", p=P))\
                    .then_inc(x_arrived, 16)

            nc.gpsimd.memset(values[:], 1.0).then_inc(ones_set, 1)
            if layer == 0:
                load_x(2)
                with pool.Fori(3, 2 * B) as k:
                    pool.wait_ge(x_arrived, 16 * (k - 2))
                    load_x(k)

        @block.sync
        def _(sp):
            sp.sem_inc(stored[0], FREE)
            sp.sem_inc(stored[1], FREE)

            ahead = iter(q_k_loads(operands, layer, bass.ds(0, 1), 0))

            def load_ahead(count):
                for _ in range(count):
                    dst, src = next(ahead)
                    sp.dma_start(dst, src).then_inc(operands["arrived"][0], 16)

            def store(b, u, loads=(0, 0, 0, 0)):
                k = 2 * b + u
                for m in range(4):
                    sp.wait_ge(low_done, FREE + 4 * k + m + 1)
                    dram = (t["q_dram"], t["k_dram"])[m // 2]
                    for g in range(2):
                        dst = dram[bass.ds(b, 1), 2 * (m % 2) + g, :, :, :, u * C:(u + 1) * C]
                        sp.dma_start(dst.rearrange("b part r j t -> (b r j) part t"),
                                     parts[64 * g:64 * g + 64, u, m]).then_inc(stored[u], 16)
                    load_ahead(loads[m])
                sp.wait_ge(v_left, FREE + 4 * k + 4)
                for g in range(NG):
                    dst = t["v_dram"][bass.ds(b, 1), g, :, 4 * u:4 * u + 4, :]
                    sp.dma_start(dst.rearrange("b p s c -> (b p) s c"),
                                 values[:, u, :, g, :]).then_inc(stored[u], 16)

            with sp.Fori(0, B - 1) as b:
                for u in range(2):
                    store(b, u)
            store(B - 1, 0, (2, 2, 2, 2))
            store(B - 1, 1, (1, 1, 1, 0))
            assert next(ahead, None) is None
            for u in range(2):
                sp.wait_ge(stored[u], FREE + 16 * stores * B)
            if layer == 0:
                sp.wait_ge(t["rest_loaded"], 16 * t["rest_loads"])

        @block.vector
        def _(dve):
            dve.sem_inc(norm_done, FREE)
            dve.sem_inc(low_done, FREE)
            dve.sem_inc(v_left, FREE)

            def statistics(b, u, first=False):
                k = 2 * b + u
                if layer == 0:
                    if first:
                        dve.wait_ge(t["x_first"][u], 16)
                    else:
                        dve.wait_ge(x_arrived, 16 * (k - 1))
                dve.wait_ge(norm_done, FREE + 8 * b)
                for s in range(4):
                    nc.vector.bn_stats(stats[:, u, s, :], x[:, bass.ds(8 * b + 4 * u + s, 1), :])\
                        .then_inc(stats_done, 1)
                dve.wait_ge(stats_done, 4 * k + 4)
                dve.sem_inc(stats_seen, 1)
                for s in range(4):
                    nc.vector.bn_aggr(moments[:, u, s, :], stats[:, u, s, :]).then_inc(moments_done, 1)

            def normalise(b, u):
                k = 2 * b + u
                dve.wait_ge(std_done, k + 1)
                nc.vector.reciprocal(rstd[:, u, :], rstd[:, u, :]).then_inc(rstd_done, 1)
                dve.wait_ge(rstd_done, k + 1)
                dve.wait_ge(transposed, FREE + 2 * b)
                for s in range(4):
                    nc.vector.tensor_scalar(norm[:, u, s:s + 1, :], x[:, bass.ds(8 * b + 4 * u + s, 1), :],
                                            moments[:, u, s, 0:1], rstd[:, u, s:s + 1],
                                            ALU.subtract, ALU.mult).then_inc(norm_done, 1)

            def split(b, u, m):
                k = 2 * b + u
                dve.wait_ge(qk_left, FREE + 2 * (4 * k + m) + 2)
                nc.vector.tensor_tensor(qk32[:, m, :], qk32[:, m, :], parts[:, u, m, 0, :], ALU.subtract)\
                    .then_inc(rest_done, 1)
                dve.wait_ge(rest_done, 4 * k + m + 1)
                nc.vector.tensor_copy(parts[:, u, m, 1, :], qk32[:, m, :]).then_inc(mid_done, 1)
                dve.wait_ge(mid_done, 4 * k + m + 1)
                nc.vector.tensor_tensor(parts[:, u, m, 2, :], qk32[:, m, :], parts[:, u, m, 1, :],
                                        ALU.subtract).then_inc(low_done, 1)

            def value(b, u, s):
                dve.wait_ge(v_made, FREE + 2 * (2 * b + u) + s // 2 + 1)
                if s == 0:
                    dve.wait_ge(stored[u], FREE + 16 * stores * b)
                dst = values[:, u, s].rearrange("p g (j c) -> p (g j) c", c=VW)[:, :, 0:HD]
                nc.vector.tensor_tensor(
                    dst, accs[:, s // 2, s % 2 * D:s % 2 * D + D].rearrange("p (h d) -> p h d", d=HD),
                    t["b_v"][:, layer, :].rearrange("p (h d) -> p h d", d=HD), ALU.add).then_inc(v_left, 1)

            def chunk(b, u, more):
                if more:
                    statistics(b + 1, u)
                split(b, u, 0)
                if more:
                    normalise(b + 1, u)
                for m in range(1, 4):
                    split(b, u, m)
                for s in range(4):
                    value(b, u, s)

            for u in range(2):
                statistics(0, u, first=True)
            for u in range(2):
                normalise(0, u)
            dve.wait_ge(ones_set, 1)
            if layer == 0:
                dve.wait_ge(t["loaded"], 16 * t["loads"])
                for other in range(2):
                    nc.vector.tensor_scalar(t["b_qk"][:, other, 0:2], t["b_qk"][:, other, 0:2], (0.25, 0.0625)[other],
                                            None, ALU.mult).then_inc(bias_scaled, 1)
            with dve.Fori(0, B - 1) as b:
                for u in range(2):
                    chunk(b, u, True)
            for u in range(2):
                chunk(B - 1, u, False)

        @block.scalar
        def _(act):
            act.sem_inc(normT_done, FREE)
            act.sem_inc(qk_left, FREE)

            def root(b, u):
                act.wait_ge(moments_done, 4 * (2 * b + u) + 4)
                nc.scalar.activation(rstd[:, u, :], moments[:, u, :, 1], ACT.Sqrt, bias=t["eps"][:, 0:1])\
                    .then_inc(std_done, 1)

            def copy(b, u):
                act.wait_ge(transposed, FREE + 2 * b + u + 1)
                act.wait_ge(v_made, FREE + 2 * (2 * b + u - 1))
                nc.scalar.copy(normT[:, u, :], big[:, u, :]).then_inc(normT_done, 1)

            def evacuate(b, u, m):
                k = 2 * b + u
                act.wait_ge(qk_made, 4 * k + m + 1)
                act.wait_ge(low_done, FREE + 4 * k)
                for dst in (qk32[:, m, :], parts[:, u, m, 0, :]):
                    nc.scalar.activation(dst, ring[:, m % 2, :], ACT.Identity, bias=t["b_qk"][:, layer, m:m + 1],
                                         scale=scale if m < 2 else 1.0).then_inc(qk_left, 1)

            def chunk(b, u, more):
                act.wait_ge(stored[u], FREE + 16 * stores * b)
                evacuate(b, u, 0)
                if more:
                    root(b + 1, u)
                for m in range(1, 4):
                    evacuate(b, u, m)
                if more:
                    copy(b + 1, u)

            if layer == 0:
                act.wait_ge(t["eps_set"], 1)
            for u in range(2):
                root(0, u)
            for u in range(2):
                copy(0, u)
            if layer == 0:
                act.wait_ge(bias_scaled, 2)
            with act.Fori(0, B - 1) as b:
                for u in range(2):
                    chunk(b, u, True)
            for u in range(2):
                chunk(B - 1, u, False)

        @block.tensor
        def _(pe):
            pe.sem_inc(transposed, FREE)
            pe.sem_inc(v_made, FREE)

            def transpose(b, u):
                pe.wait_ge(norm_done, FREE + 4 * (2 * b + u) + 4)
                pe.wait_ge(normT_done, FREE + 2 * b)
                for s in range(4):
                    for c in range(DC):
                        last = nc.tensor.transpose(big[:, u, c * C + s * P:c * C + (s + 1) * P],
                                                   norm[:, u, s, c * P:(c + 1) * P], t["ident"][:])
                last.then_inc(transposed, 1)

            def products(b, u):
                k = 2 * b + u
                pe.wait_ge(normT_done, FREE + k + 1)
                for m in range(4):
                    if u or m >= 2:
                        pe.wait_ge(qk_left, FREE + 2 * (4 * k + m - 1))
                    else:
                        pe.wait_ge(qk_left, FREE + 16 * b)
                    for c in range(DC):
                        last = nc.tensor.matmul(ring[:, m % 2, :],
                                                t["w_qkv"][:, layer, c, m * P:(m + 1) * P],
                                                normT[:, u, c * C:(c + 1) * C], start=c == 0, stop=c == DC - 1)
                    last.then_inc(qk_made, 1)
                for s in range(4):
                    if s % 2 == 0:
                        pe.wait_ge(v_left, FREE + 4 * k)
                    for c in range(DC):
                        last = nc.tensor.matmul(accs[:, s // 2, s % 2 * D:s % 2 * D + D],
                                                normT[:, u, c * C + s * P:c * C + (s + 1) * P],
                                                t["w_qkv"][:, layer, c, 2 * D:3 * D],
                                                start=c == 0, stop=c == DC - 1)
                    if s % 2:
                        last.then_inc(v_made, 1)

            if layer == 0:
                pe.wait_ge(t["loaded"], 16 * t["loads"])
            for u in range(2):
                transpose(0, u)
            if layer == 0:
                pe.wait_ge(t["weights_loaded"], 32)
            with pe.Fori(0, B - 1) as b:
                for u in range(2):
                    products(b, u)
                    transpose(b + 1, u)
            for u in range(2):
                products(B - 1, u)


def q_k_loads(t, layer, b, s):
    qT, kT = t["qT"], t["kT"]
    loads = [(qT[block0 * HD:(block0 + count) * HD, s],
              t["q_dram"][b, s, part:part + count].rearrange("b a r j t -> (b a r) j t"))
             for block0, part, count in Q_RUNS]
    loads += [(kT[block0 * HD:(block0 + 1) * HD, s], t["k_dram"][b, s, part].rearrange("b r j t -> (b r) j t"))
              for block0, part in K_RUNS]
    return loads + [(qT[QK_ROWS:K_MAX, s], t["pos_q"][layer, s]), (kT[QK_ROWS:K_EXP, s], t["pos_k"][layer, s])]


def attend(nc, sem, layer, t):
    scores, ring, accs = t["psum"][:, 0:DEPTH, :], t["psum"][:, DEPTH:2 * DEPTH, :], t["psum"][:, 6:8, :]
    n = f"a{layer}_"
    with ExitStack() as ctx:
        def sb(name, shape, dt=F32):
            return ctx.enter_context(nc.sbuf_tensor(n + name, shape, dt))

        qT, kT, arrived = t["qT"], t["kT"], t["arrived"]
        val = sb("val", [P, SLOTS, TB, P])
        prob = sb("prob", [P, PROBS, GH, C])
        tops = sb("tops", [P, SLOTS, 3, 4, GH])
        rest = sb("rest", [P, SLOTS, 2 * 4 * GH])
        unread = sb("unread", [P, 1])
        topp = sb("topp", [P, SLOTS, PARTS, GH, 8], BF16)
        topT = sb("topT", [PARTS * GH * 8, SLOTS, P], BF16)
        heads = sb("heads", [P, 2, C])
        bias_parts = sb("bias_parts", [BIAS_ROWS, PARTS, D], BF16)
        bias_rest = sb("bias_rest", [BIAS_ROWS, D])
        den = sb("den", [2 * NH * (B - 1), C])

        val_arrived = [sem(n + f"val_arrived{i}") for i in range(SLOTS)]
        toprows = [sem(n + f"toprows{i}") for i in range(SLOTS)]
        ring_made = sem(n + "ring_made")
        ring_free = sem(n + "ring_free")
        ring_seen = sem(n + "ring_seen")
        table_loaded = sem(n + "table_loaded")
        chain = sem(n + "chain")
        scores_made = sem(n + "scores_made")
        scores_free = sem(n + "scores_free")
        prob_used = sem(n + "prob_used")
        heads_left = sem(n + "heads_left")
        top_merged = sem(n + "top_merged")
        top_high = sem(n + "top_high")
        top_rest = sem(n + "top_rest")
        top_mid = sem(n + "top_mid")
        top_low = sem(n + "top_low")
        stored = [sem(n + f"stored{i}") for i in range(2)]
        den_loaded = sem(n + "den_loaded")
        den_inverted = sem(n + "den_inverted")
        inv_stored = sem(n + "inv_stored")

        def loop(eng, run, batch_begins=lambda it: None):
            run(BEFORE, 0, 0)
            with eng.Fori(0, B - 1) as it:
                batch_begins(it)
                run(BODY, it, banks(BEFORE))
            batch_begins(B - 1)
            run(LAST, B - 1, banks(BEFORE))

        n_blocks = len(BLOCKS)
        causal = sem(n + "causal")
        exps_seen = sem(n + "exps_seen")

        def where(g):
            return g % SLOTS, g // SLOTS

        with nc.Block() as block:
            @block.sync
            def _(sp):
                def load_q_k(b, s):
                    for dst, src in q_k_loads(t, layer, b, s):
                        sp.dma_start(dst, src).then_inc(arrived[s], 16)

                def load_values(it, g):
                    s, more = where(g)
                    sp.dma_start(val[:, s], t["v_dram"][bass.ds(it + more, 1), s].rearrange("b p k c -> (b p) k c"))\
                        .then_inc(val_arrived[s], 16)

                def run(steps, it, first):
                    r = 0
                    for step in steps:
                        g = step[1]
                        s, more = where(g)
                        if step[0] in "MT":
                            made = first + r + it * banks(BODY)
                            r += 1
                        if step[0] == "T":
                            sp.wait_ge(ring_free, DEPTH + made + 1)
                            for part in range(PARTS):
                                rows = slice(part * GH * 8, (part + 1) * GH * 8)
                                sp.dma_start(qT[K_MAX + part:K_MAX + part + 1, s],
                                             topT[rows, s, :]).then_inc(toprows[s], 16)
                        if step[0] == "D":
                            for qc in range(2):
                                sp.wait_ge(stored[qc], FREE + 16 * NG * (B - 1))
                            den_rows = t["o_dram"][0:B - 1].rearrange("b g (j r) t -> (b g j) r t", r=VW)[:, HD, :]
                            sp.dma_start(den[:], den_rows.rearrange("h (u t) -> h u t", u=2)).then_inc(den_loaded, 16)
                        if step[0] == "W":
                            sp.wait_ge(den_inverted, 1)
                            sp.dma_start(t["i_dram"][0:NH * (B - 1)].rearrange("h (u t) -> (h u) t", u=2), den[:])\
                                .then_inc(inv_stored, 16)
                        if step[0] == "H":
                            sp.wait_ge(inv_stored, 16)
                            for dst, src in head_loads(t["o_dram"], t["i_dram"], t["head_slot"], 0):
                                sp.dma_start(dst, src).then_inc(t["head_arrived"], 16)
                        if step[0] == "O":
                            qc = step[2]
                            sp.wait_ge(heads_left, 2 + 2 * (NG * it + g) + qc + 1)
                            dst = t["o_dram"][bass.ds(it, 1), g, :, qc * C:(qc + 1) * C]
                            sp.dma_start(dst.rearrange("b r t -> (b r) t"), heads[:, qc, :])\
                                .then_inc(stored[qc], 16)
                            if qc and steps is not LAST:
                                sp.wait_ge(prob_used, PROBS + n_blocks * (NG * it + g + 1))
                                load_q_k(bass.ds(it + 1, 1), s)
                                load_values(it, g + SLOTS)

                for i in range(SLOTS):
                    sp.sem_inc(toprows[i], FREE)
                for qc in range(2):
                    sp.sem_inc(stored[qc], FREE)
                for g in range(SLOTS):
                    if g:
                        load_q_k(bass.ds(0, 1), g)
                    load_values(0, g)
                loop(sp, run)
                for qc in range(2):
                    sp.wait_ge(stored[qc], FREE + 16 * GROUPS)

            @block.tensor
            def _(pe):
                pe.sem_inc(prob_used, PROBS)

                def run(steps, it, first):
                    r = 0
                    for step in steps:
                        g = step[1]
                        s, more = where(g)
                        G = NG * it + g
                        if step[0] in "MT":
                            bank = (first + r) % DEPTH
                            made = first + r + it * banks(BODY)
                            r += 1
                        if step[0] == "M":
                            cls, hs, qb, k0, keys = MAX_UNITS[step[2]]
                            if step[2] == 0:
                                pe.wait_ge(arrived[s], 16 * LOADS * (it + more + 1))
                            pe.wait_ge(ring_free, made + 1)
                            for i, h in enumerate(hs):
                                cols = ring[:, bank, i * keys:(i + 1) * keys]
                                last = nc.tensor.matmul(cols, qT[0:K_MAX, s, h, qb * P:(qb + 1) * P],
                                                        kT[0:K_MAX, s, h, k0:k0 + keys],
                                                        start=True, stop=True, skip_group_check=True)
                            last.then_inc(ring_made, 1)
                        if step[0] == "T":
                            pe.wait_ge(top_low, G + 1)
                            pe.wait_ge(ring_free, made + 1)
                            nc.tensor.transpose(ring[:, bank, 0:P // 2].bitcast(BF16)[0:PARTS * GH * 8, :],
                                                topp[:, s].rearrange("p a h q -> p (a h q)"), t["ident_b"][:])\
                                .then_inc(ring_made, 1)
                        if step[0] == "E":
                            _, _, n, h = step
                            kb, qc = BLOCKS[n]
                            e = GH * (n_blocks * G + n) + h
                            slot = (GH * (n_blocks * g + n) + h) % DEPTH
                            if n == 0 and h == 0:
                                pe.wait_ge(toprows[s], FREE + 16 * PARTS * (it + more + 1))
                            pe.wait_ge(scores_free, e + 1)
                            q0, q1 = max(kb * P, qc * C), (qc + 1) * C
                            last = nc.tensor.matmul(scores[:, slot, 0:q1 - q0],
                                                    kT[0:K_EXP, s, h, kb * P:(kb + 1) * P],
                                                    qT[0:K_EXP, s, h, q0:q1],
                                                    start=True, stop=True)
                            last.then_inc(scores_made, 1)
                        if step[0] == "V":
                            n = step[2]
                            kb, qc = BLOCKS[n]
                            v = n_blocks * G + n
                            if n in DIAGONAL:
                                pe.wait_ge(causal, TB * G + DIAGONAL.index(n) + 1)
                            else:
                                pe.wait_ge(scores_free, DEPTH + GH * (v + 1))
                            if n == 0:
                                pe.wait_ge(val_arrived[s], 16 * (it + more + 1))
                            if kb == 0:
                                pe.wait_ge(heads_left, 2 * G + qc + 1)
                            q0, q1 = max(kb * P, qc * C), (qc + 1) * C
                            for h in range(GH):
                                last = nc.tensor.matmul(accs[h * VW:(h + 1) * VW, qc, q0 - qc * C:C],
                                                        val[:, s, kb, h * VW:(h + 1) * VW],
                                                        prob[:, n % PROBS, h, 0:q1 - q0],
                                                        start=kb == 0, stop=kb == 4 * qc + 3,
                                                        skip_group_check=True)
                            last.then_inc(prob_used, 1)

                loop(pe, run)

            @block.scalar
            def _(act):
                act.sem_inc(scores_free, DEPTH)
                act.sem_inc(heads_left, 2)

                def run(steps, it, _):
                    for step in steps:
                        G = NG * it + step[1]
                        if step[0] == "E":
                            _, _, n, h = step
                            kb, qc = BLOCKS[n]
                            e = GH * (n_blocks * G + n) + h
                            slot = (GH * (n_blocks * step[1] + n) + h) % DEPTH
                            width = (qc + 1) * C - max(kb * P, qc * C)
                            act.wait_ge(scores_made, e + 1)
                            if h == 0:
                                act.wait_ge(prob_used, n_blocks * G + n + 1)
                            nc.scalar.activation(prob[:, n % PROBS, h, 0:width], scores[:, slot, 0:width], ACT.Exp)\
                                .then_inc(scores_free, 1)
                        if step[0] == "O":
                            qc = step[2]
                            act.wait_ge(prob_used, PROBS + n_blocks * G + BLOCKS.index((4 * qc + 3, qc)) + 1)
                            act.wait_ge(stored[qc], FREE + 16 * G)
                            nc.scalar.copy(heads[:, qc, :], accs[:, qc, :]).then_inc(heads_left, 1)

                def load_exponential(it):
                    act.wait_ge(table_loaded, it + 1)
                    nc.scalar.activation(unread[:], t["eps"][:], ACT.Exp).then_inc(table_loaded, 1)

                act.sem_inc(table_loaded, 1)
                loop(act, run, load_exponential)

            @block.vector
            def _(dve):
                dve.sem_inc(ring_free, DEPTH)
                steps_done = [0]

                def link(ins):
                    steps_done[0] += 1
                    ins.then_inc(chain, 1)
                    dve.wait_ge(chain, steps_done[0])

                def split_bias(no, bias):
                    left = bias_rest[:]
                    link(nc.vector.tensor_copy(bias_parts[:, 0, :], bias))
                    link(nc.vector.tensor_tensor(left, bias, bias_parts[:, 0, :], ALU.subtract))
                    link(nc.vector.tensor_copy(bias_parts[:, 1, :], left))
                    link(nc.vector.tensor_tensor(bias_parts[:, 2, :], left, bias_parts[:, 1, :], ALU.subtract))
                    for part in range(PARTS):
                        row = slice(32 * part, 32 * part + 1)
                        link(nc.vector.tensor_copy(t["bias_rows"][row, no, :], bias_parts[row, part, :]))

                def run(steps, it, first):
                    r = 0
                    for step in steps:
                        g = step[1]
                        s, more = where(g)
                        G = NG * it + g
                        if step[0] in "MT":
                            bank = (first + r) % DEPTH
                            made = first + r + it * banks(BODY)
                            r += 1
                            dve.wait_ge(ring_made, made + 1)
                        if step[0] == "M":
                            cls, hs, qb, _, keys = MAX_UNITS[step[2]]
                            if cls == 2:
                                nc.vector.reduce_max(tops[:, s, cls, qb % 4, hs[0]:hs[0] + 1], ring[:, bank, 0:keys],
                                                     axis=AX_X).then_inc(ring_free, 1)
                            else:
                                dve.sem_inc(ring_seen, 1)
                                for i, h in enumerate(hs):
                                    cols = ring[:, bank, i * keys:(i + 1) * keys]
                                    last = nc.vector.tensor_tensor_reduce(
                                        cols, cols, t["mask_row"][:, C - keys:C], 1.0, 2 * MASKED, ALU.add, ALU.max,
                                        accum_out=tops[:, s, cls, qb % 4, h:h + 1])
                                last.then_inc(ring_free, 1)
                        if step[0] == "F":
                            dve.wait_ge(ring_free, DEPTH + first + r + it * banks(BODY))
                            nc.vector.tensor_tensor(tops[:, s, 1], tops[:, s, 1], tops[:, s, 2], ALU.max)\
                                .then_inc(top_merged, 1)
                            top = tops[:, s, 0:2].rearrange("p c q h -> p (c q) h")
                            left = rest[:, s].rearrange("p (q h) -> p q h", h=GH)

                            def part(i):
                                return topp[:, s, i].rearrange("p h q -> p q h")

                            dve.wait_ge(top_merged, G + 1)
                            nc.vector.tensor_scalar(part(0), top, OFFSET, -1.0, ALU.add, ALU.mult)\
                                .then_inc(top_high, 1)
                            dve.wait_ge(top_high, G + 1)
                            nc.vector.scalar_tensor_tensor(left, top, OFFSET, part(0), ALU.add, ALU.add)\
                                .then_inc(top_rest, 1)
                            dve.wait_ge(top_rest, G + 1)
                            nc.vector.tensor_scalar(part(1), left, -1.0, None, ALU.mult).then_inc(top_mid, 1)
                            dve.wait_ge(top_mid, G + 1)
                            nc.vector.scalar_tensor_tensor(part(2), left, -1.0, part(1), ALU.mult, ALU.subtract)\
                                .then_inc(top_low, 1)
                        if step[0] == "R":
                            dve.wait_ge(den_loaded, 16)
                            nc.vector.reciprocal(den[:], den[:]).then_inc(den_inverted, 1)
                            if layer == 0:
                                for no, bias in enumerate(t["biases"]):
                                    split_bias(no, bias)
                        if step[0] == "T":
                            dve.wait_ge(toprows[s], FREE + 16 * PARTS * (it + more))
                            nc.vector.tensor_copy(topT[:, s, :],
                                                  ring[:, bank, 0:P // 2].bitcast(BF16)[0:PARTS * GH * 8, :])\
                                .then_inc(ring_free, 1)

                loop(dve, run)

            @block.gpsimd
            def _(pool):
                def run(steps, it, _):
                    for step in steps:
                        if step[0] == "E" and step[2] in DIAGONAL and step[3] == GH - 1:
                            G, n = NG * it + step[1], step[2]
                            pool.wait_ge(scores_free, DEPTH + GH * (n_blocks * G + n + 1))
                            pool.sem_inc(exps_seen, 1)
                            own = prob[:, n % PROBS, :, 0:P]
                            nc.gpsimd.affine_select(out=own, in_=own, compare_op=ALU.is_ge, fill=0.0, base=0,
                                                    pattern=[[0, GH], [1, P]], channel_multiplier=-1)\
                                .then_inc(causal, 1)

                loop(pool, run)


def head_loads(o_dram, i_dram, slot, k):
    b, tokens = k // 2, slice(k % 2 * C, k % 2 * C + C)
    rows = o_dram.rearrange("b g (j r) t -> (b g j) r t", r=VW)
    loads = []
    for c in range(DC):
        heads = slice(NH * b + c * NH // 2, NH * b + (c + 1) * NH // 2)
        loads.append((slot[:, 0, c], rows[heads, 0:HD, tokens]))
        src = i_dram[heads, tokens].rearrange("h (o t) -> h o t", o=1)
        loads.append((slot[:, 1, c], src.to_broadcast([NH // 2, HD, C])))
    return loads


def project_out(nc, sem, layer, t):
    x, y = t["x"], t["norm"]
    stats, moments, rstd, shift, slots = t["stats"], t["moments"], t["rstd"], t["shift"], t["slots"]
    n = f"o{layer}_"
    IN_SLOTS = 4
    arrived = [t["head_arrived"]] + [sem(n + f"arrived{j}") for j in range(1, IN_SLOTS)]
    den_loaded = sem(n + "den_loaded")
    den_inverted = sem(n + "den_inverted")
    inv_stored = sem(n + "inv_stored")
    scaled = sem(n + "scaled")
    y_made = sem(n + "y_made")
    stats_done = sem(n + "stats_done")
    stats_seen = sem(n + "stats_seen")
    moments_done = sem(n + "moments_done")
    std_done = sem(n + "std_done")
    rstd_done = sem(n + "rstd_done")
    shift_done = sem(n + "shift_done")
    y_done = sem(n + "y_done")
    x_done = sem(n + "x_done")
    sizes = sem(n + "sizes")
    chain = sem(n + "chain")
    binary_done = sem(n + "binary_done")
    binary_transposed = sem(n + "binary_transposed")
    binaryT_done = sem(n + "binaryT_done")
    w = t["w_ffn"]
    with (nc.sbuf_tensor(n + "size", [P, DC, D], F32) as size,
          nc.sbuf_tensor(n + "alpha", [P, DC], F32) as alpha,
          nc.sbuf_tensor(n + "binary", [P, DC, D], F32) as binary,
          nc.sbuf_tensor(n + "heads_in", [P, IN_SLOTS - 1, 2, DC, C], F32) as heads_in,
          nc.sbuf_tensor(n + "denominators", [P, NH * S // P], F32) as den, nc.Block() as block):
        rows = t["o_dram"].rearrange("b g (j r) t -> (b g j) r t", r=VW)
        last = slice((B - 1) * NH, B * NH)
        head_slots = [t["head_slot"]] + [heads_in[:, j] for j in range(IN_SLOTS - 1)]
        pieces = P // NH

        @block.sync
        def _(sp):
            for k in range(1, 2 * B):
                if k == 2 * (B - 1):
                    sp.wait_ge(inv_stored, 16)
                if k >= IN_SLOTS:
                    sp.wait_ge(y_made, FREE + 2 * (k - IN_SLOTS + 1))
                for dst, src in head_loads(t["o_dram"], t["i_dram"], head_slots[k % IN_SLOTS], k):
                    sp.dma_start(dst, src).then_inc(arrived[k % IN_SLOTS], 16)

        @block.gpsimd
        def _(pool):
            with pool.Fori(0, 2 * B // IN_SLOTS) as i:
                for j in range(IN_SLOTS):
                    pool.wait_ge(arrived[j], 16 * 2 * DC * (i + 1))
                    sums, inverses = head_slots[j][:, 0], head_slots[j][:, 1]
                    nc.gpsimd.tensor_tensor(sums, sums, inverses, ALU.mult)\
                        .then_inc(scaled, 1)

        @block.tensor
        def _(pe):
            pe.sem_inc(y_made, FREE)
            with pe.Fori(0, 2 * B // IN_SLOTS) as i:
                for j in range(IN_SLOTS):
                    k = IN_SLOTS * i + j
                    pe.wait_ge(scaled, k + 1)
                    pe.wait_ge(y_done, FREE + 4 * (k - IN_SLOTS + 1))
                    for half in range(2):
                        nc.tensor.matmul(slots[:, j, half * C:(half + 1) * C].rearrange("p (s d) -> p s d", d=D),
                                         t["ones_b"][:], t["bias_rows"][:, layer:layer + 1, :].to_broadcast(
                                             [BIAS_ROWS, 2, D]), start=True, stop=False, skip_group_check=True)
                        for s in range(2 * half, 2 * half + 2):
                            for c in range(DC):
                                last = nc.tensor.matmul(slots[:, j, s * D:(s + 1) * D],
                                                        head_slots[j][:, 0, c, s * P:(s + 1) * P],
                                                        t["w_out"][:, layer, c, :],
                                                        start=False, stop=c == DC - 1, skip_group_check=True)
                        last.then_inc(y_made, 1)
            if layer == 1:
                pe.wait_ge(binary_done, 1)
                pe.wait_ge(y_done, FREE + 4 * (2 * B - IN_SLOTS + 1))
                for co in range(DC):
                    for ci in range(DC):
                        last = nc.tensor.transpose(slots[:, 0, ci * D + co * P:ci * D + (co + 1) * P],
                                                   binary[:, co, ci * P:(ci + 1) * P], t["ident"][:])
                last.then_inc(binary_transposed, 1)

        @block.vector
        def _(dve):
            dve.sem_inc(x_done, FREE)
            dve.wait_ge(den_loaded, 16)
            nc.vector.reciprocal(den[:], den[:]).then_inc(den_inverted, 1)
            steps = [0]

            def link(ins):
                steps[0] += 1
                ins.then_inc(chain, 1)
                dve.wait_ge(chain, steps[0])

            if layer == 1:
                dve.wait_ge(sizes, DC)
                link(nc.vector.tensor_scalar(alpha[:], alpha[:], 1.0 / D, None, ALU.mult))
                for c in range(DC):
                    link(nc.vector.tensor_scalar(binary[:, c, :], w[:, c, :], 0.0, 2.0, ALU.is_ge, ALU.mult))
                    link(nc.vector.tensor_scalar(binary[:, c, :], binary[:, c, :], -1.0, alpha[:, c:c + 1],
                                                 ALU.add, ALU.mult))
                    link(nc.vector.tensor_tensor(binary[:, c, :], binary[:, c, :], w[:, c, :], ALU.subtract))
                    link(nc.vector.tensor_tensor(binary[:, c, :], binary[:, c, :], w[:, c, :], ALU.add))
                dve.sem_inc(binary_done, 1)

            def moments_of(i, j):
                k, u = IN_SLOTS * i + j, j % 2
                for s in range(4):
                    if s % 2 == 0:
                        dve.wait_ge(y_made, FREE + 2 * k + s // 2 + 1)
                    nc.vector.bn_stats(stats[:, u, s, :], slots[:, j, s * D:(s + 1) * D]).then_inc(stats_done, 1)
                dve.wait_ge(stats_done, 4 * k + 4)
                dve.sem_inc(stats_seen, 1)
                for s in range(4):
                    nc.vector.bn_aggr(moments[:, u, s, :], stats[:, u, s, :]).then_inc(moments_done, 1)

            def inverted(i, j):
                k, u = IN_SLOTS * i + j, j % 2
                dve.wait_ge(std_done, k + 1)
                nc.vector.reciprocal(rstd[:, u, :], rstd[:, u, :]).then_inc(rstd_done, 1)
                dve.wait_ge(rstd_done, k + 1)
                nc.vector.scalar_tensor_tensor(shift[:, u, :], moments[:, u, :, 0], -1.0, rstd[:, u, :],
                                               ALU.mult, ALU.mult).then_inc(shift_done, 1)

            def residual(i, j):
                k = IN_SLOTS * i + j
                for s in range(4):
                    dve.wait_ge(y_done, FREE + 4 * k + s + 1)
                    here = x[:, bass.ds(4 * k + s, 1), :]
                    nc.vector.tensor_tensor(here, here, y[:, j % 2, s:s + 1, :], ALU.add).then_inc(x_done, 1)

            with dve.Fori(0, 2 * B // IN_SLOTS) as i:
                for j in range(IN_SLOTS):
                    moments_of(i, j)
                    if j:
                        residual(i, j - 1)
                    inverted(i, j)
                residual(i, IN_SLOTS - 1)
            if layer == 1:
                dve.wait_ge(binary_transposed, 1)
                nc.vector.tensor_copy(t["binaryT"][:].rearrange("p c o -> p (c o)"), slots[:, 0, 0:C])\
                    .then_inc(binaryT_done, 1)

        @block.scalar
        def _(act):
            act.dma_start(den[:], rows[last, HD, :].rearrange("h (u t) -> h u t", u=pieces)).then_inc(den_loaded, 16)
            if layer == 1:
                for c in range(DC):
                    nc.scalar.activation(size[:, c, :], w[:, c, :], ACT.Abs, accum_out=alpha[:, c:c + 1])\
                        .then_inc(sizes, 1)
            act.wait_ge(den_inverted, 1)
            act.dma_start(t["i_dram"][last].rearrange("h (u t) -> (h u) t", u=pieces), den[:]).then_inc(inv_stored, 16)
            act.sem_inc(y_done, FREE)
            with act.Fori(0, 2 * B // IN_SLOTS) as i:
                for j in range(IN_SLOTS):
                    k, u = IN_SLOTS * i + j, j % 2
                    act.wait_ge(moments_done, 4 * k + 4)
                    nc.scalar.activation(rstd[:, u, :], moments[:, u, :, 1], ACT.Sqrt, bias=t["eps"][:, 0:1])\
                        .then_inc(std_done, 1)
                    act.wait_ge(shift_done, k + 1)
                    act.wait_ge(x_done, FREE + 4 * (k - 1))
                    for s in range(4):
                        nc.scalar.activation(y[:, u, s, :], slots[:, j, s * D:(s + 1) * D], ACT.Identity,
                                             bias=shift[:, u, s:s + 1], scale=rstd[:, u, s:s + 1])\
                            .then_inc(y_done, 1)


def experts(nc, sem, io, t):
    x, norm, normT, big, ring, accs = t["x"], t["norm"], t["normT"], t["big"], t["ring"], t["accs"]
    stats, moments, rstd, shift = t["stats"], t["moments"], t["rstd"], t["shift"]
    nt = MT_TILES
    with ExitStack() as ctx:
        def sb(name, shape, dt=F32):
            return ctx.enter_context(nc.sbuf_tensor("e_" + name, shape, dt))

        w_in = sb("w_in", [P, 2, DC, 2 * FI])
        w_down = sb("w_down", [FC, 2, 2, D])
        idx = sb("idx", [P, nt, TOPK], I32)
        idx_f = sb("idx_f", [P, nt, TOPK])
        chosen_w = sb("chosen_w", [P, nt, TOPK])
        expert_no = sb("expert_no", [P, NE])
        share = sb("share", [P, nt, TOPK, NE])
        zero = sb("zero", [P, P])
        gated = sb("gated", [P, 2, nt, FI])
        act_in = sb("act_in", [P, 2, nt, FI])
        act_inT = sb("act_inT", [FC, 2, 2, nt * P])
        y = sb("y", [P, nt, D])

        routing = sem("e_routing")
        in_arrived = [sem(f"e_in_arrived{i}") for i in range(2)]
        down_arrived = [sem(f"e_down_arrived{i}") for i in range(2)]
        chain = sem("e_chain")
        moments_done = sem("e_moments_done")
        std_done = sem("e_std_done")
        zero_set = sem("e_zero_set")
        norm_done = sem("e_norm_done")
        transposed = sem("e_transposed")
        normT_done = sem("e_normT_done")
        in_made = sem("e_in_made")
        gate_done = sem("e_gate_done")
        act_done = sem("e_act_done")
        act_transposed = sem("e_act_transposed")
        actT_done = sem("e_actT_done")
        down_done = sem("e_down_done")
        y_done = sem("e_y_done")
        x_done = sem("e_x_done")

        with nc.Block() as block:
            @block.sync
            def _(sp):
                sp.dma_start(idx[:], io["topk_idx"].rearrange("(n p) k -> p n k", p=P)).then_inc(routing, 16)
                sp.dma_start(chosen_w[:], io["topk_weight"].rearrange("(n p) k -> p n k", p=P)).then_inc(routing, 16)
                sp.dma_start(expert_no[:], io["expert_no"]).then_inc(routing, 16)

                def load_in(i, e):
                    sp.wait_ge(in_made, FREE + nt * (2 * i + e - 1))
                    sp.dma_start(w_in[:, e % 2], io["w_in"][bass.ds(2 * i + e, 1)].rearrange("e p c f -> (e p) c f"))\
                        .then_inc(in_arrived[e % 2], 16)

                def load_down(i, e):
                    sp.wait_ge(down_done, FREE + 2 * i + e - 1)
                    sp.dma_start(w_down[:, e], io["w_down"][bass.ds(2 * i + e, 1)].rearrange("e p c f -> (e p) c f"))\
                        .then_inc(down_arrived[e], 16)

                for e in range(2):
                    load_in(0, e)
                with sp.Fori(0, NE // 2 - 1) as i:
                    for e in range(2):
                        load_in(i, e + 2)
                        load_down(i, e)
                for e in range(2):
                    load_down(NE // 2 - 1, e)

            @block.gpsimd
            def _(pool):
                nc.gpsimd.memset(zero[:], 0.0).then_inc(zero_set, 1)

            @block.vector
            def _(dve):
                dve.sem_inc(act_done, FREE)
                dve.sem_inc(actT_done, FREE)
                steps = [0]

                def link(ins):
                    steps[0] += 1
                    ins.then_inc(chain, 1)
                    dve.wait_ge(chain, steps[0])

                for s in range(nt):
                    link(nc.vector.bn_stats(stats[:, 0, s, :], x[:, s, :]))
                    link(nc.vector.bn_aggr(moments[:, 0, s, :], stats[:, 0, s, :]))
                dve.sem_inc(moments_done, 1)
                dve.wait_ge(std_done, 1)
                link(nc.vector.reciprocal(rstd[:, 0, 0:nt], rstd[:, 0, 0:nt]))
                for s in range(nt):
                    nc.vector.tensor_scalar(norm[:, 0, s, :], x[:, s, :], moments[:, 0, s, 0:1], rstd[:, 0, s:s + 1],
                                            ALU.subtract, ALU.mult).then_inc(norm_done, 1)
                dve.wait_ge(transposed, 1)
                nc.vector.tensor_copy(normT[:, 0, 0:DC * nt * P], big[:, 0, 0:DC * nt * P]).then_inc(normT_done, 1)
                dve.wait_ge(routing, 48)
                link(nc.vector.tensor_copy(idx_f[:], idx[:]))
                for s in range(nt):
                    for k in range(TOPK):
                        link(nc.vector.tensor_scalar(share[:, s, k, :], expert_no[:], idx_f[:, s, k:k + 1],
                                                     chosen_w[:, s, k:k + 1], ALU.is_equal, ALU.mult))
                for s in range(nt):
                    for k in range(1, TOPK):
                        link(nc.vector.tensor_tensor(share[:, s, 0, :], share[:, s, 0, :], share[:, s, k, :],
                                                     ALU.add))

                def weighted(i, e):
                    no = 2 * i + e
                    dve.wait_ge(gate_done, nt * no + nt)
                    dve.wait_ge(act_transposed, FREE + no - 1)
                    for s in range(nt):
                        nc.vector.scalar_tensor_tensor(
                            act_in[:, e % 2, s, :], gated[:, e % 2, s, :], share[:, s, 0, bass.ds(no, 1)],
                            big[:, e % 2, s * C + FI:s * C + 2 * FI], ALU.mult, ALU.mult).then_inc(act_done, 1)

                def copied(i, e):
                    no = 2 * i + e
                    dve.wait_ge(act_transposed, FREE + no + 1)
                    dve.wait_ge(down_done, FREE + no - 1)
                    nc.vector.tensor_copy(act_inT[:, e].rearrange("p c t -> p (c t)"),
                                          ring[0:FC, e, :]).then_inc(actT_done, 1)

                weighted(0, 0)
                with dve.Fori(0, NE // 2 - 1) as i:
                    for e in range(2):
                        weighted(i, e + 1)
                        copied(i, e)
                weighted(NE // 2 - 1, 1)
                for e in range(2):
                    copied(NE // 2 - 1, e)
                dve.wait_ge(down_done, FREE + NE)
                link(nc.vector.tensor_copy(y[:].rearrange("p s d -> p (s d)"), accs[:, 0, :]))
                for s in range(nt):
                    link(nc.vector.bn_stats(stats[:, 0, s, :], y[:, s, :]))
                    link(nc.vector.bn_aggr(moments[:, 0, s, :], stats[:, 0, s, :]))
                dve.sem_inc(moments_done, 1)
                dve.wait_ge(std_done, 2)
                link(nc.vector.reciprocal(rstd[:, 0, 0:nt], rstd[:, 0, 0:nt]))
                for s in range(nt):
                    link(nc.vector.tensor_scalar(y[:, s, :], y[:, s, :], moments[:, 0, s, 0:1], rstd[:, 0, s:s + 1],
                                                 ALU.subtract, ALU.mult))
                    link(nc.vector.tensor_tensor(x[:, s, :], x[:, s, :], y[:, s, :], ALU.add))

            @block.scalar
            def _(act):
                def root(n):
                    act.wait_ge(moments_done, n)
                    nc.scalar.activation(rstd[:, 0, 0:nt], moments[:, 0, 0:nt, 1], ACT.Sqrt, bias=t["eps"][:, 0:1])\
                        .then_inc(std_done, 1)

                root(1)
                with act.Fori(0, NE // 2) as i:
                    for e in range(2):
                        for s in range(nt):
                            act.wait_ge(in_made, FREE + nt * (2 * i + e) + s + 1)
                            act.wait_ge(act_done, FREE + nt * (2 * i + e - 1))
                            nc.scalar.activation(gated[:, e, s, :], big[:, e, s * C:s * C + FI], ACT.Silu)\
                                .then_inc(gate_done, 1)
                root(2)

            @block.tensor
            def _(pe):
                pe.sem_inc(down_done, FREE)
                pe.sem_inc(in_made, FREE)
                pe.sem_inc(act_transposed, FREE)
                pe.wait_ge(norm_done, nt)
                for s in range(nt):
                    for c in range(DC):
                        last = nc.tensor.transpose(big[:, 0, (c * nt + s) * P:(c * nt + s + 1) * P],
                                                   norm[:, 0, s, c * P:(c + 1) * P], t["ident"][:])
                last.then_inc(transposed, 1)
                pe.wait_ge(normT_done, 1)
                pe.wait_ge(zero_set, 1)
                nc.tensor.matmul(accs[:, 0, :], zero[:], normT[:, 0, 0:C], start=True, stop=True,
                                 skip_group_check=True)

                def gate_up(i, e):
                    pe.wait_ge(in_arrived[e % 2], 16 * (i + e // 2 + 1))
                    pe.wait_ge(act_done, FREE + nt * (2 * i + e - 1))
                    for s in range(nt):
                        for c in range(DC):
                            last = nc.tensor.matmul(big[:, e % 2, s * C:s * C + 2 * FI],
                                                    normT[:, 0, (c * nt + s) * P:(c * nt + s + 1) * P],
                                                    w_in[:, e % 2, c, :], start=c == 0, stop=c == DC - 1)
                        last.then_inc(in_made, 1)

                def turn(i, e):
                    no = 2 * i + e
                    pe.wait_ge(act_done, FREE + nt * no + nt)
                    pe.wait_ge(actT_done, FREE + no - 1)
                    for c in range(2):
                        for s in range(nt):
                            last = nc.tensor.transpose(ring[0:FC, e % 2, (c * nt + s) * P:(c * nt + s + 1) * P],
                                                       act_in[:, e % 2, s, c * FC:(c + 1) * FC], t["ident"][:])
                    last.then_inc(act_transposed, 1)

                def down(i, e):
                    pe.wait_ge(down_arrived[e], 16 * (i + 1))
                    pe.wait_ge(actT_done, FREE + 2 * i + e + 1)
                    for s in range(nt):
                        for c in range(2):
                            last = nc.tensor.matmul(accs[:, 0, s * D:(s + 1) * D],
                                                    act_inT[:, e, c, s * P:(s + 1) * P], w_down[:, e, c, :],
                                                    start=False, stop=True, skip_group_check=True)
                    last.then_inc(down_done, 1)

                gate_up(0, 0)
                gate_up(0, 1)
                turn(0, 0)
                with pe.Fori(0, NE // 2 - 1) as i:
                    for e in range(2):
                        gate_up(i, e + 2)
                        turn(i, e + 1)
                        down(i, e)
                turn(NE // 2 - 1, 1)
                for e in range(2):
                    down(NE // 2 - 1, e)


def linear(nc, sem, io, out, t):
    x, norm, normT, big, turned = t["x"], t["norm"], t["normT"], t["big"], t["turned"]
    stats, moments, rstd, shift = t["stats"], t["moments"], t["rstd"], t["shift"]
    with ExitStack() as ctx:
        def sb(name, shape, dt=F32):
            return ctx.enter_context(nc.sbuf_tensor("l_" + name, shape, dt))

        binaryT = t["binaryT"]
        y = sb("y", [P, 2, 4, D])
        statsy = sb("statsy", [P, 2, 4, 6])
        momentsy = sb("momentsy", [P, 2, 4, 2])
        rstdy = sb("rstdy", [P, 2, 4])

        stats_done = sem("l_stats_done")
        stats_seen = sem("l_stats_seen")
        moments_done = sem("l_moments_done")
        std_done = sem("l_std_done")
        rstd_done = sem("l_rstd_done")
        norm_done = sem("l_norm_done")
        transposed = sem("l_transposed")
        normT_done = sem("l_normT_done")
        y_made = sem("l_y_made")
        statsy_done = sem("l_statsy_done")
        statsy_seen = sem("l_statsy_seen")
        momentsy_done = sem("l_momentsy_done")
        stdy_done = sem("l_stdy_done")
        rstdy_done = sem("l_rstdy_done")
        shift_done = sem("l_shift_done")
        y_done = sem("l_y_done")
        y_seen = sem("l_y_seen")
        x_done = sem("l_x_done")
        written = sem("l_written")

        with nc.Block() as block:
            @block.sync
            def _(sp):
                with sp.Fori(0, B) as b:
                    for u in range(2):
                        sp.wait_ge(x_done, FREE + 2 * b + u + 1)
                        dst = out[bass.ds(b, 1), u * C:(u + 1) * C, :]
                        sp.dma_start(dst.rearrange("b (s p) d -> p (b s) d", p=P),
                                     x[:, bass.ds(8 * b + 4 * u, 4), :]).then_inc(written, 16)
                sp.wait_ge(written, 16 * 2 * B)

            @block.scalar
            def _(act):
                act.sem_inc(normT_done, FREE)
                act.sem_inc(y_done, FREE)

                def root(b, u):
                    act.wait_ge(moments_done, 4 * (2 * b + u) + 4)
                    nc.scalar.activation(rstd[:, u, :], moments[:, u, :, 1], ACT.Sqrt, bias=t["eps"][:, 0:1])\
                        .then_inc(std_done, 1)

                def copy(b, u):
                    k = 2 * b + u
                    act.wait_ge(transposed, FREE + k + 1)
                    act.wait_ge(y_made, FREE + 2 * (k - 1))
                    nc.scalar.copy(normT[:, u, :], turned[:, u, :]).then_inc(normT_done, 1)

                def root_y(b, u):
                    act.wait_ge(momentsy_done, 4 * (2 * b + u) + 4)
                    nc.scalar.activation(rstdy[:, u, :], momentsy[:, u, :, 1], ACT.Sqrt, bias=t["eps"][:, 0:1])\
                        .then_inc(stdy_done, 1)

                def normalise_y(b, u):
                    act.wait_ge(shift_done, 2 * b + u + 1)
                    act.wait_ge(x_done, FREE + 2 * b + u - 1)
                    for s in range(4):
                        nc.scalar.activation(y[:, u, s, :], big[:, u, s * D:(s + 1) * D], ACT.Identity,
                                             bias=shift[:, u, s:s + 1], scale=rstdy[:, u, s:s + 1]).then_inc(y_done, 1)

                for u in range(2):
                    root(0, u)
                for u in range(2):
                    copy(0, u)
                root(1, 0)
                copy(1, 0)
                root_y(0, 0)
                with act.Fori(0, B - 2) as b:
                    root(b + 1, 1)
                    normalise_y(b, 0)
                    copy(b + 1, 1)
                    root_y(b, 1)
                    root(b + 2, 0)
                    normalise_y(b, 1)
                    copy(b + 2, 0)
                    root_y(b + 1, 0)
                root(B - 1, 1)
                normalise_y(B - 2, 0)
                copy(B - 1, 1)
                root_y(B - 2, 1)
                normalise_y(B - 2, 1)
                root_y(B - 1, 0)
                normalise_y(B - 1, 0)
                root_y(B - 1, 1)
                normalise_y(B - 1, 1)

            @block.gpsimd
            def _(pool):
                pool.sem_inc(x_done, FREE)
                with pool.Fori(0, B) as b:
                    for u in range(2):
                        pool.wait_ge(y_done, FREE + 4 * (2 * b + u) + 4)
                        pool.sem_inc(y_seen, 1)
                        here = x[:, bass.ds(8 * b + 4 * u, 4), :]
                        nc.gpsimd.tensor_tensor(here, here, y[:, u], ALU.add).then_inc(x_done, 1)

            @block.vector
            def _(dve):
                dve.sem_inc(norm_done, FREE)

                def statistics(b, u):
                    k = 2 * b + u
                    dve.wait_ge(norm_done, FREE + 8 * b)
                    for s in range(4):
                        nc.vector.bn_stats(stats[:, u, s, :], x[:, bass.ds(8 * b + 4 * u + s, 1), :])\
                            .then_inc(stats_done, 1)
                    dve.wait_ge(stats_done, 4 * k + 4)
                    dve.sem_inc(stats_seen, 1)
                    for s in range(4):
                        nc.vector.bn_aggr(moments[:, u, s, :], stats[:, u, s, :]).then_inc(moments_done, 1)

                def normalise(b, u):
                    k = 2 * b + u
                    dve.wait_ge(std_done, k + 1)
                    nc.vector.reciprocal(rstd[:, u, :], rstd[:, u, :]).then_inc(rstd_done, 1)
                    dve.wait_ge(rstd_done, k + 1)
                    dve.wait_ge(transposed, FREE + 2 * b)
                    for s in range(4):
                        nc.vector.tensor_scalar(norm[:, u, s:s + 1, :], x[:, bass.ds(8 * b + 4 * u + s, 1), :],
                                                moments[:, u, s, 0:1], rstd[:, u, s:s + 1],
                                                ALU.subtract, ALU.mult).then_inc(norm_done, 1)

                def moments_of(b, u):
                    k = 2 * b + u
                    for s in range(4):
                        if s % 2 == 0:
                            dve.wait_ge(y_made, FREE + 2 * k + s // 2 + 1)
                        nc.vector.bn_stats(statsy[:, u, s, :], big[:, u, s * D:(s + 1) * D]).then_inc(statsy_done, 1)
                    dve.wait_ge(statsy_done, 4 * k + 4)
                    dve.sem_inc(statsy_seen, 1)
                    for s in range(4):
                        nc.vector.bn_aggr(momentsy[:, u, s, :], statsy[:, u, s, :]).then_inc(momentsy_done, 1)

                def inverted(b, u):
                    k = 2 * b + u
                    dve.wait_ge(stdy_done, k + 1)
                    nc.vector.reciprocal(rstdy[:, u, :], rstdy[:, u, :]).then_inc(rstdy_done, 1)
                    dve.wait_ge(rstdy_done, k + 1)
                    nc.vector.scalar_tensor_tensor(shift[:, u, :], momentsy[:, u, :, 0], -1.0, rstdy[:, u, :],
                                                   ALU.mult, ALU.mult).then_inc(shift_done, 1)

                for u in range(2):
                    statistics(0, u)
                for u in range(2):
                    normalise(0, u)
                statistics(1, 0)
                normalise(1, 0)
                moments_of(0, 0)
                with dve.Fori(0, B - 2) as b:
                    statistics(b + 1, 1)
                    inverted(b, 0)
                    normalise(b + 1, 1)
                    moments_of(b, 1)
                    statistics(b + 2, 0)
                    inverted(b, 1)
                    normalise(b + 2, 0)
                    moments_of(b + 1, 0)
                statistics(B - 1, 1)
                inverted(B - 2, 0)
                normalise(B - 1, 1)
                moments_of(B - 2, 1)
                inverted(B - 2, 1)
                moments_of(B - 1, 0)
                inverted(B - 1, 0)
                moments_of(B - 1, 1)
                inverted(B - 1, 1)

            @block.tensor
            def _(pe):
                pe.sem_inc(transposed, FREE)
                pe.sem_inc(y_made, FREE)

                def transpose(b, u):
                    k = 2 * b + u
                    pe.wait_ge(norm_done, FREE + 4 * k + 4)
                    pe.wait_ge(normT_done, FREE + k - 1)
                    for s in range(4):
                        for c in range(DC):
                            last = nc.tensor.transpose(turned[:, u, c * C + s * P:c * C + (s + 1) * P],
                                                       norm[:, u, s, c * P:(c + 1) * P], t["ident"][:])
                    last.then_inc(transposed, 1)

                def product(b, u):
                    k = 2 * b + u
                    pe.wait_ge(normT_done, FREE + k + 1)
                    pe.wait_ge(y_done, FREE + 4 * (k - 1))
                    for half in range(2):
                        nc.tensor.matmul(big[:, u, half * C:(half + 1) * C].rearrange("p (s d) -> p s d", d=D),
                                         t["ones_b"][:], t["bias_rows"][:, 2:3, :].to_broadcast([BIAS_ROWS, 2, D]),
                                         start=True, stop=False, skip_group_check=True)
                        for s in range(2 * half, 2 * half + 2):
                            for c in range(DC):
                                last = nc.tensor.matmul(big[:, u, s * D:(s + 1) * D],
                                                        normT[:, u, c * C + s * P:c * C + (s + 1) * P],
                                                        binaryT[:, c, :], start=False, stop=c == DC - 1,
                                                        skip_group_check=True)
                        last.then_inc(y_made, 1)

                for u in range(2):
                    transpose(0, u)
                with pe.Fori(0, B - 1) as b:
                    for u in range(2):
                        product(b, u)
                        transpose(b + 1, u)
                for u in range(2):
                    product(B - 1, u)



def three_parts(a):
    bf16 = mybir.dt.np(BF16)
    high = a.astype(bf16)
    rest = a - high.astype(np.float32)
    mid = rest.astype(bf16)
    low = (rest - mid.astype(np.float32)).astype(bf16)
    return [p.astype(np.float32) for p in (high, mid, low)]


def constants():
    bf16 = mybir.dt.np(BF16)
    i = np.arange(P)
    pos = np.arange(S)
    near, far = (pos % P).astype(np.float32), (pos // P * P).astype(np.float32)
    start = 2.0 ** (-2.0 ** (-(np.log2(NH) - 3)))
    slopes = np.array([start * start ** n for n in range(NH)]).astype(np.float32).reshape(NG, GH)
    pos_q = np.zeros((2, NG, POS_ROWS, GH, S), np.float32)
    pos_k = np.zeros((2, NG, POS_ROWS + MAX_ROWS, GH, S), np.float32)
    pos_k[:, :, POS_ROWS:] = 1.0
    for n, part in enumerate(three_parts(slopes)):
        for m, place in enumerate((far, near)):
            row = 4 * n + 2 * m
            pos_q[1, :, row] = part[:, :, None]
            pos_k[1, :, row] = place
            pos_q[1, :, row + 1] = -place
            pos_k[1, :, row + 1] = part[:, :, None]
    return {
        "ident": np.eye(P, dtype=np.float32),
        "ident_b": np.eye(P, dtype=bf16),
        "mask_row": np.where(np.arange(C)[None, :] - (C - P) > i[:, None], MASKED, 0.0).astype(np.float32),
        "pos_q": pos_q.astype(bf16),
        "pos_k": pos_k.astype(bf16),
        "expert_no": np.broadcast_to(np.arange(NE, dtype=np.float32), (P, NE)),
    }


def layouts(a):
    order = np.arange(2 * D).reshape(4, 2, GH, HD).transpose(0, 1, 3, 2).reshape(-1)
    order = np.concatenate([order, np.arange(2 * D, 3 * D)])
    w_qkv = np.stack([a["L0_attn_w_qkv"].T, a["L1_attn_w_qkv"]])[:, :, order]
    b_qkv = np.stack([a["L0_attn_b_qkv"], a["L1_attn_b_qkv"]])
    w_out = np.stack([a["L0_attn_w_out"].T, a["L1_attn_w_proj"]])
    rows = (P, 2, D)
    w_in = np.concatenate([a["L0_ffn_gate_weight"], a["L0_ffn_up_weight"]], axis=1)
    return {
        "x": a["L0_attn_x"].reshape(B * S, D),
        "w_qkv": w_qkv.reshape(2, DC, P, 3 * D).transpose(2, 0, 1, 3),
        "b_qk": b_qkv[:, order[:2 * D]].reshape(2, 4, P).transpose(2, 0, 1),
        "b_v": np.broadcast_to(b_qkv[:, 2 * D:], rows),
        "w_out": w_out.reshape(2, DC, P, D).transpose(2, 0, 1, 3),
        "b_out": np.broadcast_to(np.stack([a["L0_attn_b_out"], a["L1_attn_b_proj"]]), rows),
        "w_in": w_in.transpose(0, 2, 1).reshape(NE, DC, P, 2 * FI).transpose(0, 2, 1, 3),
        "w_down": a["L0_ffn_down_weight"].transpose(0, 2, 1).reshape(NE, 2, FC, D).transpose(0, 2, 1, 3),
        "topk_idx": a["L0_ffn_topk_idx"].reshape(MT_TILES * P, TOPK),
        "topk_weight": a["L0_ffn_topk_weight"].reshape(MT_TILES * P, TOPK),
        "w_ffn": a["L1_ffn_weight"],
        "b_ffn": np.broadcast_to(a["L1_ffn_bias"], (P, D)),
    }


def kernel(**inputs):
    import concourse.bacc as bacc
    from concourse.bass_utils import run_bass_kernel_spmd

    nc = bacc.Bacc("TRN2", target_bir_lowering=False, num_devices=1)
    a = {name: np.asarray(v) for name, v in inputs.items()}
    arrays = {name: np.ascontiguousarray(v) for name, v in {**layouts(a), **constants()}.items()}
    io = {name: nc.dram_tensor(f"in_{name}", v.shape, mybir.dt.from_np(v.dtype), kind="ExternalInput").ap()
          for name, v in arrays.items()}
    out = nc.dram_tensor("out_x", (B, S, D), F32, kind="ExternalOutput").ap()
    sandwich(nc, io, out)
    result = run_bass_kernel_spmd(nc, [{f"in_{name}": v for name, v in arrays.items()}], core_ids=[0])
    return result.results[0]["out_x"]
```
